# Optimizing a Trainium2 kernel written in Bass

```python
import numpy as np
import jax
import jax.numpy as jnp

def _softmax(x, axis=-1):
    return jax.nn.softmax(x, axis=axis)

def _gelu(x):
    return jax.nn.gelu(x, approximate=True)

def _silu(x):
    return jax.nn.silu(x)

def _sigmoid(x):
    return jax.nn.sigmoid(x)

def _layernorm(x, axis=-1, eps=1e-05):
    m = jnp.mean(x, axis=axis, keepdims=True)
    v = jnp.var(x, axis=axis, keepdims=True)
    return (x - m) / jnp.sqrt(v + eps)

def _scatter_add(tgt, idx, src, axis=0):
    return tgt.at[idx].add(src)

def _segment_sum(src, seg, n):
    return jax.ops.segment_sum(src, seg, n)
kernel_name = 'mk_gnn_preln_d4_gnn_r32_810f37'

def setup_inputs(seed: int=0):
    np.random.seed(seed)
    _w = jnp.asarray

    def _rec_inputs():
        import jax
        import jax.numpy as jnp
        _gk = jax.random.key(seed)
        x = -0.0009044 + 1 * jax.random.normal(jax.random.fold_in(_gk, 1), (3125, 16), jnp.float32)
        _s = jax.random.randint(jax.random.fold_in(_gk, 2), (50000,), 0, 3125, jnp.int32)
        _d = jax.random.randint(jax.random.fold_in(_gk, 3), (50000,), 0, 3125, jnp.int32)
        _loop = jnp.arange(3125, dtype=jnp.int32)
        src = jnp.concatenate([_s, _d, _loop])
        dst = jnp.concatenate([_d, _s, _loop])
        _o = jnp.argsort(dst, stable=True)
        src = src[_o]
        dst = dst[_o]
        edge_attr_16 = -3.57403e-05 + 0.999761 * jax.random.normal(jax.random.fold_in(_gk, 12), (103125, 16), jnp.float32)
        return (x, src, dst, edge_attr_16)
    x, src, dst, edge_attr_16 = _rec_inputs()

    def _L0_gnn_setup():
        import jax, jax.numpy as jnp
        import numpy as np
        N_NODES = 3125
        N_EDGES = 100000
        FEAT = 16
        HID = 64
        key = jax.random.key(seed)
        ks = jax.random.split(key, 8)
        x = jax.random.normal(ks[0], (N_NODES, FEAT), dtype=jnp.float32)
        edge_index = jax.random.randint(ks[1], (2, N_EDGES), 0, N_NODES, dtype=jnp.int64)
        W1 = jax.random.normal(ks[2], (FEAT, HID), dtype=jnp.float32) * (1.0 / np.sqrt(FEAT))
        b1 = jax.random.normal(ks[3], (HID,), dtype=jnp.float32) * 0.01
        W2 = jax.random.normal(ks[4], (HID, HID), dtype=jnp.float32) * (1.0 / np.sqrt(HID))
        b2 = jax.random.normal(ks[5], (HID,), dtype=jnp.float32) * 0.01
        W3 = jax.random.normal(ks[6], (HID, FEAT), dtype=jnp.float32) * (1.0 / np.sqrt(HID))
        b3 = jax.random.normal(ks[7], (FEAT,), dtype=jnp.float32) * 0.01
        return {'x': x, 'edge_index': edge_index, 'W1': W1, 'b1': b1, 'W2': W2, 'b2': b2, 'W3': W3, 'b3': b3}
    _L0_gnn_all = _L0_gnn_setup()
    _L0_gnn_in = {k: v for k, v in _L0_gnn_all.items() if k in ('W1', 'b1', 'W2', 'b2', 'W3', 'b3')}
    del _L0_gnn_all

    def _L1_gnn_setup():
        import jax, jax.numpy as jnp
        import numpy as np
        N_NODES = 50000
        N_EDGES = 25000
        F_IN = 16
        F_OUT = 16
        HID = 256

        def _glorot(key, shape):
            fan_in, fan_out = (shape[0], shape[1])
            lim = np.sqrt(6.0 / (fan_in + fan_out)).astype(np.float32)
            return jax.random.uniform(key, shape, jnp.float32, -lim, lim)
        key = jax.random.key(seed)
        ks = jax.random.split(key, 12)
        x = jax.random.normal(ks[0], (N_NODES, F_IN), jnp.float32)
        edge_index = jax.random.randint(ks[1], (2, N_EDGES), 0, N_NODES, jnp.int64 if jax.config.jax_enable_x64 else jnp.int32)
        return {'x': x, 'edge_index': edge_index, 'pre_w1': _glorot(ks[2], (F_IN, HID)), 'pre_b1': jnp.zeros((HID,), jnp.float32), 'pre_w2': _glorot(ks[3], (HID, HID)), 'pre_b2': jnp.zeros((HID,), jnp.float32), 'conv_w': _glorot(ks[4], (HID, HID)), 'conv_b': jnp.zeros((HID,), jnp.float32), 'post_w1': _glorot(ks[5], (2 * HID, HID)), 'post_b1': jnp.zeros((HID,), jnp.float32), 'post_w2': _glorot(ks[6], (HID, F_OUT)), 'post_b2': jnp.zeros((F_OUT,), jnp.float32)}
    _L1_gnn_all = _L1_gnn_setup()
    _L1_gnn_in = {k: v for k, v in _L1_gnn_all.items() if k in ('pre_w1', 'pre_b1', 'pre_w2', 'pre_b2', 'conv_w', 'conv_b', 'post_w1', 'post_b1', 'post_w2', 'post_b2')}
    del _L1_gnn_all

    def _L2_gnn_setup():
        import jax, jax.numpy as jnp
        import numpy as np
        N_NODES = 3125
        key = jax.random.key(seed)
        k1, k2, k3 = jax.random.split(key, 3)
        features = jax.random.normal(k1, (N_NODES, 16), dtype=jnp.float32)
        src = jax.random.randint(k2, (156250,), 0, N_NODES, dtype=jnp.int64)
        dst = jax.random.randint(k3, (156250,), 0, N_NODES, dtype=jnp.int64)
        return {'features': features, 'src': src, 'dst': dst}
    _L2_gnn_all = _L2_gnn_setup()
    _L2_gnn_in = {k: v for k, v in _L2_gnn_all.items() if k in ()}
    del _L2_gnn_all

    def _L3_gnn_setup():
        import jax, jax.numpy as jnp
        import numpy as np
        N_NODES = 30000
        N_EDGES = 9375
        IN_FEATS = 16
        OUT_FEATS = 16
        EDGE_DIM = 16
        key = jax.random.key(seed)
        ks = jax.random.split(key, 8)
        feat = jax.random.normal(ks[0], (N_NODES, IN_FEATS), dtype=jnp.float32)
        efeat = jax.random.normal(ks[1], (N_EDGES, EDGE_DIM), dtype=jnp.float32)
        W_msg = jax.random.normal(ks[2], (EDGE_DIM, IN_FEATS * OUT_FEATS), dtype=jnp.float32) * 0.1
        b_msg = jnp.zeros((IN_FEATS * OUT_FEATS,), dtype=jnp.float32)
        W_attn = jax.random.normal(ks[3], (EDGE_DIM, IN_FEATS * OUT_FEATS), dtype=jnp.float32) * 0.1
        b_attn = jnp.zeros((IN_FEATS * OUT_FEATS,), dtype=jnp.float32)
        src = jax.random.randint(ks[4], (N_EDGES,), 0, N_NODES, dtype=jnp.int32)
        dst = jax.random.randint(ks[5], (N_EDGES,), 0, N_NODES, dtype=jnp.int32)
        return {'feat': feat, 'efeat': efeat, 'W_msg': W_msg, 'b_msg': b_msg, 'W_attn': W_attn, 'b_attn': b_attn, 'src': src, 'dst': dst}
    _L3_gnn_all = _L3_gnn_setup()
    _L3_gnn_in = {k: v for k, v in _L3_gnn_all.items() if k in ('W_msg', 'b_msg', 'W_attn', 'b_attn')}
    del _L3_gnn_all
    return {'x': x, 'src': src, 'dst': dst, 'edge_attr_16': edge_attr_16, 'L0_gnn_W1': _L0_gnn_in['W1'], 'L0_gnn_b1': _L0_gnn_in['b1'], 'L0_gnn_W2': _L0_gnn_in['W2'], 'L0_gnn_b2': _L0_gnn_in['b2'], 'L0_gnn_W3': _L0_gnn_in['W3'], 'L0_gnn_b3': _L0_gnn_in['b3'], 'L1_gnn_pre_w1': _L1_gnn_in['pre_w1'], 'L1_gnn_pre_b1': _L1_gnn_in['pre_b1'], 'L1_gnn_pre_w2': _L1_gnn_in['pre_w2'], 'L1_gnn_pre_b2': _L1_gnn_in['pre_b2'], 'L1_gnn_conv_w': _L1_gnn_in['conv_w'], 'L1_gnn_conv_b': _L1_gnn_in['conv_b'], 'L1_gnn_post_w1': _L1_gnn_in['post_w1'], 'L1_gnn_post_b1': _L1_gnn_in['post_b1'], 'L1_gnn_post_w2': _L1_gnn_in['post_w2'], 'L1_gnn_post_b2': _L1_gnn_in['post_b2'], 'L3_gnn_W_msg': _L3_gnn_in['W_msg'], 'L3_gnn_b_msg': _L3_gnn_in['b_msg'], 'L3_gnn_W_attn': _L3_gnn_in['W_attn'], 'L3_gnn_b_attn': _L3_gnn_in['b_attn']}

def reference(x, src, dst, edge_attr_16, L0_gnn_W1, L0_gnn_b1, L0_gnn_W2, L0_gnn_b2, L0_gnn_W3, L0_gnn_b3, L1_gnn_pre_w1, L1_gnn_pre_b1, L1_gnn_pre_w2, L1_gnn_pre_b2, L1_gnn_conv_w, L1_gnn_conv_b, L1_gnn_post_w1, L1_gnn_post_b1, L1_gnn_post_w2, L1_gnn_post_b2, L3_gnn_W_msg, L3_gnn_b_msg, L3_gnn_W_attn, L3_gnn_b_attn):
    import jax
    import jax.numpy as jnp

    def _L0_gnn_ref(x, edge_index, W1, b1, W2, b2, W3, b3):
        import jax, jax.numpy as jnp
        import numpy as np
        N_NODES = 3125
        N_EDGES = 100000
        FEAT = 16
        HID = 64
        N = x.shape[0]
        loops = jnp.arange(N, dtype=edge_index.dtype)
        row = jnp.concatenate([edge_index[0], loops])
        col = jnp.concatenate([edge_index[1], loops])
        deg = jax.ops.segment_sum(jnp.ones_like(col, dtype=x.dtype), col, num_segments=N)
        deg_inv_sqrt = jnp.where(deg > 0, jax.lax.rsqrt(jnp.maximum(deg, 1e-12)), 0.0)
        norm = deg_inv_sqrt[row] * deg_inv_sqrt[col]

        def gcn_layer(h, W, b):
            h = h @ W
            msg = norm[:, None] * h[row]
            agg = jax.ops.segment_sum(msg, col, num_segments=N)
            return agg + b
        h = jax.nn.relu(gcn_layer(x, W1, b1))
        h = jax.nn.relu(gcn_layer(h, W2, b2))
        return gcn_layer(h, W3, b3)

    def _L1_gnn_ref(x, edge_index, pre_w1, pre_b1, pre_w2, pre_b2, conv_w, conv_b, post_w1, post_b1, post_w2, post_b2):
        import jax, jax.numpy as jnp
        import numpy as np
        N_NODES = 50000
        N_EDGES = 25000
        F_IN = 16
        F_OUT = 16
        HID = 256

        def _glorot(key, shape):
            fan_in, fan_out = (shape[0], shape[1])
            lim = np.sqrt(6.0 / (fan_in + fan_out)).astype(np.float32)
            return jax.random.uniform(key, shape, jnp.float32, -lim, lim)
        h = jax.nn.relu(x @ pre_w1 + pre_b1) @ pre_w2 + pre_b2
        src, dst = (edge_index[0], edge_index[1])
        msg = jax.nn.relu(h[src] @ conv_w + conv_b)
        agg = jax.ops.segment_sum(msg, dst, num_segments=h.shape[0])
        h = jnp.concatenate([h, agg], axis=-1)
        out = jax.nn.relu(h @ post_w1 + post_b1) @ post_w2 + post_b2
        return jnp.tanh(out)

    def _L2_gnn_ref(features, src, dst):
        import jax, jax.numpy as jnp
        import numpy as np
        N_NODES = 3125
        n = features.shape[0]
        ones = jnp.ones(src.shape[0], dtype=features.dtype)
        out_deg = jnp.zeros(n, dtype=features.dtype).at[src].add(ones)
        out_deg = jnp.clip(out_deg, 1.0, None)
        in_deg = jnp.zeros(n, dtype=features.dtype).at[dst].add(ones)
        in_deg = jnp.clip(in_deg, 1.0, None)
        x = features * (out_deg ** (-0.5))[:, None]
        agg = jnp.zeros_like(features).at[dst].add(x[src])
        return agg * (in_deg ** (-0.5))[:, None]

    def _L3_gnn_ref(feat, efeat, W_msg, b_msg, W_attn, b_attn, src, dst):
        import jax, jax.numpy as jnp
        import numpy as np
        N_NODES = 30000
        N_EDGES = 9375
        IN_FEATS = 16
        OUT_FEATS = 16
        EDGE_DIM = 16
        N, in_f = feat.shape
        E = efeat.shape[0]
        w_m = (efeat @ W_msg + b_msg).reshape(E, in_f, -1)
        w_a = (efeat @ W_attn + b_attn).reshape(E, in_f, -1)
        h_src = feat[src][:, :, None]
        e1 = w_m * h_src
        e2 = w_a * h_src
        seg_max = jax.ops.segment_max(e2, dst, num_segments=N)
        ex = jnp.exp(e2 - seg_max[dst])
        denom = jax.ops.segment_sum(ex, dst, num_segments=N)
        attn = ex / denom[dst]
        ft = jax.ops.segment_sum(e1 * attn, dst, num_segments=N)
        return ft.sum(axis=1)
    edge_index = jnp.stack([src, dst])
    h = jnp.maximum(_layernorm(x, axis=-1), 0.0)
    x = x + _L0_gnn_ref(h, edge_index, L0_gnn_W1, L0_gnn_b1, L0_gnn_W2, L0_gnn_b2, L0_gnn_W3, L0_gnn_b3)
    h = jnp.maximum(_layernorm(x, axis=-1), 0.0)
    x = x + _L1_gnn_ref(h, edge_index, L1_gnn_pre_w1, L1_gnn_pre_b1, L1_gnn_pre_w2, L1_gnn_pre_b2, L1_gnn_conv_w, L1_gnn_conv_b, L1_gnn_post_w1, L1_gnn_post_b1, L1_gnn_post_w2, L1_gnn_post_b2)
    h = jnp.maximum(_layernorm(x, axis=-1), 0.0)
    x = x + _L2_gnn_ref(h, src, dst)
    h = jnp.maximum(_layernorm(x, axis=-1), 0.0)
    x = x + _L3_gnn_ref(h, edge_attr_16, L3_gnn_W_msg, L3_gnn_b_msg, L3_gnn_W_attn, L3_gnn_b_attn, src, dst)
    return x

_drawn_inputs = setup_inputs


def setup_inputs(seed=0):
    import zlib

    import numpy as np

    out = dict(_drawn_inputs(seed))
    spreads = {'L1_gnn_pre_b1': (0.0, 0.1),
     'L1_gnn_pre_b2': (0.0, 0.1),
     'L1_gnn_conv_b': (0.0, 0.1),
     'L1_gnn_post_b1': (0.0, 0.464),
     'L1_gnn_post_b2': (0.0, 0.8),
     'L3_gnn_b_msg': (0.0, 0.1),
     'L3_gnn_b_attn': (0.0, 0.677)}
    factors = {'L0_gnn_b1': 8.0, 'L0_gnn_b2': 8.0, 'L0_gnn_b3': 7.469}
    for name, (base, spread) in spreads.items():
        noise = np.random.default_rng([zlib.crc32(name.encode()), seed]).standard_normal(out[name].shape)
        drawn = base * np.exp(spread * noise) if base else spread * noise
        out[name] = jnp.asarray(drawn.astype(out[name].dtype))
    for name, factor in factors.items():
        out[name] = (out[name] * factor).astype(out[name].dtype)
    return out
```

```python
from contextlib import ExitStack

import concourse.bass as bass
from concourse import mybir

F32 = mybir.dt.float32
BF16 = mybir.dt.bfloat16
I32 = mybir.dt.int32
ALU = mybir.AluOpType
ACT = mybir.ActivationFunctionType
X = mybir.AxisListType.X

P = 128
NODES = 3125
EDGES = 103125
F = 16
TILES = -(-NODES // P)
NPAD = TILES * P
STEPS = -(-EDGES // P)
EPAD = STEPS * P
HID0 = 64
HID1 = 256
LN_EPS = 1e-5

W = 16
STRIPS = -(-(NODES + 1) // W)
COLS = STRIPS * W
GROUP = 2 * P
GROUPS = EPAD // GROUP
PAIRS = GROUPS + STRIPS - 1
UNROLL = 12
BODY = 2 * UNROLL
TURNS = -(-PAIRS // BODY)
PAIR_TILES = -(-TURNS * BODY // P)
QW = TILES * W
HALFQ = QW // 2
QRING = 4
BANKS = 8

CHUNKS = 7
CW = COLS // CHUNKS

BLK = 13
BLOCKS = STEPS // BLK
CH = F * F
ROW = 3 * CH
HEADS = P
TABLE = NPAD + HEADS
BIG = 1e30
FAR = 1 << 20

assert EPAD % GROUP == 0 and COLS % CHUNKS == 0 and STEPS % BLK == 0 and BLOCKS % 2 == 0
assert PAIR_TILES * P >= TURNS * BODY and QW <= 512 and 2 * HALFQ <= 512


class Line:

    def __init__(self, eng, sem):
        self.eng, self.sem, self.n = eng, sem, 0

    def add(self, ins):
        ins.then_inc(self.sem, 1)
        self.n += 1

    def then(self, ins):
        self.add(ins)
        self.eng.wait_ge(self.sem, self.n)


def bc(ap, axis, n):
    shape = list(ap.shape)
    shape.insert(axis, n)
    return ap.unsqueeze(axis).broadcast_to(shape)


def program(nc, io, out):
    with ExitStack() as ctx:
        def sem(name):
            return ctx.enter_context(nc.semaphore(name))

        def dram(name, shape, dt):
            return nc.dram_tensor(name, shape, dt, kind="Internal").ap()

        keep = {
            "x": ctx.enter_context(nc.sbuf_tensor("x_sb", [P, TILES, F], F32)),
            "ident": ctx.enter_context(nc.sbuf_tensor("ident", [P, P], F32)),
            "ones": ctx.enter_context(nc.sbuf_tensor("ones", [P, P], F32)),
        }
        d = {
            "strip_of_pair": dram("strip_of_pair", [PAIR_TILES, P], I32),
            "h2T": dram("h2T", [2, P, NPAD], F32),
            "msg": dram("msg", [2, P, TILES, 3, P], BF16),
            "aggT": dram("aggT", [2, P, COLS], F32),
            "h_table": dram("h_table", [NPAD, F], F32),
            "table": dram("table", [TABLE, ROW], F32),
        }
        with ExitStack() as graph:
            keep["edges"] = graph.enter_context(nc.sbuf_tensor("edges", [P, TILES, COLS], BF16))
            keep["deg"] = graph.enter_context(nc.sbuf_tensor("deg", [P, 3, TILES], F32))
            build_edges(nc, io, keep, d, sem)
            degrees(nc, io, keep, d, sem)
            layer0(nc, io, keep, d, sem)
            layer1_nodes(nc, io, keep, d, sem)
            layer1_sum(nc, io, keep, d, sem)
            layer1_post(nc, io, keep, d, sem)
            layer2(nc, io, keep, d, sem)
        attention(nc, io, keep, d, sem, out)


def build_edges(nc, io, keep, d, sem):
    ident, ones, edges = keep["ident"], keep["ones"], keep["edges"]
    with ExitStack() as ctx:
        def sb(name, shape, dt=F32):
            return ctx.enter_context(nc.sbuf_tensor(name, shape, dt))

        loT = sb("loT", [P, 2, PAIR_TILES * P])
        qT = sb("qT", [P, 2, PAIR_TILES * P])
        lane = sb("lane", [P, P])
        qcol = sb("qcol", [P, QW], BF16)
        strip = sb("strip", [1, PAIR_TILES * P], I32)
        b_consts, b_cast = sem("b_consts"), sem("b_cast")
        b_loaded, b_pairs, b_gather, b_stripdma = sem("b_loaded"), sem("b_pairs"), sem("b_gather"), sem("b_stripdma")
        b_dve, b_pe, b_evac = sem("b_dve"), sem("b_pe"), sem("b_evac")
        with ExitStack() as prep:
            def tb(name, shape, dt=F32):
                return prep.enter_context(nc.sbuf_tensor(name, shape, dt))

            ends = tb("ends", [1, GROUPS], I32)
            laneI = tb("laneI", [P, P], I32)
            qcolI = tb("qcolI", [P, QW], I32)
            pairI = tb("pairI", [P, PAIR_TILES], I32)
            groupI = tb("groupI", [1, GROUPS], I32)
            groupF = tb("groupF", [1, GROUPS])
            cut = tb("cut", [1, GROUPS])
            pair = tb("pair", [P, PAIR_TILES])
            below = tb("below", [P, GROUPS])
            gidx = tb("gidx", [P, PAIR_TILES])
            gidxI = tb("gidxI", [P, PAIR_TILES], I32)
            first = tb("first", [P, PAIR_TILES])
            stripI = tb("stripI", [P, PAIR_TILES], I32)
            srcg = tb("srcg", [P, PAIR_TILES, GROUP], I32)
            dstg = tb("dstg", [P, PAIR_TILES, GROUP], I32)
            t1 = tb("t1", [P, PAIR_TILES, GROUP])
            t2 = tb("t2", [P, PAIR_TILES, GROUP])
            t3 = tb("t3", [P, PAIR_TILES, GROUP], I32)
            cuts = prep.enter_context(nc.psum_tensor("cuts", [P, GROUPS], F32))
            tr = prep.enter_context(nc.psum_tensor("tr", [P, PAIR_TILES, 4, P], F32))

            with nc.Block() as block:
                @block.sync
                def _(sp):
                    sp.dma_start(ends[:, :], io["group_ends"]).then_inc(b_loaded, 16)
                    sp.wait_ge(b_pairs, 1)
                    sp.dma_start(d["strip_of_pair"].rearrange("k p -> p k"), stripI[:, :],
                                 allow_slow_non_contiguous=True).then_inc(b_stripdma, 16)
                    sp.wait_ge(b_stripdma, 16)
                    sp.dma_start(strip[:, :], d["strip_of_pair"].rearrange("(a k) p -> a (k p)", a=1)
                                 ).then_inc(b_stripdma, 16)
                    sp.wait_ge(b_stripdma, 32)

                @block.gpsimd
                def _(pool):
                    nc.gpsimd.iota(laneI[:, :], [[1, P]], base=0, channel_multiplier=0)
                    nc.gpsimd.iota(qcolI[:, :], [[1, QW]], base=-HALFQ, channel_multiplier=0)
                    nc.gpsimd.iota(groupI[:, :], [[1, GROUPS]], base=1, channel_multiplier=0)
                    nc.gpsimd.iota(pairI[:, :], [[P, PAIR_TILES]], base=0, channel_multiplier=1)
                    nc.gpsimd.memset(ones[:, :], 1.0)
                    nc.gpsimd.memset(ident[:, :], 0.0).then_inc(b_consts, 1)
                    pool.wait_ge(b_consts, 1)
                    nc.gpsimd.affine_select(out=ident[:, :], in_=ident[:, :], compare_op=ALU.not_equal, fill=1.0,
                                            base=0, pattern=[[-1, P]], channel_multiplier=1).then_inc(b_consts, 1)
                    nc.gpsimd.memset(edges[:, 0:TILES // 2, :], 0.0).then_inc(b_consts, 1)
                    pool.wait_ge(b_pairs, 1)
                    for k in range(PAIR_TILES):
                        for rows, name in ((srcg, "src"), (dstg, "dst")):
                            nc.gpsimd.indirect_dma_start(
                                out=rows[:, k, :], out_offset=None,
                                in_=io[name].rearrange("(g e) -> g e", e=GROUP),
                                in_offset=bass.IndirectOffsetOnAxis(ap=gidxI[:, k:k + 1], axis=0),
                            ).then_inc(b_gather, 16)

                @block.tensor
                def _(pe):
                    pe.wait_ge(b_cast, 1)
                    pe.wait_ge(b_consts, 1)
                    nc.tensor.matmul(cuts[:, :], ones[0:1, :], cut[:, :], start=True, stop=True).then_inc(b_pe, 1)
                    pe.wait_ge(b_cast, 2)
                    pe.wait_ge(b_consts, 2)
                    for k in range(PAIR_TILES):
                        for s in range(2):
                            nc.tensor.transpose(tr[:, k, s, :], t1[:, k, s * P:(s + 1) * P], ident[:, :])
                            last = nc.tensor.transpose(tr[:, k, 2 + s, :], t2[:, k, s * P:(s + 1) * P], ident[:, :])
                        last.then_inc(b_pe, 1)

                @block.vector
                def _(dve):
                    v = Line(dve, b_dve)
                    v.add(nc.vector.memset(edges[:, TILES // 2:TILES, :], 0.0))
                    dve.wait_ge(b_consts, 1)
                    v.add(nc.vector.tensor_copy(lane[:, :], laneI[:, :]))
                    v.add(nc.vector.tensor_copy(qcol[:, :], qcolI[:, :]))
                    v.add(nc.vector.tensor_copy(pair[:, :], pairI[:, :]))
                    v.add(nc.vector.tensor_copy(groupF[:, :], groupI[:, :]))
                    dve.wait_ge(b_loaded, 16)
                    v.then(nc.vector.tensor_scalar(ends[:, :], ends[:, :], 4, None, ALU.arith_shift_right))
                    nc.vector.tensor_tensor(cut[:, :], ends[:, :], groupF[:, :], ALU.add).then_inc(b_cast, 1)
                    dve.wait_ge(b_pe, 1)
                    for k in range(PAIR_TILES):
                        v.then(nc.vector.tensor_scalar(below[:, :], cuts[:, :], pair[:, k:k + 1], None, ALU.is_le))
                        v.then(nc.vector.tensor_reduce(gidx[:, k:k + 1], below[:, :], X, ALU.add))
                    v.then(nc.vector.tensor_scalar(gidx[:, :], gidx[:, :], float(GROUPS - 1), None, ALU.min))
                    v.add(nc.vector.tensor_copy(gidxI[:, :], gidx[:, :]))
                    v.then(nc.vector.tensor_tensor(first[:, :], pair[:, :], gidx[:, :], ALU.subtract))
                    v.then(nc.vector.tensor_scalar(stripI[:, :], first[:, :], float(STRIPS - 1), float(W),
                                                   ALU.min, ALU.mult))
                    nc.vector.tensor_scalar(first[:, :], first[:, :], float(W), None, ALU.mult).then_inc(b_pairs, 1)
                    dve.wait_ge(b_pairs, 1)
                    dve.wait_ge(b_consts, 3)
                    for t in range(TILES):
                        w = min(P, COLS - t * P)
                        v.add(nc.vector.tensor_copy(edges[:, t, t * P:t * P + w], ident[:, 0:w]))
                    dve.wait_ge(b_gather, 16 * 2 * PAIR_TILES)
                    v.then(nc.vector.tensor_copy(t1[:, :, :], dstg[:, :, :]))
                    v.then(nc.vector.tensor_tensor(t1[:, :, :], t1[:, :, :], bc(first[:, :], 2, GROUP), ALU.subtract))
                    v.then(nc.vector.tensor_scalar(t2[:, :, :], t1[:, :, :], 0.0, None, ALU.is_ge))
                    v.then(nc.vector.scalar_tensor_tensor(t2[:, :, :], t1[:, :, :], float(W - 1), t2[:, :, :],
                                                          ALU.is_le, ALU.mult))
                    v.then(nc.vector.tensor_scalar(t3[:, :, :], srcg[:, :, :], 7, 4,
                                                   ALU.arith_shift_right, ALU.logical_shift_left))
                    v.then(nc.vector.tensor_tensor(t1[:, :, :], t1[:, :, :], t3[:, :, :], ALU.add))
                    v.then(nc.vector.scalar_tensor_tensor(t1[:, :, :], t1[:, :, :], 4096.0 - HALFQ, t2[:, :, :],
                                                          ALU.add, ALU.mult))
                    v.then(nc.vector.tensor_scalar(t1[:, :, :], t1[:, :, :], -4096.0, None, ALU.add))
                    v.then(nc.vector.tensor_scalar(t3[:, :, :], srcg[:, :, :], P - 1, None, ALU.bitwise_and))
                    nc.vector.tensor_scalar(t2[:, :, :], t3[:, :, :], -1.0, None, ALU.mult).then_inc(b_cast, 1)
                    for k in range(PAIR_TILES):
                        dve.wait_ge(b_pe, 2 + k)
                        v.add(nc.vector.tensor_copy(qT[:, :, k * P:(k + 1) * P], tr[:, k, 0:2, :]))
                        v.add(nc.vector.tensor_copy(loT[:, :, k * P:(k + 1) * P], tr[:, k, 2:4, :]))

        lo_hot = sb("lo_hot", [P, 2, 2, UNROLL, P], BF16)
        q_hot = sb("q_hot", [P, QRING, 2, QW], BF16)
        acc = ctx.enter_context(nc.psum_tensor("acc", [P, BANKS, 512], F32))
        lo_far, lo_ready, q_ready = sem("lo_far"), sem("lo_ready"), sem("q_ready")
        multiplied, added = sem("multiplied"), sem("added")
        with nc.Block() as block:
            @block.scalar
            def _(act):
                with act.Fori(0, TURNS) as i:
                    for u in range(2):
                        act.wait_ge(multiplied, i * BODY + (u + 1) * UNROLL)
                        for k in range(UNROLL):
                            for s in range(2):
                                ins = nc.scalar.activation(lo_hot[:, u, s, k, :], lane[:, :], ACT.Abs,
                                                           bias=loT[:, s, bass.ds(i * BODY + u * UNROLL + k, 1)])
                        ins.then_inc(lo_far, 1)
                        act.wait_ge(lo_far, i * 2 + (u + 1))
                        nc.scalar.activation(lo_hot[:, u, :, :, :], lo_hot[:, u, :, :, :], ACT.Relu,
                                             scale=-1.0, bias=1.0).then_inc(lo_ready, 1)

            @block.vector
            def _(dve):
                dve.sem_inc(added, BANKS)
                strips = [dve.alloc_register(f"strip{k}") for k in range(BODY)]
                with dve.Fori(0, TURNS) as i:
                    for k in range(0, BODY, 4):
                        dve.load(strips[k:k + 4], strip[0:1, bass.ds(i * BODY + k, 4)])
                    def one_hot(k):
                        dve.wait_ge(multiplied, i * BODY + (BODY + k + 1 - QRING))
                        for s in range(2):
                            ins = nc.vector.tensor_scalar(q_hot[:, k % QRING, s, :], qcol[:, :],
                                                          qT[:, s, bass.ds(i * BODY + k, 1)], None, ALU.is_equal)
                        ins.then_inc(q_ready, 1)

                    def add(k):
                        s16 = dve.snap(strips[k], min_val=0, max_val=COLS - W)
                        dve.wait_ge(multiplied, i * BODY + (BODY + k + 1))
                        dve.wait_ge(added, i * BODY + (BANKS + k))
                        cell = edges[:, :, bass.ds(s16, W)]
                        nc.vector.tensor_tensor(cell, acc[:, k % BANKS, 0:QW].rearrange("p (t w) -> p t w", w=W),
                                                cell, ALU.add).then_inc(added, 1)

                    for k in range(BODY):
                        one_hot(k)
                        if k >= 2:
                            add(k - 2)
                    add(BODY - 2)
                    add(BODY - 1)

            @block.tensor
            def _(pe):
                pe.sem_inc(multiplied, BODY)
                with pe.Fori(0, TURNS) as i:
                    for k in range(BODY):
                        pe.wait_ge(lo_ready, i * 2 + (k // UNROLL + 1))
                        pe.wait_ge(q_ready, i * BODY + (k + 1))
                        pe.wait_ge(added, i * BODY + (k + 1))
                        for s in range(2):
                            ins = nc.tensor.matmul(acc[:, k % BANKS, 0:QW],
                                                   lo_hot[:, k // UNROLL, s, k % UNROLL, :],
                                                   q_hot[:, k % QRING, s, :], start=(s == 0), stop=(s == 1))
                        ins.then_inc(multiplied, 1)


def degrees(nc, io, keep, d, sem):
    ident, ones, edges, deg = keep["ident"], keep["ones"], keep["edges"], keep["deg"]
    with ExitStack() as ctx:
        def sb(name, shape, dt=F32):
            return ctx.enter_context(nc.sbuf_tensor(name, shape, dt))

        ones_b = sb("ones_b", [P, P], BF16)
        colsum = sb("colsum", [1, NPAD])
        junk = sb("junk", [P, COLS], BF16)
        raw = sb("raw", [P, 3, TILES])
        sums = ctx.enter_context(nc.psum_tensor("sums", [P, CHUNKS, 512], F32))
        turned = ctx.enter_context(nc.psum_tensor("turned", [P, TILES], F32))
        g_ready, g_sum, g_row, g_turn, g_out, g_raw, g_sqrt, g_dve = (
            sem(n) for n in ("g_ready", "g_sum", "g_row", "g_turn", "g_out", "g_raw", "g_sqrt", "g_dve"))
        g_x = sem("g_x")
        with nc.Block() as block:
            @block.sync
            def _(sp):
                sp.dma_start(keep["x"][:, :, :], io["x"].rearrange("(t p) f -> p t f", p=P)).then_inc(g_x, 16)
                sp.wait_ge(g_x, 16)

            @block.tensor
            def _(pe):
                pe.wait_ge(g_ready, 1)
                for n in range(CHUNKS):
                    for k in range(TILES):
                        ins = nc.tensor.matmul(sums[:, n, 0:CW], ones_b[:, :], edges[:, k, n * CW:(n + 1) * CW],
                                               start=(k == 0), stop=(k == TILES - 1))
                    ins.then_inc(g_sum, 1)
                pe.wait_ge(g_row, CHUNKS + 1)
                for t in range(TILES):
                    ins = nc.tensor.matmul(turned[:, t:t + 1], colsum[0:1, t * P:(t + 1) * P], ones[0:1, 0:1],
                                           start=True, stop=True)
                ins.then_inc(g_turn, 1)

            @block.vector
            def _(dve):
                nc.vector.tensor_copy(ones_b[:, :], ones[:, :]).then_inc(g_ready, 1)
                nc.vector.memset(colsum[:, COLS:NPAD], 1.0).then_inc(g_row, 1)
                for n in range(CHUNKS):
                    dve.wait_ge(g_sum, n + 1)
                    nc.vector.tensor_copy(colsum[:, n * CW:(n + 1) * CW], sums[0:1, n, 0:CW]).then_inc(g_row, 1)
                v = Line(dve, g_dve)
                dve.wait_ge(g_turn, 1)
                v.add(nc.vector.tensor_copy(raw[:, 0, :], turned[:, :]))
                dve.wait_ge(g_out, TILES)
                v.then(nc.vector.tensor_scalar(raw[:, 1, :], raw[:, 1, :], -1.0, 1.0, ALU.add, ALU.max))
                v.then(nc.vector.tensor_scalar(raw[:, 2, :], raw[:, 0, :], -1.0, 1.0, ALU.add, ALU.max))
                nc.vector.tensor_scalar(raw[:, 0, :], raw[:, 0, :], 1.0, None, ALU.max).then_inc(g_raw, 1)
                dve.wait_ge(g_sqrt, 1)
                v.then(nc.vector.reciprocal(deg[:, :, :], raw[:, :, :]))

            @block.scalar
            def _(act):
                for k in range(TILES):
                    nc.scalar.activation(junk[:, :], edges[:, k, :], ACT.Copy,
                                         accum_out=raw[:, 1, k:k + 1]).then_inc(g_out, 1)
                    act.wait_ge(g_out, k + 1)
                act.wait_ge(g_raw, 1)
                nc.scalar.activation(raw[:, :, :], raw[:, :, :], ACT.Sqrt).then_inc(g_sqrt, 1)
                act.wait_ge(g_sqrt, 1)


def layer_norm(dve, v, x, h, mean, cen, need_sqrt, sqrt_done, count):
    v.then(dve.tensor_reduce(mean[:, :], x[:, :, :], X, ALU.add))
    v.then(dve.tensor_scalar(mean[:, :], mean[:, :], 1.0 / F, None, ALU.mult))
    v.then(dve.tensor_tensor(cen[:, :, :], x[:, :, :], bc(mean[:, :], 2, F), ALU.subtract))
    v.then(dve.tensor_tensor(h[:, :, :], cen[:, :, :], cen[:, :, :], ALU.mult))
    v.then(dve.tensor_reduce(mean[:, :], h[:, :, :], X, ALU.add))
    dve.tensor_scalar(mean[:, :], mean[:, :], 1.0 / F, LN_EPS, ALU.mult, ALU.add).then_inc(need_sqrt, 1)
    dve.wait_ge(sqrt_done, count)
    v.then(dve.reciprocal(mean[:, :], mean[:, :]))
    v.then(dve.tensor_tensor(h[:, :, :], cen[:, :, :], bc(mean[:, :], 2, F), ALU.mult))
    v.then(dve.tensor_scalar(h[:, :, :], h[:, :, :], 0.0, None, ALU.max))


def split3(dve, v, value, rest, parts):
    v.then(dve.tensor_copy(parts[0], value))
    v.then(dve.tensor_tensor(rest, value, parts[0], ALU.subtract))
    v.then(dve.tensor_copy(parts[1], rest))
    v.then(dve.tensor_tensor(parts[2], rest, parts[1], ALU.subtract))


def times_edges(pe, nc, out, groups, edges, done):
    last = len(groups) - 1
    with pe.Fori(0, CHUNKS) as n:
        for g, lhs in enumerate(groups):
            for k in range(TILES):
                ins = nc.tensor.matmul(out[:, bass.ds(n, 1), 0:CW], lhs(k), edges[:, k, bass.ds(n * CW, CW)],
                                       start=(g == 0 and k == 0), stop=(g == last and k == TILES - 1))
        ins.then_inc(done, 1)


def layer0(nc, io, keep, d, sem):
    ident, ones, edges, deg, x = (keep[n] for n in ("ident", "ones", "edges", "deg", "x"))
    dis = deg[:, 0, :]
    with ExitStack() as ctx:
        def sb(name, shape, dt=F32):
            return ctx.enter_context(nc.sbuf_tensor(name, shape, dt))

        parts = sb("parts", [P, TILES, 2 * P], BF16)
        y = sb("y", [P, TILES, HID0])
        rest = sb("rest", [P, TILES, HID0])
        mean = sb("mean", [P, TILES])
        agg = sb("agg", [P, NPAD])
        w1, w2, w3 = sb("w1", [3 * F, HID0]), sb("w2", [2 * HID0, HID0]), sb("w3", [HID0, F])
        sel = sb("sel", [3 * F, F])
        b1, b2, b3 = sb("b1", [P, HID0]), sb("b2", [P, HID0]), sb("b3", [P, F])
        h = rest[:, :, 0:F]
        cen = rest[:, :, F:2 * F]
        h2T = sb("h2T_sb", [HID0, 4 * P])
        acc = ctx.enter_context(nc.psum_tensor("acc0", [P, CHUNKS, 512], F32))
        small = ctx.enter_context(nc.psum_tensor("small0", [P, 512], F32))
        (c_w, c_dve, c_sq, c_sqd, c_parts, c_agg, c_evac, c_small, c_used) = (
            sem(n) for n in ("c_w", "c_dve", "c_sq", "c_sqd", "c_parts", "c_agg", "c_evac", "c_small", "c_used"))
        G1 = [range(t, min(t + 8, TILES)) for t in range(0, TILES, 8)]
        G3 = [range(t, min(t + 4, TILES)) for t in range(0, TILES, 4)]
        with nc.Block() as block:
            @block.sync
            def _(sp):
                for a in range(3):
                    sp.dma_start(w1[a * F:(a + 1) * F, :], io["L0_gnn_W1"]).then_inc(c_w, 16)
                    sp.dma_start(sel[a * F:(a + 1) * F, :], ident[0:F, 0:F]).then_inc(c_w, 16)
                for a in range(2):
                    sp.dma_start(w2[a * HID0:(a + 1) * HID0, :], io["L0_gnn_W2"]).then_inc(c_w, 16)
                sp.dma_start(w3[:, :], io["L0_gnn_W3"]).then_inc(c_w, 16)
                for b, name in ((b1, "L0_gnn_b1"), (b2, "L0_gnn_b2"), (b3, "L0_gnn_b3")):
                    sp.dma_start(b[:, :], io[name].rearrange("(a n) -> a n", a=1).broadcast_to(list(b.shape))
                                 ).then_inc(c_w, 16)
                sp.wait_ge(c_w, 16 * 12)

            @block.scalar
            def _(act):
                act.wait_ge(c_sq, 1)
                nc.scalar.activation(mean[:, :], mean[:, :], ACT.Sqrt).then_inc(c_sqd, 1)
                for rnd, rows in ((0, 3 * F), (1, P), (2, 3 * F)):
                    for n in range(CHUNKS):
                        act.wait_ge(c_agg, rnd * CHUNKS + n + 1)
                        nc.scalar.activation(agg[0:rows, n * CW:(n + 1) * CW], acc[0:rows, n, 0:CW],
                                             ACT.Copy).then_inc(c_evac, 1)
                act.wait_ge(c_evac, 3 * CHUNKS)

            @block.tensor
            def _(pe):
                lo = lambda k: parts[:, k, 0:P]
                hi = lambda k: parts[:, k, P:2 * P]
                pe.wait_ge(c_parts, 1)
                times_edges(pe, nc, acc, [lo], edges, c_agg)
                pe.wait_ge(c_w, 16 * 12)
                pe.wait_ge(c_evac, CHUNKS)
                for g, tiles in enumerate(G1):
                    if g:
                        pe.wait_ge(c_used, g)
                    for t in tiles:
                        ins = nc.tensor.matmul(small[:, (t % 8) * HID0:(t % 8 + 1) * HID0],
                                               agg[0:3 * F, t * P:(t + 1) * P], w1[:, :], start=True, stop=True)
                    ins.then_inc(c_small, 1)
                pe.wait_ge(c_parts, 2)
                times_edges(pe, nc, acc, [lo, hi], edges, c_agg)
                pe.wait_ge(c_evac, 2 * CHUNKS)
                n1 = len(G1)
                for g, tiles in enumerate(G1):
                    pe.wait_ge(c_used, n1 + g)
                    for t in tiles:
                        ins = nc.tensor.matmul(small[:, (t % 8) * HID0:(t % 8 + 1) * HID0],
                                               agg[:, t * P:(t + 1) * P], w2[:, :], start=True, stop=True)
                    ins.then_inc(c_small, 1)
                for g, tiles in enumerate(G3):
                    pe.wait_ge(c_used, 2 * n1 + 2 * g)
                    for t in tiles:
                        ins = nc.tensor.transpose(small[0:HID0, (t % 4) * P:(t % 4 + 1) * P], y[:, t, :], ident[:, :])
                    ins.then_inc(c_small, 1)
                    pe.wait_ge(c_used, 2 * n1 + 2 * g + 1)
                    for t in tiles:
                        ins = nc.tensor.matmul(small[:, (t % 4) * F:(t % 4 + 1) * F],
                                               h2T[:, (t % 4) * P:(t % 4 + 1) * P], w3[:, :], start=True, stop=True)
                    ins.then_inc(c_small, 1)
                pe.wait_ge(c_parts, 3)
                times_edges(pe, nc, acc, [lo], edges, c_agg)
                pe.wait_ge(c_evac, 3 * CHUNKS)
                for t in range(TILES):
                    ins = nc.tensor.matmul(small[:, t * F:(t + 1) * F], agg[0:3 * F, t * P:(t + 1) * P], sel[:, :],
                                           start=True, stop=True)
                ins.then_inc(c_small, 1)

            @block.vector
            def _(dve):
                v = Line(dve, c_dve)
                v.add(nc.vector.memset(parts[:, :, :], 0.0))
                v.add(nc.vector.memset(agg[:, COLS:NPAD], 0.0))
                layer_norm(dve, v, x, h, mean, cen, c_sq, c_sqd, 1)
                v.then(nc.vector.tensor_tensor(y[:, :, 0:F], h, bc(dis, 2, F), ALU.mult))
                split3(dve, v, y[:, :, 0:F], cen, [parts[:, :, a * F:(a + 1) * F] for a in range(3)])
                nc.vector.tensor_copy(mean[:, :], dis).then_inc(c_parts, 1)
                dve.wait_ge(c_w, 16 * 12)
                small_count = 0
                for rnd, b in ((0, b1), (1, b2)):
                    for g, tiles in enumerate(G1):
                        a, e = tiles[0], tiles[-1] + 1
                        small_count += 1
                        dve.wait_ge(c_small, small_count)
                        part = y[:, a:e, :]
                        v.then(nc.vector.tensor_tensor(
                            part, small[:, 0:(e - a) * HID0].rearrange("p (t f) -> p t f", f=HID0),
                            bc(dis[:, a:e], 2, HID0), ALU.mult))
                        v.then(nc.vector.tensor_tensor(part, part, bc(b[:, :], 1, e - a), ALU.add))
                        nc.vector.tensor_scalar(part, part, 0.0, None, ALU.max).then_inc(c_used, 1)
                    if rnd == 0:
                        dve.wait_ge(c_used, len(G1))
                        v.then(nc.vector.tensor_tensor(y[:, :, :], y[:, :, :], bc(dis, 2, HID0), ALU.mult))
                        split3(dve, v, y[:, :, :], rest[:, :, :],
                               [parts[:, :, a * HID0:(a + 1) * HID0] for a in range(3)])
                        nc.vector.tensor_copy(mean[:, :], dis).then_inc(c_parts, 1)
                for g, tiles in enumerate(G3):
                    a, e = tiles[0], tiles[-1] + 1
                    small_count += 1
                    dve.wait_ge(c_small, small_count)
                    nc.vector.tensor_copy(h2T[:, 0:(e - a) * P], small[0:HID0, 0:(e - a) * P]).then_inc(c_used, 1)
                    small_count += 1
                    dve.wait_ge(c_small, small_count)
                    nc.vector.tensor_tensor(h[:, a:e, :], small[:, 0:(e - a) * F].rearrange("p (t f) -> p t f", f=F),
                                            bc(dis[:, a:e], 2, F), ALU.mult).then_inc(c_used, 1)
                dve.wait_ge(c_used, 2 * len(G1) + 2 * len(G3))
                v.add(nc.vector.memset(parts[:, :, 3 * F:2 * P], 0.0))
                split3(dve, v, h, cen, [parts[:, :, a * F:(a + 1) * F] for a in range(3)])
                nc.vector.tensor_copy(mean[:, :], dis).then_inc(c_parts, 1)
                small_count += 1
                dve.wait_ge(c_small, small_count)
                v.then(nc.vector.tensor_tensor(h, small[:, 0:TILES * F].rearrange("p (t f) -> p t f", f=F),
                                               bc(dis, 2, F), ALU.mult))
                v.then(nc.vector.tensor_tensor(h, h, bc(b3[:, :], 1, TILES), ALU.add))
                v.then(nc.vector.tensor_tensor(x[:, :, :], x[:, :, :], h, ALU.add))


def layer1_nodes(nc, io, keep, d, sem):
    ident, edges, x = keep["ident"], keep["edges"], keep["x"]
    PART = 5
    PN = PART * P
    HALF = PN // 2
    ROUNDS = TILES // PART
    with ExitStack() as ctx:
        def sb(name, shape, dt=F32):
            return ctx.enter_context(nc.sbuf_tensor(name, shape, dt))

        h, cen, mean = sb("h1", [P, TILES, F]), sb("cen1", [P, TILES, F]), sb("mean1", [P, TILES])
        w1, w2, wc = sb("pre_w1", [F, HID1]), sb("pre_w2", [P, 2, HID1]), sb("conv_w", [P, 2, HID1])
        b1, b2, bconv = sb("pre_b1", [P, 2]), sb("pre_b2", [P, 2]), sb("conv_b", [P, HID1])
        hT, a1T, h2T = sb("hT", [F, PN]), sb("a1T", [P, 2, PN]), sb("h2T_part", [P, 2, PN])
        m, rest = sb("m", [P, PART, HID1]), sb("m_rest", [P, PART, HID1])
        parts = sb("m_parts", [P, PART, 3, HID1], BF16)
        low = ctx.enter_context(nc.psum_tensor("low1", [P, 4, 512], F32))
        high = ctx.enter_context(nc.psum_tensor("high1", [P, 4, 512], F32))
        (n_w, n_dve, n_sq, n_sqd, n_h, n_tr, n_hT, n_a, n_a1, n_h2, n_h2T, n_m, n_read, n_split, n_dh, n_dm) = (
            sem("n_" + s) for s in "w dve sq sqd h tr hT a a1 h2 h2T m read split dh dm".split())
        with nc.Block() as block:
            @block.sync
            def _(sp):
                sp.dma_start(w1[:, :], io["L1_gnn_pre_w1"]).then_inc(n_w, 16)
                sp.dma_start(w2[:, :, :], io["L1_gnn_pre_w2"].rearrange("(k p) n -> p k n", p=P)).then_inc(n_w, 16)
                sp.dma_start(wc[:, :, :], io["L1_gnn_conv_w"].rearrange("(k p) n -> p k n", p=P)).then_inc(n_w, 16)
                sp.dma_start(b1[:, :], io["L1_gnn_pre_b1"]).then_inc(n_w, 16)
                sp.dma_start(b2[:, :], io["L1_gnn_pre_b2"]).then_inc(n_w, 16)
                sp.dma_start(bconv[:, :], io["L1_gnn_conv_b"].rearrange("(a n) -> a n", a=1).broadcast_to([P, HID1])
                             ).then_inc(n_w, 16)
                for c in range(ROUNDS):
                    sp.wait_ge(n_h2T, 2 * (c + 1))
                    sp.dma_start(d["h2T"][:, :, c * PN:(c + 1) * PN].rearrange("k p n -> p k n"), h2T[:, :, :]
                                 ).then_inc(n_dh, 16)
                    sp.wait_ge(n_split, c + 1)
                    for f in range(2):
                        sp.dma_start(d["msg"][f, :, c * PART:(c + 1) * PART, :, :],
                                     parts[:, :, :, f * P:(f + 1) * P]).then_inc(n_dm, 16)
                sp.wait_ge(n_dh, 16 * ROUNDS)
                sp.wait_ge(n_dm, 32 * ROUNDS)

            @block.tensor
            def _(pe):
                pe.wait_ge(n_w, 16 * 6)
                pe.wait_ge(n_h, 1)
                for c in range(ROUNDS):
                    if c:
                        pe.wait_ge(n_h2T, 2 * c)
                    for t in range(PART):
                        ins = nc.tensor.transpose(high[0:F, t // 4, (t % 4) * P:(t % 4 + 1) * P],
                                                  h[:, c * PART + t, :], ident[:, :])
                    ins.then_inc(n_tr, 1)
                    pe.wait_ge(n_hT, 2 * (c + 1))
                    if c:
                        pe.wait_ge(n_read, c)
                    for g in range(2):
                        for b in range(2):
                            ins = nc.tensor.matmul(low[:, 2 * g + b, 0:HALF], w1[:, g * P:(g + 1) * P],
                                                   hT[:, b * HALF:(b + 1) * HALF], start=True, stop=True)
                        ins.then_inc(n_a, 1)
                    pe.wait_ge(n_a1, 2 * (c + 1))
                    for g in range(2):
                        for b in range(2):
                            for k in range(2):
                                ins = nc.tensor.matmul(high[:, 2 * g + b, 0:HALF], w2[:, k, g * P:(g + 1) * P],
                                                       a1T[:, k, b * HALF:(b + 1) * HALF], start=(k == 0), stop=(k == 1))
                        ins.then_inc(n_h2, 1)
                    pe.wait_ge(n_h2T, 2 * (c + 1))
                    for t in range(PART):
                        for k in range(2):
                            ins = nc.tensor.matmul(low[:, t // 2, (t % 2) * HID1:(t % 2 + 1) * HID1],
                                                   h2T[:, k, t * P:(t + 1) * P], wc[:, k, :],
                                                   start=(k == 0), stop=(k == 1))
                    ins.then_inc(n_m, 1)

            @block.scalar
            def _(act):
                act.wait_ge(n_sq, 1)
                nc.scalar.activation(mean[:, :], mean[:, :], ACT.Sqrt).then_inc(n_sqd, 1)
                act.wait_ge(n_w, 16 * 6)
                for c in range(ROUNDS):
                    act.wait_ge(n_tr, c + 1)
                    if c:
                        act.wait_ge(n_a, 2 * c)
                    nc.scalar.copy(hT[:, 0:4 * P], high[0:F, 0, :]).then_inc(n_hT, 1)
                    nc.scalar.copy(hT[:, 4 * P:PN], high[0:F, 1, 0:PN - 4 * P]).then_inc(n_hT, 1)
                    for g in range(2):
                        act.wait_ge(n_a, 2 * c + g + 1)
                        if c:
                            act.wait_ge(n_h2, 2 * c)
                        nc.scalar.activation(a1T[:, g, :].rearrange("p (b n) -> p b n", b=2),
                                             low[:, 2 * g:2 * g + 2, 0:HALF], ACT.Relu, bias=b1[:, g:g + 1]
                                             ).then_inc(n_a1, 1)
                    for g in range(2):
                        act.wait_ge(n_h2, 2 * c + g + 1)
                        if c:
                            act.wait_ge(n_m, c)
                            act.wait_ge(n_dh, 16 * c)
                        nc.scalar.activation(h2T[:, g, :].rearrange("p (b n) -> p b n", b=2),
                                             high[:, 2 * g:2 * g + 2, 0:HALF], ACT.Identity, bias=b2[:, g:g + 1]
                                             ).then_inc(n_h2T, 1)

            @block.vector
            def _(dve):
                v = Line(dve, n_dve)
                layer_norm(dve, v, x, h, mean, cen, n_sq, n_sqd, 1)
                nc.vector.tensor_copy(cen[:, :, :], h[:, :, :]).then_inc(n_h, 1)
                for t in range(TILES):
                    w = min(P, COLS - t * P)
                    cell = edges[:, t, t * P:t * P + w]
                    v.add(nc.vector.tensor_tensor(cell, cell, ident[:, 0:w], ALU.subtract))
                dve.wait_ge(n_w, 16 * 6)
                for c in range(ROUNDS):
                    dve.wait_ge(n_m, c + 1)
                    for t0 in range(0, PART, 2):
                        n = min(2, PART - t0)
                        v.add(nc.vector.tensor_tensor(m[:, t0:t0 + n, :],
                                                      low[:, t0 // 2, 0:n * HID1].rearrange("p (t f) -> p t f", f=HID1),
                                                      bc(bconv[:, :], 1, n), ALU.add))
                    dve.wait_ge(n_dve, v.n)
                    nc.vector.tensor_scalar(m[:, :, :], m[:, :, :], 0.0, None, ALU.max).then_inc(n_read, 1)
                    dve.wait_ge(n_read, c + 1)
                    if c:
                        dve.wait_ge(n_dm, 32 * c)
                    v.then(nc.vector.tensor_copy(parts[:, :, 0, :], m[:, :, :]))
                    v.then(nc.vector.tensor_tensor(rest[:, :, :], m[:, :, :], parts[:, :, 0, :], ALU.subtract))
                    v.then(nc.vector.tensor_copy(parts[:, :, 1, :], rest[:, :, :]))
                    nc.vector.tensor_tensor(parts[:, :, 2, :], rest[:, :, :], parts[:, :, 1, :], ALU.subtract
                                            ).then_inc(n_split, 1)


def layer1_sum(nc, io, keep, d, sem):
    edges = keep["edges"]
    with ExitStack() as ctx:
        parts = ctx.enter_context(nc.sbuf_tensor("msg_parts", [P, 2, TILES, 3, P], BF16))
        stage = ctx.enter_context(nc.sbuf_tensor("agg_stage", [P, 2, CW], F32))
        acc = ctx.enter_context(nc.psum_tensor("acc1", [P, CHUNKS, 512], F32))
        m_load = [sem("m_load0"), sem("m_load1")]
        m_store = [sem("m_store0"), sem("m_store1")]
        m_sum, m_evac = sem("m_sum"), sem("m_evac")
        with nc.Block() as block:
            @block.sync
            def _(sp):
                for f in range(2):
                    sp.dma_start(parts[:, f, :, :, :], d["msg"][f]).then_inc(m_load[f], 16)
                for n in range(2 * CHUNKS):
                    sp.wait_ge(m_evac, n + 1)
                    c = n % CHUNKS
                    sp.dma_start(d["aggT"][n // CHUNKS, :, c * CW:(c + 1) * CW], stage[:, n % 2, :]
                                 ).then_inc(m_store[n % 2], 16)
                for s in m_store:
                    sp.wait_ge(s, 16 * CHUNKS)

            @block.tensor
            def _(pe):
                for f in range(2):
                    pe.wait_ge(m_load[f], 16)
                    with pe.Fori(0, CHUNKS) as n:
                        if f:
                            pe.wait_ge(m_evac, n + 1)
                        for a in range(3):
                            for k in range(TILES):
                                ins = nc.tensor.matmul(acc[:, bass.ds(n, 1), 0:CW], parts[:, f, k, a, :],
                                                       edges[:, k, bass.ds(n * CW, CW)],
                                                       start=(a == 0 and k == 0), stop=(a == 2 and k == TILES - 1))
                        ins.then_inc(m_sum, 1)

            @block.scalar
            def _(act):
                for n in range(2 * CHUNKS):
                    act.wait_ge(m_sum, n + 1)
                    if n >= 2:
                        act.wait_ge(m_store[n % 2], 16 * (n // 2))
                    nc.scalar.copy(stage[:, n % 2, :], acc[:, n % CHUNKS, 0:CW]).then_inc(m_evac, 1)


def layer1_post(nc, io, keep, d, sem):
    ident, x = keep["ident"], keep["x"]
    with ExitStack() as ctx:
        def sb(name, shape, dt=F32):
            return ctx.enter_context(nc.sbuf_tensor(name, shape, dt))

        w1, w2 = sb("post_w1", [P, 4, HID1]), sb("post_w2", [P, 2, F])
        b1, b2 = sb("post_b1", [P, 2]), sb("post_b2", [F, 1])
        hid = sb("hid", [P, 2, 4, CW])
        z = sb("z", [P, 2, CW])
        oT = sb("oT", [F, NPAD])
        zps = ctx.enter_context(nc.psum_tensor("zps", [P, 4, 512], F32))
        ops = ctx.enter_context(nc.psum_tensor("ops", [F, 2, 512], F32))
        xps = ctx.enter_context(nc.psum_tensor("xps", [P, TILES * F], F32))
        p_w, p_tail, p_z, p_zr, p_o, p_oT, p_x, p_dve = (sem("p_" + s) for s in "w tail z zr o oT x dve".split())
        p_load = [sem("p_load0"), sem("p_load1")]
        with nc.Block() as block:
            @block.sync
            def _(sp):
                sp.dma_start(w1[:, :, :], io["L1_gnn_post_w1"].rearrange("(k p) n -> p k n", p=P)).then_inc(p_w, 16)
                sp.dma_start(w2[:, :, :], io["L1_gnn_post_w2"].rearrange("(k p) n -> p k n", p=P)).then_inc(p_w, 16)
                sp.dma_start(b1[:, :], io["L1_gnn_post_b1"]).then_inc(p_w, 16)
                sp.dma_start(b2[:, :], io["L1_gnn_post_b2"].rearrange("(n a) -> n a", a=1)).then_inc(p_w, 16)
                for n in range(CHUNKS):
                    if n >= 2:
                        sp.wait_ge(p_z, n - 1)
                    at = slice(n * CW, (n + 1) * CW)
                    sp.dma_start(hid[:, n % 2, 0:2, :], d["h2T"][:, :, at].rearrange("k p n -> p k n")
                                 ).then_inc(p_load[n % 2], 16)
                    sp.dma_start(hid[:, n % 2, 2:4, :], d["aggT"][:, :, at].rearrange("k p n -> p k n")
                                 ).then_inc(p_load[n % 2], 16)

            @block.tensor
            def _(pe):
                pe.wait_ge(p_w, 16 * 4)

                def out_part(n):
                    pe.wait_ge(p_zr, n + 1)
                    if n >= 2:
                        pe.wait_ge(p_oT, n - 1)
                    for k in range(2):
                        ins = nc.tensor.matmul(ops[:, n % 2, 0:CW], w2[:, k, :], z[:, k, :],
                                               start=(k == 0), stop=(k == 1))
                    ins.then_inc(p_o, 1)

                for n in range(CHUNKS):
                    pe.wait_ge(p_load[n % 2], 32 * (n // 2 + 1))
                    if n >= 2:
                        pe.wait_ge(p_zr, n - 1)
                    for g in range(2):
                        for k in range(4):
                            ins = nc.tensor.matmul(zps[:, 2 * (n % 2) + g, 0:CW], w1[:, k, g * P:(g + 1) * P],
                                                   hid[:, n % 2, k, :], start=(k == 0), stop=(k == 3))
                    ins.then_inc(p_z, 1)
                    if n:
                        out_part(n - 1)
                out_part(CHUNKS - 1)
                pe.wait_ge(p_oT, CHUNKS)
                pe.wait_ge(p_tail, 1)
                for t in range(TILES):
                    ins = nc.tensor.transpose(xps[:, t * F:(t + 1) * F], oT[:, t * P:(t + 1) * P], ident[0:F, 0:F])
                ins.then_inc(p_x, 1)

            @block.scalar
            def _(act):
                act.wait_ge(p_w, 16 * 4)
                for n in range(CHUNKS):
                    act.wait_ge(p_z, n + 1)
                    if n:
                        act.wait_ge(p_o, n)
                    nc.scalar.activation(z[:, 0, :], zps[:, 2 * (n % 2), 0:CW], ACT.Relu, bias=b1[:, 0:1])
                    nc.scalar.activation(z[:, 1, :], zps[:, 2 * (n % 2) + 1, 0:CW], ACT.Relu, bias=b1[:, 1:2]
                                         ).then_inc(p_zr, 1)
                    act.wait_ge(p_o, n + 1)
                    nc.scalar.activation(oT[:, n * CW:(n + 1) * CW], ops[:, n % 2, 0:CW], ACT.Tanh, bias=b2[:, :]
                                         ).then_inc(p_oT, 1)

            @block.vector
            def _(dve):
                nc.vector.memset(oT[:, COLS:NPAD], 0.0).then_inc(p_tail, 1)
                dve.wait_ge(p_x, 1)
                v = Line(dve, p_dve)
                v.then(nc.vector.tensor_tensor(x[:, :, :], x[:, :, :],
                                               xps[:, :].rearrange("p (t f) -> p t f", f=F), ALU.add))


def layer2(nc, io, keep, d, sem):
    ident, edges, deg, x = (keep[n] for n in ("ident", "edges", "deg", "x"))
    with ExitStack() as ctx:
        def sb(name, shape, dt=F32):
            return ctx.enter_context(nc.sbuf_tensor(name, shape, dt))

        parts = sb("parts2", [P, TILES, P], BF16)
        h, cen, mean = sb("h_2", [P, TILES, F]), sb("cen2", [P, TILES, F]), sb("mean2", [P, TILES])
        agg = sb("agg2", [3 * F, NPAD])
        sel = sb("sel2", [3 * F, F])
        blank = sb("blank", [P, ROW])
        acc = ctx.enter_context(nc.psum_tensor("acc2", [P, CHUNKS, 512], F32))
        small = ctx.enter_context(nc.psum_tensor("small2", [P, TILES * F], F32))
        r_sel, r_dve, r_sq, r_sqd, r_parts, r_agg, r_evac, r_small, r_h, r_st, r_blank = (
            sem("r_" + s) for s in "sel dve sq sqd parts agg evac small h st blank".split())
        with nc.Block() as block:
            @block.sync
            def _(sp):
                for a in range(3):
                    sp.dma_start(sel[a * F:(a + 1) * F, :], ident[0:F, 0:F]).then_inc(r_sel, 16)
                sp.wait_ge(r_blank, 2)
                for t in range(TABLE // P):
                    sp.dma_start(d["table"][t * P:(t + 1) * P, :], blank[:, :]).then_inc(r_st, 16)
                sp.wait_ge(r_h, 1)
                sp.dma_start(d["h_table"].rearrange("(t p) f -> p t f", p=P), h[:, :, :]).then_inc(r_st, 16)
                sp.wait_ge(r_st, 16 * (TABLE // P + 1))

            @block.gpsimd
            def _(pool):
                nc.gpsimd.memset(blank[:, :], 0.0).then_inc(r_blank, 1)
                pool.wait_ge(r_blank, 1)
                nc.gpsimd.memset(blank[:, CH:ROW].rearrange("p (i a o) -> p i a o", a=2, o=F)[:, :, 0, :], 1.0
                                 ).then_inc(r_blank, 1)

            @block.tensor
            def _(pe):
                pe.wait_ge(r_parts, 1)
                times_edges(pe, nc, acc, [lambda k: parts[:, k, :]], edges, r_agg)
                pe.wait_ge(r_sel, 48)
                pe.wait_ge(r_evac, CHUNKS)
                for t in range(TILES):
                    ins = nc.tensor.matmul(small[:, t * F:(t + 1) * F], agg[:, t * P:(t + 1) * P], sel[:, :],
                                           start=True, stop=True)
                ins.then_inc(r_small, 1)

            @block.scalar
            def _(act):
                for n in range(2):
                    act.wait_ge(r_sq, n + 1)
                    nc.scalar.activation(mean[:, :], mean[:, :], ACT.Sqrt).then_inc(r_sqd, 1)
                    if n == 0:
                        for c in range(CHUNKS):
                            act.wait_ge(r_agg, c + 1)
                            nc.scalar.copy(agg[:, c * CW:(c + 1) * CW], acc[0:3 * F, c, 0:CW]).then_inc(r_evac, 1)

            @block.vector
            def _(dve):
                v = Line(dve, r_dve)
                v.add(nc.vector.memset(parts[:, :, :], 0.0))
                v.add(nc.vector.memset(agg[:, COLS:NPAD], 0.0))
                layer_norm(dve, v, x, h, mean, cen, r_sq, r_sqd, 1)
                v.then(nc.vector.tensor_tensor(h[:, :, :], h[:, :, :], bc(deg[:, 1, :], 2, F), ALU.mult))
                split3(dve, v, h[:, :, :], cen[:, :, :], [parts[:, :, a * F:(a + 1) * F] for a in range(3)])
                nc.vector.tensor_copy(mean[:, :], deg[:, 1, :]).then_inc(r_parts, 1)
                dve.wait_ge(r_small, 1)
                v.then(nc.vector.tensor_tensor(h[:, :, :], small[:, :].rearrange("p (t f) -> p t f", f=F),
                                               bc(deg[:, 2, :], 2, F), ALU.mult))
                v.then(nc.vector.tensor_tensor(x[:, :, :], x[:, :, :], h[:, :, :], ALU.add))
                layer_norm(dve, v, x, h, mean, cen, r_sq, r_sqd, 2)
                nc.vector.tensor_copy(cen[:, :, :], h[:, :, :]).then_inc(r_h, 1)


class Steps:

    def __init__(self, eng, sem):
        self.eng, self.sem, self.n = eng, sem, 0

    def add(self, ins):
        ins.then_inc(self.sem, 1)
        self.n += 1
        return self.n

    def wait(self, n):
        self.eng.wait_ge(self.sem, n)

    def then(self, ins):
        self.wait(self.add(ins))

    def restart(self):
        self.wait(self.n)
        self.eng.sem_clear(self.sem)
        self.n = 0


def attention(nc, io, keep, d, sem, out):
    ident, ones, x = keep["ident"], keep["ones"], keep["x"]
    with ExitStack() as ctx:
        def sb(name, shape, dt=F32, c=ctx):
            return c.enter_context(nc.sbuf_tensor(name, shape, dt))

        src = sb("src_slab", [P, STEPS], I32)
        row = sb("row_slab", [P, STEPS], I32)
        same = sb("same", [P, STEPS])
        drop = sb("drop", [P, STEPS])
        merge_row = sb("merge_row", [P, 1], I32)
        flags = sb("flags", [P, 2])
        lastrow = sb("lastrow", [P, ROW])
        attention_masks(nc, io, keep, sem, src, row, same, drop, merge_row, flags)
        attention_edges(nc, io, d, sem, src, row, same, drop, lastrow)
        attention_merge(nc, keep, d, sem, merge_row, flags, lastrow)
        attention_out(nc, keep, d, sem, out)


def attention_masks(nc, io, keep, sem, src, row, same, drop, merge_row, flags):
    with ExitStack() as ctx:
        def sb(name, shape, dt=F32):
            return ctx.enter_context(nc.sbuf_tensor(name, shape, dt))

        ints = sb("dst_ints", [P, 3, STEPS], I32)
        ids = sb("dst_ids", [P, 3, STEPS])
        t1, t2 = sb("mask1", [P, STEPS]), sb("mask2", [P, STEPS])
        head, headI, s = sb("head", [P, 1]), sb("headI", [P, 1], I32), sb("mask_small", [P, 4])
        k_load, k_head, k_dve = sem("k_load"), sem("k_head"), sem("k_dve")
        before, this, after = (ids[:, n, :] for n in range(3))
        with nc.Block() as block:
            @block.sync
            def _(sp):
                sp.dma_start(src[:, :], io["src"].rearrange("(p j) -> p j", p=P)).then_inc(k_load, 16)
                for n in range(3):
                    sp.dma_start(ints[:, n, :], io["dst_wide"][n:n + EPAD].rearrange("(p j) -> p j", p=P)
                                 ).then_inc(k_load, 16)
                sp.wait_ge(k_load, 64)

            @block.gpsimd
            def _(pool):
                nc.gpsimd.iota(headI[:, :], [[1, 1]], base=NPAD, channel_multiplier=1).then_inc(k_head, 1)

            @block.vector
            def _(dve):
                v = Line(dve, k_dve)
                dve.wait_ge(k_head, 1)
                v.add(nc.vector.tensor_copy(head[:, :], headI[:, :]))
                dve.wait_ge(k_load, 64)
                v.then(nc.vector.tensor_copy(ids[:, :, :], ints[:, :, :]))
                v.then(nc.vector.tensor_tensor(same[:, :], this, before, ALU.is_equal))
                whole, going = flags[:, 0:1], flags[:, 1:2]
                v.then(nc.vector.tensor_copy(going, same[:, 0:1]))
                v.then(nc.vector.memset(same[:, 0:1], 0.0))
                v.then(nc.vector.tensor_scalar(drop[:, :], same[:, :], BIG, -BIG, ALU.mult, ALU.add))
                first, last = ids[:, 1, 0:1], ids[:, 1, STEPS - 1:STEPS]
                v.then(nc.vector.tensor_tensor(s[:, 0:1], first, last, ALU.is_equal))
                v.then(nc.vector.tensor_tensor(whole, s[:, 0:1], going, ALU.mult))
                v.then(nc.vector.tensor_scalar(s[:, 1:2], first, 5.0, None, ALU.add))
                v.then(nc.vector.tensor_tensor(s[:, 1:2], s[:, 1:2], going, ALU.mult))
                v.then(nc.vector.tensor_scalar(s[:, 1:2], s[:, 1:2], -5.0, None, ALU.add))
                v.then(nc.vector.tensor_scalar(t1[:, :], this, -1.0, head[:, :], ALU.mult, ALU.add))
                v.then(nc.vector.scalar_tensor_tensor(t1[:, :], this, s[:, 1:2], t1[:, :], ALU.is_equal, ALU.mult))
                v.then(nc.vector.tensor_tensor(t1[:, :], t1[:, :], this, ALU.add))
                v.then(nc.vector.tensor_tensor(t2[:, :], this, after, ALU.is_equal))
                v.then(nc.vector.scalar_tensor_tensor(t1[:, :], t2[:, :], float(FAR), t1[:, :], ALU.mult, ALU.add))
                v.then(nc.vector.tensor_copy(row[:, :], t1[:, :]))
                v.then(nc.vector.tensor_tensor(s[:, 2:3], whole, t2[:, STEPS - 1:STEPS], ALU.mult))
                v.then(nc.vector.tensor_tensor(s[:, 2:3], going, s[:, 2:3], ALU.subtract))
                v.then(nc.vector.tensor_scalar(s[:, 3:4], s[:, 2:3], -float(FAR), float(FAR), ALU.mult, ALU.add))
                v.then(nc.vector.tensor_tensor(s[:, 3:4], s[:, 3:4], first, ALU.add))
                v.then(nc.vector.tensor_copy(merge_row[:, :], s[:, 3:4]))


def attention_edges(nc, io, d, sem, src, row, same, drop, lastrow):
    QUAD = BANKS // 2
    ACT_EARLY, ACT_LATE = range(2 * QUAD, 2 * QUAD + 2), range(2 * QUAD + 2, BLK)
    assert 2 * QUAD + QUAD < BLK <= 4 * QUAD
    with ExitStack() as ctx:
        def sb(name, shape, dt=F32):
            return ctx.enter_context(nc.sbuf_tensor(name, shape, dt))

        w = sb("w_edge", [F + 1, 2 * CH])
        ef = [sb(f"ef{u}", [F + 1, BLK * P]) for u in range(2)]
        hs = [sb(f"hs{u}", [P, BLK, F]) for u in range(2)]
        gix = [sb(f"gix{u}", [P, BLK], I32) for u in range(2)]
        six = [sb(f"six{u}", [P, BLK], I32) for u in range(2)]
        mk = [sb(f"mk{u}", [P, 2, BLK]) for u in range(2)]
        e = [sb(f"e{u}", [P, BLK, 2 * CH]) for u in range(2)]
        rows = [sb(f"rows{u}", [P, BLK, ROW]) for u in range(2)]
        scale = [sb(f"scale{u}", [P, CH]) for u in range(2)]
        wps = ctx.enter_context(nc.psum_tensor("wps", [P, BANKS, 2 * CH], F32))
        a_w, a_mult, a_read_v, a_read_s, a_e, a_sub, a_exp, a_rows, a_step, a_idx, a_go = (
            sem("a_" + s) for s in "w mult read_v read_s e sub exp rows step idx go".split())
        a_ef = [sem("a_ef0"), sem("a_ef1")]
        a_gather = [sem("a_gather0"), sem("a_gather1")]
        a_scatter = [sem("a_scatter0"), sem("a_scatter1")]
        DM = 16 * BLK
        ef_t = io["ef"]

        def product(s):
            return wps[:, s % BANKS, :]

        def four(ap):
            return ap.rearrange("p (i a o) -> p i a o", a=2, o=F)

        with nc.Block() as block:
            @block.sync
            def _(sp):
                sp.dma_start(w[:, :], io["w_edge"]).then_inc(a_w, 16)
                for u in range(2):
                    sp.dma_start(ef[u][:, :], ef_t[:, u * BLK * P:(u + 1) * BLK * P]).then_inc(a_ef[u], 16)
                with sp.Fori(0, BLOCKS // 2 - 1) as i:
                    for u in range(2):
                        sp.wait_ge(a_mult, i * 2 * BLK + (u + 1) * BLK)
                        sp.dma_start(ef[u][:, :], ef_t[:, bass.ds(i * (2 * BLK * P) + (2 + u) * BLK * P, BLK * P)]
                                     ).then_inc(a_ef[u], 16)
                sp.wait_ge(a_scatter[0], DM * (BLOCKS // 2))
                sp.wait_ge(a_scatter[1], DM * (BLOCKS // 2))

            @block.gpsimd
            def _(pool):
                def gather(u, b, copies):
                    pool_copy(gix[u], src, b)
                    pool.wait_ge(a_idx, copies)
                    pool.sem_inc(a_go, 1)
                    for s in range(BLK):
                        nc.gpsimd.indirect_dma_start(
                            out=hs[u][:, s, :], out_offset=None, in_=d["h_table"],
                            in_offset=bass.IndirectOffsetOnAxis(ap=gix[u][:, s:s + 1], axis=0)).then_inc(a_gather[u], 16)

                def pool_copy(to, table, b):
                    at = bass.ds(b * BLK, BLK) if not isinstance(b, int) else slice(b * BLK, (b + 1) * BLK)
                    nc.gpsimd.tensor_copy(to[:, :], table[:, at]).then_inc(a_idx, 1)

                def scatter(u, b, before, copies):
                    if before is not None:
                        pool.wait_ge(a_scatter[u], before)
                    pool_copy(six[u], row, b)
                    pool.wait_ge(a_idx, copies)
                    pool.wait_ge(a_rows, b + 1)
                    pool.sem_inc(a_go, 1)
                    for s in range(BLK):
                        nc.gpsimd.indirect_dma_start(
                            out=d["table"], out_offset=bass.IndirectOffsetOnAxis(ap=six[u][:, s:s + 1], axis=0),
                            in_=rows[u][:, s, :], in_offset=None, bounds_check=TABLE - 1, oob_is_err=False,
                        ).then_inc(a_scatter[u], 16)

                def turn(k):
                    for u in range(2):
                        pool.wait_ge(a_gather[u], k * DM + DM)
                        pool.wait_ge(a_read_v, k * 4 + (2 * (u + 1)))
                        pool.wait_ge(a_read_s, k * 4 + (2 + 2 * (u + 1)))
                        gather(u, k * 2 + (u + 2), k * 4 + (3 + 2 * u))
                        scatter(u, k * 2 + u, None if isinstance(k, int) else k * DM, k * 4 + (4 + 2 * u))

                gather(0, 0, 1)
                gather(1, 1, 2)
                turn(0)
                with pool.Fori(1, BLOCKS // 2 - 1) as k:
                    turn(k)
                n = 2 + 4 * (BLOCKS // 2 - 1)
                for u in range(2):
                    scatter(u, BLOCKS - 2 + u, DM * (BLOCKS // 2 - 1), n + 1 + u)

            @block.tensor
            def _(pe):
                pe.wait_ge(a_w, 16)
                with pe.Fori(0, BLOCKS // 2) as i:
                    for u in range(2):
                        pe.wait_ge(a_ef[u], (i + 1) * 16)
                        for s in range(BLK):
                            if s in (0, QUAD):
                                pe.wait_ge(a_read_s, i * 4 + (2 * u + s // QUAD + 1))
                            if s in (2 * QUAD, 3 * QUAD):
                                pe.wait_ge(a_read_v, i * 4 + (2 * u + s // QUAD - 1))
                            nc.tensor.matmul(product(s), ef[u][:, s * P:(s + 1) * P], w[:, :],
                                             start=True, stop=True).then_inc(a_mult, 1)

            @block.scalar
            def _(act):
                def multiply(u, b, gathered, steps):
                    act.wait_ge(a_gather[u], gathered)
                    for s in steps:
                        act.wait_ge(a_mult, b * BLK + (s + 1))
                        for f in range(F):
                            at = slice(f * 2 * F, (f + 1) * 2 * F)
                            ins = nc.scalar.mul(e[u][:, s, at], product(s)[:, at], hs[u][:, s, f:f + 1])
                        if s % QUAD == QUAD - 1 or s == BLK - 1:
                            ins.then_inc(a_read_s, 1)

                def exponentials(u, b):
                    act.wait_ge(a_sub, b + 1)
                    nc.scalar.activation(scale[u][:, :], scale[u][:, :], ACT.Exp).then_inc(a_exp, 1)
                    e2 = e[u][:, :, :].rearrange("p s (i a o) -> p (s i) a o", a=2, o=F)[:, :, 0, :]
                    nc.scalar.activation(e2, e2, ACT.Exp).then_inc(a_exp, 1)

                act.sem_inc(a_read_s, 2)
                multiply(0, 0, DM, [*ACT_EARLY, *ACT_LATE])

                def turn(u, b, gathered):
                    act.wait_ge(a_e, b + 1)
                    multiply(1 - u, b + 1, gathered, ACT_EARLY)
                    exponentials(u, b)
                    multiply(1 - u, b + 1, gathered, ACT_LATE)

                with act.Fori(0, BLOCKS // 2 - 1) as i:
                    turn(0, i * 2, i * DM + DM)
                    turn(1, i * 2 + 1, i * DM + 2 * DM)
                turn(0, BLOCKS - 2, BLOCKS // 2 * DM)
                exponentials(1, BLOCKS - 1)

            @block.vector
            def _(dve):
                def multiply(u, b, half):
                    s0, s1 = half * QUAD, (half + 1) * QUAD
                    dve.wait_ge(a_mult, b * BLK + s1)
                    nc.vector.tensor_tensor(
                        e[u][:, s0:s1, :].rearrange("p s (i c) -> p (s i) c", c=2 * F),
                        wps[:, s0:s1, :].rearrange("p s (i c) -> p (s i) c", c=2 * F),
                        bc(hs[u][:, s0:s1, :].rearrange("p s i -> p (s i)"), 2, 2 * F), ALU.mult
                    ).then_inc(a_read_v, 1)

                def masks(v, u, b):
                    at = bass.ds(b * BLK, BLK) if not isinstance(b, int) else slice(b * BLK, (b + 1) * BLK)
                    v.add(nc.vector.tensor_copy(mk[u][:, 0, :], drop[:, at]))
                    v.add(nc.vector.tensor_copy(mk[u][:, 1, :], same[:, at]))

                def shift(u, s):
                    return rows[u][:, s, 0:CH].rearrange("p (i o) -> p i o", o=F)

                def state(u, s):
                    return rows[u][:, s, CH:ROW]

                def up(u, s):
                    before = shift(u, s - 1) if s else shift(1 - u, BLK - 1)
                    return nc.vector.scalar_tensor_tensor(shift(u, s), before, mk[u][:, 0, s:s + 1],
                                                          four(e[u][:, s, :])[:, :, 0, :], ALU.add, ALU.max)

                def down(v, u):
                    for s in reversed(range(BLK - 1)):
                        v.then(nc.vector.scalar_tensor_tensor(shift(u, s), shift(u, s + 1), mk[u][:, 0, s + 1:s + 2],
                                                              shift(u, s), ALU.add, ALU.max))

                def subtract(v, u):
                    v.add(nc.vector.scalar_tensor_tensor(
                        scale[u][:, :].rearrange("p (i o) -> p i o", o=F), shift(1 - u, BLK - 1), mk[u][:, 0, 0:1],
                        shift(u, 0), ALU.add, ALU.subtract))
                    v.wait(v.n)
                    e2 = e[u][:, :, :].rearrange("p s (i a o) -> p s i a o", a=2, o=F)[:, :, :, 0, :]
                    nc.vector.tensor_tensor(e2, e2, rows[u][:, :, 0:CH].rearrange("p s (i o) -> p s i o", o=F),
                                            ALU.subtract).then_inc(a_sub, 1)

                def weigh(v, u, b):
                    dve.wait_ge(a_exp, b * 2 + 2)
                    both = e[u][:, :, :].rearrange("p s (i a o) -> p (s i) a o", a=2, o=F)
                    v.add(nc.vector.tensor_tensor(both[:, :, 1, :], both[:, :, 0, :], both[:, :, 1, :], ALU.mult))
                    v.then(nc.vector.tensor_tensor(
                        four(state(u, 0)), four(state(1 - u, BLK - 1)),
                        bc(scale[u][:, :].rearrange("p (i o) -> p i o", o=F), 2, 2), ALU.mult))

                def accumulate(u, s):
                    if s == 0:
                        return nc.vector.tensor_tensor(state(u, 0), state(u, 0), e[u][:, 0, :], ALU.add)
                    return nc.vector.scalar_tensor_tensor(state(u, s), state(u, s - 1), mk[u][:, 1, s:s + 1],
                                                          e[u][:, s, :], ALU.mult, ALU.add)

                v = Steps(dve, a_step)
                v.then(nc.vector.memset(rows[1][:, BLK - 1, :], 0.0))
                masks(v, 0, 0)
                v.wait(v.n)
                dve.wait_ge(a_gather[0], DM)
                multiply(0, 0, 0)
                multiply(0, 0, 1)
                dve.wait_ge(a_read_v, 2)
                dve.wait_ge(a_read_s, 2 + 2)
                for s in range(BLK):
                    v.then(up(0, s))
                dve.wait_ge(a_gather[1], DM)
                dve.sem_inc(a_e, 1)
                multiply(1, 1, 0)
                down(v, 0)
                subtract(v, 0)
                multiply(1, 1, 1)

                def block_step(v, u, b, i, more=True):
                    masks(v, u, b)
                    weigh(v, 1 - u, b - 1)
                    dve.wait_ge(a_read_v, b * 2 + 2)
                    if not isinstance(i, int):
                        dve.wait_ge(a_scatter[u], i * DM)
                    shifted = summed = None
                    for s in range(BLK):
                        if shifted is not None:
                            v.wait(shifted)
                        if s == 2 * QUAD:
                            dve.wait_ge(a_read_s, b * 2 + 4)
                        shifted = v.add(up(u, s))
                        if summed is not None:
                            v.wait(summed)
                        if s < BLK - 1:
                            summed = v.add(accumulate(1 - u, s))
                        else:
                            accumulate(1 - u, s).then_inc(a_rows, 1)
                    v.wait(shifted)
                    dve.wait_ge(a_rows, b)
                    if more:
                        dve.sem_inc(a_e, 1)
                        dve.wait_ge(a_gather[1 - u], (i + (1 + u)) * DM)
                        multiply(1 - u, b + 1, 0)
                    down(v, u)
                    subtract(v, u)
                    if more:
                        multiply(1 - u, b + 1, 1)

                block_step(v, 1, 1, 0)
                v.restart()
                with dve.Fori(0, BLOCKS // 2 - 2) as i:
                    block_step(v, 0, i * 2 + 2, i + 1)
                    block_step(v, 1, i * 2 + 3, i + 1)
                    v.restart()
                dve.wait_ge(a_scatter[0], (BLOCKS // 2 - 1) * DM)
                block_step(v, 0, BLOCKS - 2, BLOCKS // 2 - 1)
                dve.wait_ge(a_scatter[1], (BLOCKS // 2 - 1) * DM)
                block_step(v, 1, BLOCKS - 1, BLOCKS // 2 - 1, more=False)
                weigh(v, 1, BLOCKS - 1)
                for s in range(BLK):
                    v.then(accumulate(1, s))
                nc.vector.tensor_copy(lastrow[:, :], rows[1][:, BLK - 1, :]).then_inc(a_rows, 1)
                dve.wait_ge(a_rows, BLOCKS)


def attention_merge(nc, keep, d, sem, merge_row, flags, lastrow):
    ident, ones = keep["ident"], keep["ones"]
    with ExitStack() as ctx:
        def sb(name, shape, dt=F32):
            return ctx.enter_context(nc.sbuf_tensor(name, shape, dt))

        heads = sb("heads", [P, ROW])
        flat = sb("flat", [P, 2, 3, CH])
        diag = sb("diag", [P, 2, P])
        mask = sb("mask", [P, 2, P])
        cols = sb("cols", [P, 12, P])
        sh = sb("sh", [P, 2, P])
        tmp = sb("mtmp", [P, 2, 4, P])
        acc = sb("macc", [P, 2, 2, P])
        joined = sb("joined", [P, 2, 2, P])
        prod = sb("mprod", [P, P])
        outrow = sb("outrow", [P, ROW])
        tps = ctx.enter_context(nc.psum_tensor("tps", [P, 12, P], F32))
        mps = ctx.enter_context(nc.psum_tensor("mps", [P, 2, P], F32))
        ops = ctx.enter_context(nc.psum_tensor("mops", [P, 4, P], F32))
        j_load, j_dve, j_flat, j_tr, j_in, j_exp, j_ready, j_back, j_row, j_out = (
            sem("j_" + s) for s in "load dve flat tr in exp ready back row out".split())
        with nc.Block() as block:
            @block.sync
            def _(sp):
                sp.dma_start(heads[:, :], d["table"][NPAD:TABLE, :]).then_inc(j_load, 16)

            @block.gpsimd
            def _(pool):
                pool.wait_ge(j_row, 1)
                nc.gpsimd.indirect_dma_start(
                    out=d["table"], out_offset=bass.IndirectOffsetOnAxis(ap=merge_row[:, 0:1], axis=0),
                    in_=outrow[:, :], in_offset=None, bounds_check=TABLE - 1, oob_is_err=False).then_inc(j_out, 16)
                pool.wait_ge(j_out, 16)

            @block.tensor
            def _(pe):
                pe.wait_ge(j_flat, 1)
                nc.tensor.matmul(mps[:, :, :], ones[:, :], diag[:, :, :], start=True, stop=True).then_inc(j_tr, 1)
                for n in range(12):
                    c, k, g = n // 6, n // 2 % 3, n % 2
                    ins = nc.tensor.transpose(tps[:, n, :], flat[:, c, k, g * P:(g + 1) * P], ident[:, :])
                ins.then_inc(j_tr, 1)
                pe.wait_ge(j_ready, 1)
                for k in range(2):
                    for g in range(2):
                        ins = nc.tensor.transpose(ops[:, 2 * k + g, :], joined[:, k, g, :], ident[:, :])
                ins.then_inc(j_back, 1)

            @block.scalar
            def _(act):
                for n in range(2):
                    act.wait_ge(j_in, n + 1)
                    nc.scalar.activation(tmp[:, :, 2 * n:2 * n + 2, :], tmp[:, :, 2 * n:2 * n + 2, :], ACT.Exp
                                         ).then_inc(j_exp, 1)

            @block.vector
            def _(dve):
                v = Line(dve, j_dve)
                dve.wait_ge(j_load, 16)
                for c, r in ((0, lastrow), (1, heads)):
                    v.add(nc.vector.tensor_copy(flat[:, c, 0, :], r[:, 0:CH]))
                    v.add(nc.vector.tensor_copy(
                        flat[:, c, 1:3, :].rearrange("p a (i o) -> p a i o", o=F),
                        r[:, CH:ROW].rearrange("p (i a o) -> p a i o", a=2, o=F)))
                v.add(nc.vector.tensor_scalar(diag[:, 0, :], ident[:, :], flags[:, 0:1], None, ALU.mult))
                v.then(nc.vector.tensor_scalar(diag[:, 1, :], ident[:, :], flags[:, 1:2], None, ALU.mult))
                nc.vector.memset(joined[:, :, :, :], 0.0).then_inc(j_flat, 1)
                dve.wait_ge(j_tr, 1)
                v.then(nc.vector.tensor_scalar(mask[:, :, :], mps[:, :, :], BIG, -BIG, ALU.mult, ALU.add))
                dve.wait_ge(j_tr, 2)
                v.then(nc.vector.tensor_copy(cols[:, :, :], tps[:, :, :]))
                for g in range(2):
                    last_sh = cols[:, g, :]
                    v.then(nc.vector.tensor_tensor_scan(sh[:, g, :], mask[:, 0, :], last_sh, 0.0, ALU.add, ALU.max))
                    v.then(nc.vector.tensor_tensor(tmp[:, g, 0, :], last_sh, sh[:, g, :], ALU.subtract))
                    v.then(nc.vector.memset(tmp[:, g, 1, 0:1], -BIG))
                    v.then(nc.vector.tensor_tensor(tmp[:, g, 1, 1:P], sh[:, g, 0:P - 1], mask[:, 0, 1:P], ALU.add))
                    v.then(nc.vector.tensor_tensor(tmp[:, g, 1, 1:P], tmp[:, g, 1, 1:P], sh[:, g, 1:P], ALU.subtract))
                dve.wait_ge(j_dve, v.n)
                nc.vector.tensor_copy(prod[:, :], cols[:, 0, :]).then_inc(j_in, 1)
                dve.wait_ge(j_exp, 1)
                for g in range(2):
                    for k in range(2):
                        own = cols[:, 2 * (k + 1) + g, :]
                        v.then(nc.vector.tensor_tensor(own, own, tmp[:, g, 0, :], ALU.mult))
                        v.then(nc.vector.tensor_tensor_scan(acc[:, k, g, :], tmp[:, g, 1, :], own, 0.0,
                                                            ALU.mult, ALU.add))
                    first_sh = cols[:, 6 + g, :]
                    v.then(nc.vector.memset(tmp[:, g, 3, 0:1], -BIG))
                    v.then(nc.vector.tensor_tensor(tmp[:, g, 3, 1:P], sh[:, g, 0:P - 1], mask[:, 1, 1:P], ALU.add))
                    v.then(nc.vector.tensor_tensor(sh[:, g, :], tmp[:, g, 3, :], first_sh, ALU.max))
                    v.then(nc.vector.tensor_tensor(tmp[:, g, 2, :], first_sh, sh[:, g, :], ALU.subtract))
                    v.then(nc.vector.tensor_tensor(tmp[:, g, 3, :], tmp[:, g, 3, :], sh[:, g, :], ALU.subtract))
                nc.vector.tensor_copy(prod[:, :], cols[:, 0, :]).then_inc(j_in, 1)
                dve.wait_ge(j_exp, 2)
                for g in range(2):
                    for k in range(2):
                        first = cols[:, 6 + 2 * (k + 1) + g, :]
                        v.then(nc.vector.tensor_tensor(prod[:, 1:P], acc[:, k, g, 0:P - 1], tmp[:, g, 3, 1:P], ALU.mult))
                        v.then(nc.vector.tensor_tensor(joined[:, k, g, :], first, tmp[:, g, 2, :], ALU.mult))
                        v.then(nc.vector.tensor_tensor(joined[:, k, g, 1:P], joined[:, k, g, 1:P], prod[:, 1:P],
                                                       ALU.add))
                nc.vector.memset(outrow[:, 0:CH], 0.0).then_inc(j_ready, 1)
                dve.wait_ge(j_back, 1)
                nc.vector.tensor_copy(outrow[:, CH:ROW].rearrange("p (i a o) -> p a i o", a=2, o=F),
                                      ops[:, :, :].rearrange("p (a g) (i o) -> p a (g i) o", a=2, o=F)
                                      ).then_inc(j_row, 1)


def attention_out(nc, keep, d, sem, out):
    x = keep["x"]
    PART = 5
    ROUNDS = TILES // PART
    full = NODES // P
    with ExitStack() as ctx:
        def sb(name, shape, dt=F32):
            return ctx.enter_context(nc.sbuf_tensor(name, shape, dt))

        t = sb("t_rows", [P, 2, PART, 2 * CH])
        inv = sb("inv", [P, PART, CH])
        o = sb("o", [P, PART, F])
        z_load = [sem("z_load0"), sem("z_load1")]
        z_dve, z_out = sem("z_dve"), sem("z_out")
        view = d["table"][0:NPAD, CH:ROW].rearrange("(t p) c -> p t c", p=P)
        PER = 4
        with nc.Block() as block:
            @block.sync
            def _(sp):
                for r in range(ROUNDS):
                    if r >= 2:
                        sp.wait_ge(z_dve, PER * (r - 1))
                    sp.dma_start(t[:, r % 2, :, :], view[:, r * PART:(r + 1) * PART, :]).then_inc(z_load[r % 2], 16)
                sp.wait_ge(z_dve, PER * ROUNDS)
                sp.dma_start(out[0:full * P, :].rearrange("(t p) f -> p t f", p=P), x[:, 0:full, :]).then_inc(z_out, 16)
                sp.dma_start(out[full * P:NODES, :], x[0:NODES - full * P, full, :]).then_inc(z_out, 16)
                sp.wait_ge(z_out, 32)

            @block.vector
            def _(dve):
                v = Line(dve, z_dve)
                for r in range(ROUNDS):
                    dve.wait_ge(z_load[r % 2], 16 * (r // 2 + 1))
                    both = t[:, r % 2, :, :].rearrange("p t (i a o) -> p (t i) a o", a=2, o=F)
                    flat = inv[:, :, :].rearrange("p t (i o) -> p (t i) o", o=F)
                    v.then(nc.vector.reciprocal(flat, both[:, :, 0, :]))
                    v.then(nc.vector.tensor_tensor(flat, flat, both[:, :, 1, :], ALU.mult))
                    v.then(nc.vector.tensor_reduce(o[:, :, :], inv[:, :, :].rearrange("p t (i o) -> p t o i", o=F),
                                                   X, ALU.add))
                    part = x[:, r * PART:(r + 1) * PART, :]
                    v.then(nc.vector.tensor_tensor(part, part, o[:, :, :], ALU.add))


def kernel(**inputs):
    import numpy as np
    import concourse.bacc as bacc
    from concourse import mybir as mb
    from concourse.bass_utils import run_bass_kernel_spmd as run

    arrays = {k: np.ascontiguousarray(v) for k, v in inputs.items()}
    src, dst, x = arrays.pop("src"), arrays.pop("dst"), arrays.pop("x")
    ef = arrays.pop("edge_attr_16")
    fill = np.full(EPAD - EDGES, NODES, np.int32)
    arrays["x"] = np.concatenate([x, np.zeros((NPAD - NODES, F), x.dtype)])
    arrays["src"] = np.concatenate([src, fill])
    arrays["dst"] = np.concatenate([dst, fill])
    arrays["group_ends"] = arrays["dst"].reshape(1, GROUPS, GROUP)[:, :, -1]
    arrays["dst_wide"] = np.concatenate([np.full(1, -1, np.int32), dst, fill, np.full(1, NODES + 1, np.int32)])
    ef = np.concatenate([ef, np.zeros((EPAD - EDGES, F), ef.dtype)]).reshape(P, STEPS, F).transpose(2, 1, 0)
    arrays["ef"] = np.concatenate([ef, np.ones((1, STEPS, P), ef.dtype)]).reshape(F + 1, STEPS * P)
    wa, wm = arrays.pop("L3_gnn_W_attn"), arrays.pop("L3_gnn_W_msg")
    ba, bm = arrays.pop("L3_gnn_b_attn"), arrays.pop("L3_gnn_b_msg")
    wa, wm = np.concatenate([wa, ba[None]]), np.concatenate([wm, bm[None]])
    arrays["w_edge"] = np.stack([wa.reshape(F + 1, F, F), wm.reshape(F + 1, F, F)], axis=2).reshape(F + 1, 2 * CH)
    for name in ("pre_b1", "pre_b2", "post_b1"):
        arrays["L1_gnn_" + name] = arrays["L1_gnn_" + name].reshape(2, P).T
    arrays = {"in_" + k: np.ascontiguousarray(v) for k, v in arrays.items()}

    nc = bacc.Bacc("TRN2", target_bir_lowering=False, num_devices=1)
    io = {k[3:]: nc.dram_tensor(k, v.shape, mb.dt.from_np(v.dtype), kind="ExternalInput").ap()
          for k, v in arrays.items()}
    out = nc.dram_tensor("out_0", (NODES, F), mb.dt.float32, kind="ExternalOutput").ap()
    program(nc, io, out)
    return run(nc, [arrays], core_ids=[0]).results[0]["out_0"]
```

```python
from contextlib import ExitStack

import concourse.bass as bass
from concourse import mybir

F32 = mybir.dt.float32
BF16 = mybir.dt.bfloat16
I32 = mybir.dt.int32
ALU = mybir.AluOpType
ACT = mybir.ActivationFunctionType
X = mybir.AxisListType.X

P = 128
NODES = 3125
EDGES = 103125
F = 16
TILES = -(-NODES // P)
NPAD = TILES * P
EPAD = -(-EDGES // P) * P
HID0 = 64
HID1 = 256
LN_EPS = 1e-5

W = 16
STRIPS = -(-(NODES + 1) // W)
COLS = STRIPS * W
GROUP = 2 * P
GROUPS = EPAD // GROUP
PAIRS = GROUPS + STRIPS - 1
UNROLL = 20
BODY = 2 * UNROLL
TURNS = -(-PAIRS // BODY)
PAIR_TILES = -(-TURNS * BODY // P)
QW = TILES * W
HALFQ = QW // 2
QRING = 4
BANKS = 8

CHUNKS = 7
CW = COLS // CHUNKS

SLOTS = 4
GSTEPS = -(-(EPAD + (SLOTS - 1) * (NODES + 1)) // (SLOTS * P))
GTOTAL = GSTEPS * P
BG = 5
BLK = BG * SLOTS
BLOCKS = GSTEPS // BG
TURN = 4
TURNS_IN_CHUNK = 4
CH = F * F
ROW = 3 * CH
HEADS = P
TABLE = NPAD + HEADS
SPARE = NPAD - 1
GORDER = 2 * CHUNKS * TURNS_IN_CHUNK * TURN
BIG = 1e30
FAR = 1 << 20

assert EPAD % GROUP == 0 and COLS % CHUNKS == 0 and GSTEPS % BG == 0 and BLOCKS % 2 == 0
assert GORDER >= GSTEPS and GSTEPS <= 256 and (2 * CHUNKS) * (COLS // (2 * CHUNKS)) == COLS
assert PAIR_TILES * P >= TURNS * BODY and QW <= 512 and 2 * HALFQ <= 512


class Line:

    def __init__(self, eng, sem):
        self.eng, self.sem, self.n = eng, sem, 0

    def add(self, ins):
        ins.then_inc(self.sem, 1)
        self.n += 1

    def then(self, ins):
        self.add(ins)
        self.wait_all()

    def wait_all(self):
        self.eng.wait_ge(self.sem, self.n)


def bc(ap, axis, n):
    shape = list(ap.shape)
    shape.insert(axis, n)
    return ap.unsqueeze(axis).broadcast_to(shape)


def program(nc, io, out):
    with ExitStack() as ctx:
        def sem(name):
            return ctx.enter_context(nc.semaphore(name))

        def dram(name, shape, dt):
            return nc.dram_tensor(name, shape, dt, kind="Internal").ap()

        keep = {
            "x": ctx.enter_context(nc.sbuf_tensor("x_sb", [P, TILES, F], F32)),
            "ident": ctx.enter_context(nc.sbuf_tensor("ident", [P, P], F32)),
            "ones": ctx.enter_context(nc.sbuf_tensor("ones", [P, P], F32)),
            "src": ctx.enter_context(nc.sbuf_tensor("src_order", [P, GORDER, SLOTS], mybir.dt.int16)),
            "rows_made": sem("rows_made"),
        }
        d = {
            "strip_of_pair": dram("strip_of_pair", [PAIR_TILES, P], I32),
            "h2T": dram("h2T", [2, P, NPAD], F32),
            "msg": dram("msg", [2, P, TILES, 3, P], BF16),
            "aggT": dram("aggT", [2, P, COLS], F32),
            "edge_rows": dram("edge_rows", [EPAD + SLOTS, F + 1], F32),
            "edges_order": dram("edges_order", [GORDER // TURN * P, TURN * SLOTS * (F + 1)], F32),
            "node_wide": dram("node_wide", [GTOTAL + 2], F32),
            "start_wide": dram("start_wide", [GTOTAL + 1], F32),
            "ef_order": dram("ef_order", [F + 1, GORDER, 3, SLOTS, P], BF16),
            "h_table": dram("h_table", [NPAD + 1, F], F32),
            "table": dram("table", [TABLE, ROW], F32),
        }
        with ExitStack() as graph:
            keep["edges"] = graph.enter_context(nc.sbuf_tensor("edges", [P, TILES, COLS], BF16))
            keep["deg"] = graph.enter_context(nc.sbuf_tensor("deg", [P, 3, TILES], F32))
            keep["indeg"] = graph.enter_context(nc.sbuf_tensor("indeg", [P, TILES], F32))
            keep["missing"] = graph.enter_context(nc.sbuf_tensor("missing", [P, GORDER, SLOTS], BF16))
            build_edges(nc, io, keep, d, sem)
            degrees(nc, io, keep, d, sem)
            with nc.sbuf_tensor("start", [P, GORDER], I32) as keep["start"]:
                edge_groups(nc, io, keep, d, sem)
                layer0(nc, io, keep, d, sem)
            layer1_nodes(nc, io, keep, d, sem)
            layer1_sum(nc, io, keep, d, sem)
            layer1_post(nc, io, keep, d, sem)
            layer2(nc, io, keep, d, sem)
        attention(nc, io, keep, d, sem, out)


def build_edges(nc, io, keep, d, sem):
    ident, ones, edges = keep["ident"], keep["ones"], keep["edges"]
    with ExitStack() as ctx:
        def sb(name, shape, dt=F32):
            return ctx.enter_context(nc.sbuf_tensor(name, shape, dt))

        loT = sb("loT", [P, 2, PAIR_TILES * P])
        qT = sb("qT", [P, 2, PAIR_TILES * P])
        lane = sb("lane", [P, P])
        qcol = sb("qcol", [P, QW], BF16)
        strip = sb("strip", [1, PAIR_TILES * P], I32)
        b_consts, b_cast = sem("b_consts"), sem("b_cast")
        b_loaded, b_pairs, b_gather, b_stripdma = sem("b_loaded"), sem("b_pairs"), sem("b_gather"), sem("b_stripdma")
        b_dve, b_pe, b_evac = sem("b_dve"), sem("b_pe"), sem("b_evac")
        with ExitStack() as prep:
            def tb(name, shape, dt=F32):
                return prep.enter_context(nc.sbuf_tensor(name, shape, dt))

            ends = tb("ends", [1, GROUPS], I32)
            laneI = tb("laneI", [P, P], I32)
            qcolI = tb("qcolI", [P, QW], I32)
            pairI = tb("pairI", [P, PAIR_TILES], I32)
            groupI = tb("groupI", [1, GROUPS], I32)
            groupF = tb("groupF", [1, GROUPS])
            cut = tb("cut", [1, GROUPS])
            pair = tb("pair", [P, PAIR_TILES])
            below = tb("below", [P, GROUPS])
            gidx = tb("gidx", [P, PAIR_TILES])
            gidxI = tb("gidxI", [P, PAIR_TILES], I32)
            first = tb("first", [P, PAIR_TILES])
            stripI = tb("stripI", [P, PAIR_TILES], I32)
            srcg = tb("srcg", [P, PAIR_TILES, GROUP], I32)
            dstg = tb("dstg", [P, PAIR_TILES, GROUP], I32)
            t1 = tb("t1", [P, PAIR_TILES, GROUP])
            t2 = tb("t2", [P, PAIR_TILES, GROUP])
            cuts = prep.enter_context(nc.psum_tensor("cuts", [P, GROUPS], F32))
            tr = prep.enter_context(nc.psum_tensor("tr", [P, PAIR_TILES, 4, P], F32))

            with nc.Block() as block:
                @block.sync
                def _(sp):
                    sp.dma_start(ends[:, :], io["group_ends"]).then_inc(b_loaded, 16)
                    sp.wait_ge(b_pairs, 1)
                    sp.dma_start(d["strip_of_pair"].rearrange("k p -> p k"), stripI[:, :],
                                 allow_slow_non_contiguous=True).then_inc(b_stripdma, 16)
                    sp.wait_ge(b_stripdma, 16)
                    sp.dma_start(strip[:, :], d["strip_of_pair"].rearrange("(a k) p -> a (k p)", a=1)
                                 ).then_inc(b_stripdma, 16)
                    sp.wait_ge(b_stripdma, 32)
                    sp.wait_ge(b_gather, 16 * 2 * PAIR_TILES)
                    sp.dma_start(d["edge_rows"][:, 0:F], io["ef"]).then_inc(keep["rows_made"], 16)
                    sp.dma_start(d["edge_rows"][:, F:F + 1], io["src_more"].bitcast(F32),
                                 allow_slow_non_contiguous=True).then_inc(keep["rows_made"], 16)

                @block.gpsimd
                def _(pool):
                    nc.gpsimd.iota(laneI[:, :], [[1, P]], base=0, channel_multiplier=0)
                    nc.gpsimd.iota(qcolI[:, :], [[1, QW]], base=-HALFQ, channel_multiplier=0)
                    nc.gpsimd.iota(groupI[:, :], [[1, GROUPS]], base=1, channel_multiplier=0)
                    nc.gpsimd.iota(pairI[:, :], [[P, PAIR_TILES]], base=0, channel_multiplier=1)
                    nc.gpsimd.memset(ones[:, :], 1.0)
                    nc.gpsimd.memset(ident[:, :], 0.0).then_inc(b_consts, 1)
                    pool.wait_ge(b_consts, 1)
                    nc.gpsimd.affine_select(out=ident[:, :], in_=ident[:, :], compare_op=ALU.not_equal, fill=1.0,
                                            base=0, pattern=[[-1, P]], channel_multiplier=1).then_inc(b_consts, 1)
                    nc.gpsimd.memset(edges[:, 0:TILES // 2, :], 0.0).then_inc(b_consts, 1)
                    pool.wait_ge(b_pairs, 1)
                    for k in range(PAIR_TILES):
                        for rows, name in ((srcg, "src"), (dstg, "dst")):
                            nc.gpsimd.indirect_dma_start(
                                out=rows[:, k, :], out_offset=None,
                                in_=io[name].rearrange("(g e) -> g e", e=GROUP),
                                in_offset=bass.IndirectOffsetOnAxis(ap=gidxI[:, k:k + 1], axis=0),
                            ).then_inc(b_gather, 16)

                @block.tensor
                def _(pe):
                    pe.wait_ge(b_cast, 1)
                    pe.wait_ge(b_consts, 1)
                    nc.tensor.matmul(cuts[:, :], ones[0:1, :], cut[:, :], start=True, stop=True).then_inc(b_pe, 1)
                    pe.wait_ge(b_cast, 2)
                    pe.wait_ge(b_consts, 2)
                    for k in range(PAIR_TILES):
                        for s in range(2):
                            nc.tensor.transpose(tr[:, k, s, :], t1[:, k, s * P:(s + 1) * P], ident[:, :])
                            last = nc.tensor.transpose(tr[:, k, 2 + s, :], t2[:, k, s * P:(s + 1) * P], ident[:, :])
                        last.then_inc(b_pe, 1)

                @block.vector
                def _(dve):
                    v = Line(dve, b_dve)
                    dve.wait_ge(b_consts, 1)
                    v.add(nc.vector.tensor_copy(lane[:, :], laneI[:, :]))
                    v.add(nc.vector.tensor_copy(qcol[:, :], qcolI[:, :]))
                    v.add(nc.vector.tensor_copy(pair[:, :], pairI[:, :]))
                    v.add(nc.vector.tensor_copy(groupF[:, :], groupI[:, :]))
                    dve.wait_ge(b_loaded, 16)
                    v.then(nc.vector.tensor_scalar(ends[:, :], ends[:, :], 4, None, ALU.arith_shift_right))
                    nc.vector.tensor_tensor(cut[:, :], ends[:, :], groupF[:, :], ALU.add).then_inc(b_cast, 1)
                    dve.wait_ge(b_pe, 1)
                    for k in range(PAIR_TILES):
                        v.then(nc.vector.tensor_scalar(below[:, :], cuts[:, :], pair[:, k:k + 1], None, ALU.is_le))
                        v.then(nc.vector.tensor_reduce(gidx[:, k:k + 1], below[:, :], X, ALU.add))
                    v.then(nc.vector.tensor_scalar(gidx[:, :], gidx[:, :], float(GROUPS - 1), None, ALU.min))
                    v.add(nc.vector.tensor_copy(gidxI[:, :], gidx[:, :]))
                    v.then(nc.vector.tensor_tensor(first[:, :], pair[:, :], gidx[:, :], ALU.subtract))
                    v.then(nc.vector.tensor_scalar(stripI[:, :], first[:, :], float(STRIPS - 1), float(W),
                                                   ALU.min, ALU.mult))
                    nc.vector.tensor_scalar(first[:, :], first[:, :], float(W), None, ALU.mult).then_inc(b_pairs, 1)
                    v.add(nc.vector.memset(edges[:, TILES // 2:TILES, :], 0.0))
                    dve.wait_ge(b_dve, v.n)
                    dve.wait_ge(b_pairs, 1)
                    dve.wait_ge(b_consts, 3)
                    for t in range(TILES):
                        w = min(P, COLS - t * P)
                        v.add(nc.vector.tensor_copy(edges[:, t, t * P:t * P + w], ident[:, 0:w]))
                    dve.wait_ge(b_gather, 16 * 2 * PAIR_TILES)
                    v.then(nc.vector.tensor_copy(t1[:, :, :], dstg[:, :, :]))
                    v.then(nc.vector.tensor_tensor(t1[:, :, :], t1[:, :, :], bc(first[:, :], 2, GROUP), ALU.subtract))
                    v.then(nc.vector.tensor_scalar(t2[:, :, :], t1[:, :, :], 0.0, None, ALU.is_ge))
                    v.then(nc.vector.scalar_tensor_tensor(t2[:, :, :], t1[:, :, :], float(W - 1), t2[:, :, :],
                                                          ALU.is_le, ALU.mult))
                    v.then(nc.vector.tensor_scalar(dstg[:, :, :], srcg[:, :, :], 7, 4,
                                                   ALU.arith_shift_right, ALU.logical_shift_left))
                    v.then(nc.vector.tensor_tensor(t1[:, :, :], t1[:, :, :], dstg[:, :, :], ALU.add))
                    v.then(nc.vector.scalar_tensor_tensor(t1[:, :, :], t1[:, :, :], 4096.0 - HALFQ, t2[:, :, :],
                                                          ALU.add, ALU.mult))
                    v.then(nc.vector.tensor_scalar(t1[:, :, :], t1[:, :, :], -4096.0, None, ALU.add))
                    v.then(nc.vector.tensor_scalar(dstg[:, :, :], srcg[:, :, :], P - 1, None, ALU.bitwise_and))
                    nc.vector.tensor_scalar(t2[:, :, :], dstg[:, :, :], -1.0, None, ALU.mult).then_inc(b_cast, 1)
                    for k in range(PAIR_TILES):
                        dve.wait_ge(b_pe, 2 + k)
                        v.add(nc.vector.tensor_copy(qT[:, :, k * P:(k + 1) * P], tr[:, k, 0:2, :]))
                        v.add(nc.vector.tensor_copy(loT[:, :, k * P:(k + 1) * P], tr[:, k, 2:4, :]))

        lo_hot = sb("lo_hot", [P, 2, 2, UNROLL, P], BF16)
        q_hot = sb("q_hot", [P, QRING, 2, QW], BF16)
        acc = ctx.enter_context(nc.psum_tensor("acc", [P, BANKS, 512], F32))
        lo_far, lo_ready, q_ready = sem("lo_far"), sem("lo_ready"), sem("q_ready")
        multiplied, added = sem("multiplied"), sem("added")
        with nc.Block() as block:
            @block.scalar
            def _(act):
                with act.Fori(0, TURNS) as i:
                    for u in range(2):
                        act.wait_ge(multiplied, i * BODY + (u + 1) * UNROLL)
                        for k in range(UNROLL):
                            for s in range(2):
                                ins = nc.scalar.activation(lo_hot[:, u, s, k, :], lane[:, :], ACT.Abs,
                                                           bias=loT[:, s, bass.ds(i * BODY + u * UNROLL + k, 1)])
                        ins.then_inc(lo_far, 1)
                        act.wait_ge(lo_far, i * 2 + (u + 1))
                        nc.scalar.activation(lo_hot[:, u, :, :, :], lo_hot[:, u, :, :, :], ACT.Relu,
                                             scale=-1.0, bias=1.0).then_inc(lo_ready, 1)

            @block.vector
            def _(dve):
                dve.sem_inc(added, BANKS)
                strips = [dve.alloc_register(f"strip{k}") for k in range(BODY)]
                with dve.Fori(0, TURNS) as i:
                    def one_hot(k):
                        dve.wait_ge(multiplied, i * BODY + (BODY + k + 1 - QRING))
                        for s in range(2):
                            ins = nc.vector.tensor_scalar(q_hot[:, k % QRING, s, :], qcol[:, :],
                                                          qT[:, s, bass.ds(i * BODY + k, 1)], None, ALU.is_equal)
                        ins.then_inc(q_ready, 1)

                    def add(k):
                        s16 = dve.snap(strips[k], min_val=0, max_val=COLS - W)
                        dve.wait_ge(multiplied, i * BODY + (BODY + k + 1))
                        dve.wait_ge(added, i * BODY + (BANKS + k))
                        cell = edges[:, :, bass.ds(s16, W)]
                        nc.vector.tensor_tensor(cell, acc[:, k % BANKS, 0:QW].rearrange("p (t w) -> p t w", w=W),
                                                cell, ALU.add).then_inc(added, 1)

                    for k in range(BODY):
                        one_hot(k)
                        if k % 4 == 0:
                            dve.load(strips[k:k + 4], strip[0:1, bass.ds(i * BODY + k, 4)])
                        if k >= 2:
                            add(k - 2)
                    add(BODY - 2)
                    add(BODY - 1)

            @block.tensor
            def _(pe):
                pe.sem_inc(multiplied, BODY)
                with pe.Fori(0, TURNS) as i:
                    for k in range(BODY):
                        pe.wait_ge(lo_ready, i * 2 + (k // UNROLL + 1))
                        pe.wait_ge(q_ready, i * BODY + (k + 1))
                        pe.wait_ge(added, i * BODY + (k + 1))
                        for s in range(2):
                            ins = nc.tensor.matmul(acc[:, k % BANKS, 0:QW],
                                                   lo_hot[:, k // UNROLL, s, k % UNROLL, :],
                                                   q_hot[:, k % QRING, s, :], start=(s == 0), stop=(s == 1))
                        ins.then_inc(multiplied, 1)


def degrees(nc, io, keep, d, sem):
    ident, ones, edges, deg, indeg = (keep[n] for n in ("ident", "ones", "edges", "deg", "indeg"))
    with ExitStack() as ctx:
        def sb(name, shape, dt=F32):
            return ctx.enter_context(nc.sbuf_tensor(name, shape, dt))

        ones_b = sb("ones_b", [P, P], BF16)
        colsum = sb("colsum", [1, NPAD])
        raw = sb("raw", [P, 2, TILES])
        sums = ctx.enter_context(nc.psum_tensor("sums", [P, CHUNKS, 512], F32))
        turned = ctx.enter_context(nc.psum_tensor("turned", [P, TILES], F32))
        g_ready, g_sum, g_row, g_turn, g_raw, g_sqrt, g_dve, g_x = (
            sem(n) for n in ("g_ready", "g_sum", "g_row", "g_turn", "g_raw", "g_sqrt", "g_dve", "g_x"))
        with nc.Block() as block:
            @block.sync
            def _(sp):
                sp.dma_start(keep["x"][:, :, :], io["x"].rearrange("(t p) f -> p t f", p=P)).then_inc(g_x, 16)
                sp.wait_ge(g_x, 16)

            @block.tensor
            def _(pe):
                pe.wait_ge(g_ready, 1)
                times_edges(pe, nc, sums, [lambda k: ones_b[:, :]], edges, g_sum)
                pe.wait_ge(g_row, CHUNKS + 1)
                for t in range(TILES):
                    ins = nc.tensor.matmul(turned[:, t:t + 1], colsum[0:1, t * P:(t + 1) * P], ones[0:1, 0:1],
                                           start=True, stop=True)
                ins.then_inc(g_turn, 1)

            @block.vector
            def _(dve):
                nc.vector.tensor_copy(ones_b[:, :], ones[:, :]).then_inc(g_ready, 1)
                nc.vector.memset(colsum[:, COLS:NPAD], 1.0).then_inc(g_row, 1)
                for n in range(CHUNKS):
                    dve.wait_ge(g_sum, n + 1)
                    nc.vector.tensor_copy(colsum[:, n * CW:(n + 1) * CW], sums[0:1, n, 0:CW]).then_inc(g_row, 1)
                v = Line(dve, g_dve)
                dve.wait_ge(g_turn, 1)
                v.add(nc.vector.tensor_copy(raw[:, 0, :], turned[:, :]))
                v.add(nc.vector.tensor_scalar(indeg[:, :], turned[:, :], -1.0, None, ALU.add))
                v.then(nc.vector.tensor_scalar(raw[:, 1, :], turned[:, :], -1.0, 1.0, ALU.add, ALU.max))
                nc.vector.tensor_scalar(raw[:, 0, :], raw[:, 0, :], 1.0, None, ALU.max).then_inc(g_raw, 1)
                dve.wait_ge(g_sqrt, 1)
                v.add(nc.vector.reciprocal(deg[:, 0, :], raw[:, 0, :]))
                v.then(nc.vector.reciprocal(deg[:, 2, :], raw[:, 1, :]))

            @block.scalar
            def _(act):
                act.wait_ge(g_raw, 1)
                nc.scalar.activation(raw[:, :, :], raw[:, :, :], ACT.Sqrt).then_inc(g_sqrt, 1)
                act.wait_ge(g_sqrt, 1)


def edge_groups(nc, io, keep, d, sem):
    ones, indeg, start, missing = keep["ones"], keep["indeg"], keep["start"], keep["missing"]
    with ExitStack() as ctx:
        def sb(name, shape, dt=F32):
            return ctx.enter_context(nc.sbuf_tensor(name, shape, dt))

        upto, before = sb("upto", [P, P]), sb("before", [P, P])
        laneI, lane = sb("q_laneI", [P, 256], I32), sb("q_lane", [P, 256], BF16)
        numberI, number = sb("numberI", [P, GSTEPS], I32), sb("number", [P, GSTEPS])
        zero = sb("q_zero", [P, GSTEPS])
        ends = sb("q_ends", [1, 4])
        ng, ngI = sb("ng", [P, TILES]), sb("ngI", [P, TILES], I32)
        short = sb("short", [P, TILES])
        total, cum, gend = sb("q_total", [P, TILES]), sb("q_cum", [P, TILES]), sb("gend", [P, TILES])
        hi, hiI, lo, off = (sb("q_hi", [P, TILES]), sb("q_hiI", [P, TILES], I32), sb("q_lo", [P, TILES]),
                            sb("q_off", [P, TILES]))
        hi_hot = sb("hi_hot", [P, TILES, P], BF16)
        lo_hot = sb("glo_hot", [P, TILES, 2, GSTEPS], BF16)
        run = sb("q_run", [P, 2, GSTEPS])
        following = sb("q_following", [P, GSTEPS])
        tot2 = sb("q_tot2", [P, 2])
        small = ctx.enter_context(nc.psum_tensor("q_small", [P, 2, TILES], F32))
        hist = ctx.enter_context(nc.psum_tensor("q_hist", [P, 2, GSTEPS], F32))
        offs = ctx.enter_context(nc.psum_tensor("q_offs", [P, 2], F32))
        q_const, q_dve, q_ng, q_small, q_hot, q_hist, q_tot, q_offs, q_done, q_out = (
            sem("q_" + n) for n in "const dve ng small hot hist tot offs done out".split())
        with nc.Block() as block:
            @block.gpsimd
            def _(pool):
                nc.gpsimd.iota(laneI[:, :], [[1, 256]], base=0, channel_multiplier=0)
                nc.gpsimd.iota(numberI[:, :], [[1, GSTEPS]], base=0, channel_multiplier=GSTEPS)
                nc.gpsimd.memset(ends[:, 0:1], -1.0)
                nc.gpsimd.memset(ends[:, 1:4], float(NPAD))
                nc.gpsimd.memset(zero[:, :], 0.0)
                nc.gpsimd.affine_select(out=upto[:, :], in_=ones[:, :], compare_op=ALU.is_ge, fill=0.0, base=0,
                                        pattern=[[1, P]], channel_multiplier=-1)
                nc.gpsimd.affine_select(out=before[:, :], in_=ones[:, :], compare_op=ALU.is_ge, fill=0.0, base=-1,
                                        pattern=[[1, P]], channel_multiplier=-1).then_inc(q_const, 1)

            @block.tensor
            def _(pe):
                pe.wait_ge(q_const, 1)
                pe.wait_ge(q_ng, 1)
                nc.tensor.matmul(small[:, 0, :], upto[:, :], ng[:, :], start=True, stop=True)
                nc.tensor.matmul(small[:, 1, :], ones[:, :], ng[:, :], start=True, stop=True).then_inc(q_small, 1)
                for t in range(TILES):
                    pe.wait_ge(q_hot, t + 1)
                    ins = nc.tensor.matmul(hist[:, :, :], hi_hot[:, t, :], lo_hot[:, t, :, :],
                                           start=(t == 0), stop=(t == TILES - 1))
                ins.then_inc(q_hist, 1)
                pe.wait_ge(q_tot, 1)
                nc.tensor.matmul(offs[:, :], before[:, :], tot2[:, :], start=True, stop=True).then_inc(q_offs, 1)

            @block.vector
            def _(dve):
                v = Line(dve, q_dve)
                v.then(nc.vector.tensor_scalar(ng[:, :], indeg[:, :], float(SLOTS - 1), None, ALU.add))
                v.then(nc.vector.tensor_copy(ngI[:, :], ng[:, :]))
                v.then(nc.vector.tensor_scalar(ngI[:, :], ngI[:, :], SLOTS.bit_length() - 1, None,
                                               ALU.arith_shift_right))
                nc.vector.tensor_copy(ng[:, :], ngI[:, :]).then_inc(q_ng, 1)
                dve.wait_ge(q_ng, 1)
                v.add(nc.vector.scalar_tensor_tensor(short[:, :], ng[:, :], -float(SLOTS), indeg[:, :],
                                                     ALU.mult, ALU.add))
                dve.wait_ge(q_const, 1)
                v.add(nc.vector.tensor_copy(lane[:, :], laneI[:, :]))
                v.add(nc.vector.tensor_copy(number[:, :], numberI[:, :]))
                dve.wait_ge(q_small, 1)
                v.then(nc.vector.tensor_copy(total[:, :], small[:, 1, :]))
                v.then(nc.vector.tensor_tensor_scan(cum[:, :], zero[:, 0:TILES], total[:, :], 0.0, ALU.add, ALU.add))
                v.then(nc.vector.tensor_tensor(cum[:, :], cum[:, :], total[:, :], ALU.subtract))
                v.then(nc.vector.tensor_tensor(gend[:, :], cum[:, :], small[:, 0, :], ALU.add))
                v.then(nc.vector.tensor_scalar(hi[:, :], gend[:, :], 1.0 / GSTEPS, 0.5 / GSTEPS - 0.5,
                                               ALU.mult, ALU.add))
                v.then(nc.vector.tensor_copy(hiI[:, :], hi[:, :]))
                v.then(nc.vector.tensor_copy(hi[:, :], hiI[:, :]))
                v.then(nc.vector.scalar_tensor_tensor(lo[:, :], hi[:, :], -float(GSTEPS), gend[:, :],
                                                      ALU.mult, ALU.add))
                for op, edge, sign in ((ALU.is_lt, 0.0, 1.0), (ALU.is_ge, float(GSTEPS), -1.0)):
                    v.then(nc.vector.tensor_scalar(off[:, :], lo[:, :], edge, sign, op, ALU.mult))
                    v.then(nc.vector.tensor_tensor(hi[:, :], hi[:, :], off[:, :], ALU.subtract))
                    v.then(nc.vector.scalar_tensor_tensor(lo[:, :], off[:, :], float(GSTEPS), lo[:, :],
                                                          ALU.mult, ALU.add))
                for t in range(TILES):
                    nc.vector.tensor_scalar(hi_hot[:, t, :], lane[:, 0:P], hi[:, t:t + 1], None, ALU.is_equal)
                    nc.vector.tensor_scalar(lo_hot[:, t, 0, :], lane[:, 0:GSTEPS], lo[:, t:t + 1], None, ALU.is_equal)
                    nc.vector.tensor_scalar(lo_hot[:, t, 1, :], lane[:, 0:GSTEPS], lo[:, t:t + 1], short[:, t:t + 1],
                                            ALU.is_equal, ALU.mult).then_inc(q_hot, 1)
                dve.wait_ge(q_hist, 1)
                for a in range(2):
                    v.then(nc.vector.tensor_tensor_scan(run[:, a, :], zero[:, :], hist[:, a, :], 0.0,
                                                        ALU.add, ALU.add))
                nc.vector.tensor_copy(tot2[:, :], run[:, :, GSTEPS - 1]).then_inc(q_tot, 1)
                dve.wait_ge(q_offs, 1)
                for a in range(2):
                    v.then(nc.vector.tensor_scalar(run[:, a, :], run[:, a, :], offs[:, a:a + 1], None, ALU.add))
                v.then(nc.vector.tensor_scalar(run[:, 0, :], run[:, 0, :], float(SPARE), None, ALU.min))
                v.then(nc.vector.scalar_tensor_tensor(run[:, 1, :], number[:, :], float(SLOTS), run[:, 1, :],
                                                      ALU.mult, ALU.add))
                v.add(nc.vector.tensor_scalar(start[:, 0:GSTEPS], run[:, 1, :], float(EPAD), None, ALU.min))
                v.then(nc.vector.memset(start[:, GSTEPS:GORDER], EPAD))
                v.then(nc.vector.memset(missing[:, :, :], 0.0))
                nc.vector.tensor_copy(tot2[:, :], run[:, :, 0]).then_inc(q_done, 1)
                dve.wait_ge(q_out, 96)
                v.then(nc.vector.tensor_tensor(following[:, :], following[:, :], run[:, 1, :], ALU.subtract))
                for c in range(1, SLOTS):
                    v.then(nc.vector.tensor_scalar(missing[:, 0:GSTEPS, c], following[:, :], float(c), None, ALU.is_le))

            @block.sync
            def _(sp):
                sp.wait_ge(q_done, 1)
                sp.dma_start(d["node_wide"][1:GTOTAL + 1].rearrange("(p g) -> p g", p=P), run[:, 0, :]).then_inc(q_out, 16)
                sp.dma_start(d["start_wide"][0:GTOTAL].rearrange("(p g) -> p g", p=P), run[:, 1, :]).then_inc(q_out, 16)
                sp.dma_start(d["node_wide"][0:1].rearrange("(a n) -> a n", a=1), ends[:, 0:1]).then_inc(q_out, 16)
                sp.dma_start(d["node_wide"][GTOTAL + 1:GTOTAL + 2].rearrange("(a n) -> a n", a=1), ends[:, 1:2]
                             ).then_inc(q_out, 16)
                sp.dma_start(d["start_wide"][GTOTAL:GTOTAL + 1].rearrange("(a n) -> a n", a=1), ends[:, 2:3]
                             ).then_inc(q_out, 16)
                sp.wait_ge(q_out, 80)
                sp.dma_start(following[:, :], d["start_wide"][1:GTOTAL + 1].rearrange("(p g) -> p g", p=P)
                             ).then_inc(q_out, 16)
                sp.wait_ge(q_out, 96)


def layer_norm(dve, v, x, h, mean, cen, need_sqrt, sqrt_done, count):
    v.then(dve.tensor_reduce(mean[:, :], x[:, :, :], X, ALU.add))
    v.then(dve.tensor_scalar(mean[:, :], mean[:, :], 1.0 / F, None, ALU.mult))
    v.then(dve.tensor_tensor(cen[:, :, :], x[:, :, :], bc(mean[:, :], 2, F), ALU.subtract))
    v.then(dve.tensor_tensor(h[:, :, :], cen[:, :, :], cen[:, :, :], ALU.mult))
    v.then(dve.tensor_reduce(mean[:, :], h[:, :, :], X, ALU.add))
    dve.tensor_scalar(mean[:, :], mean[:, :], 1.0 / F, LN_EPS, ALU.mult, ALU.add).then_inc(need_sqrt, 1)
    dve.wait_ge(sqrt_done, count)
    v.then(dve.reciprocal(mean[:, :], mean[:, :]))
    v.then(dve.tensor_tensor(h[:, :, :], cen[:, :, :], bc(mean[:, :], 2, F), ALU.mult))
    v.then(dve.tensor_scalar(h[:, :, :], h[:, :, :], 0.0, None, ALU.max))


def split3(dve, v, value, rest, parts):
    v.then(dve.tensor_copy(parts[0], value))
    v.then(dve.tensor_tensor(rest, value, parts[0], ALU.subtract))
    v.then(dve.tensor_copy(parts[1], rest))
    v.then(dve.tensor_tensor(parts[2], rest, parts[1], ALU.subtract))


def times_edges(pe, nc, out, groups, edges, done):
    last = len(groups) - 1
    with pe.Fori(0, CHUNKS) as n:
        for g, lhs in enumerate(groups):
            for k in range(TILES):
                ins = nc.tensor.matmul(out[:, bass.ds(n, 1), 0:CW], lhs(k), edges[:, k, bass.ds(n * CW, CW)],
                                       start=(g == 0 and k == 0), stop=(g == last and k == TILES - 1))
        ins.then_inc(done, 1)


def layer0(nc, io, keep, d, sem):
    ident, ones, edges, deg, x = (keep[n] for n in ("ident", "ones", "edges", "deg", "x"))
    dis = deg[:, 0, :]
    with ExitStack() as ctx:
        def sb(name, shape, dt=F32):
            return ctx.enter_context(nc.sbuf_tensor(name, shape, dt))

        parts = sb("parts", [P, TILES, 2 * P], BF16)
        y = sb("y", [P, TILES, HID0])
        rest = sb("rest", [P, TILES, HID0])
        mean = sb("mean", [P, TILES])
        agg = sb("agg", [P, NPAD])
        w1, w2, w3 = sb("w1", [3 * F, HID0]), sb("w2", [2 * HID0, HID0]), sb("w3", [HID0, F])
        sel = sb("sel", [3 * F, F])
        b1, b2, b3 = sb("b1", [P, HID0]), sb("b2", [P, HID0]), sb("b3", [P, F])
        h = rest[:, :, 0:F]
        cen = rest[:, :, F:2 * F]
        h2T = sb("h2T_sb", [HID0, 4 * P])
        ix = [sb(f"ix{v}", [P, TURN], I32) for v in range(2)]
        got = [sb(f"got{v}", [P, TURN, SLOTS * (F + 1)]) for v in range(2)]
        y_gather = [sem("y_gather0"), sem("y_gather1")]
        y_stored = [sem("y_stored0"), sem("y_stored1")]
        y_idx, y_go = sem("y_idx"), sem("y_go")
        acc = ctx.enter_context(nc.psum_tensor("acc0", [P, CHUNKS, 512], F32))
        small = ctx.enter_context(nc.psum_tensor("small0", [P, 512], F32))
        (c_w, c_dve, c_sq, c_sqd, c_parts, c_agg, c_evac, c_small, c_used) = (
            sem(n) for n in ("c_w", "c_dve", "c_sq", "c_sqd", "c_parts", "c_agg", "c_evac", "c_small", "c_used"))
        G1 = [range(t, min(t + 8, TILES)) for t in range(0, TILES, 8)]
        G3 = [range(t, min(t + 4, TILES)) for t in range(0, TILES, 4)]
        with nc.Block() as block:
            @block.sync
            def _(sp):
                for a in range(3):
                    sp.dma_start(w1[a * F:(a + 1) * F, :], io["L0_gnn_W1"]).then_inc(c_w, 16)
                    sp.dma_start(sel[a * F:(a + 1) * F, :], ident[0:F, 0:F]).then_inc(c_w, 16)
                for a in range(2):
                    sp.dma_start(w2[a * HID0:(a + 1) * HID0, :], io["L0_gnn_W2"]).then_inc(c_w, 16)
                sp.dma_start(w3[:, :], io["L0_gnn_W3"]).then_inc(c_w, 16)
                for b, name in ((b1, "L0_gnn_b1"), (b2, "L0_gnn_b2"), (b3, "L0_gnn_b3")):
                    sp.dma_start(b[:, :], io[name].rearrange("(a n) -> a n", a=1).broadcast_to(list(b.shape))
                                 ).then_inc(c_w, 16)
                with sp.Fori(0, GORDER // TURN // 2) as i:
                    for v in range(2):
                        sp.wait_ge(y_gather[v], i * (16 * TURN) + 16 * TURN)
                        sp.dma_start(d["edges_order"][bass.ds(i * (2 * P) + v * P, P), :],
                                     got[v][:, :, :].rearrange("p g n -> p (g n)")).then_inc(y_stored[v], 16)
                sp.wait_ge(c_w, 16 * 12)
                for v in range(2):
                    sp.wait_ge(y_stored[v], 16 * (GORDER // TURN // 2))

            @block.gpsimd
            def _(pool):
                def fetch(i, v):
                    nc.gpsimd.tensor_copy(ix[v][:, :], keep["start"][:, bass.ds(i * (2 * TURN) + v * TURN, TURN)]
                                          ).then_inc(y_idx, 1)
                    pool.wait_ge(y_idx, i * 2 + (v + 1))
                    pool.sem_inc(y_go, 1)
                    for g in range(TURN):
                        nc.gpsimd.indirect_dma_start(
                            out=got[v][:, g, :], out_offset=None, in_=d["edge_rows"],
                            in_offset=bass.IndirectOffsetOnAxis(ap=ix[v][:, g:g + 1], axis=0)).then_inc(y_gather[v], 16)

                pool.wait_ge(keep["rows_made"], 32)
                for v in range(2):
                    fetch(0, v)
                with pool.Fori(1, GORDER // TURN // 2) as i:
                    for v in range(2):
                        pool.wait_ge(y_gather[v], i * (16 * TURN))
                        pool.wait_ge(y_stored[v], i * 16)
                        fetch(i, v)

            @block.scalar
            def _(act):
                act.wait_ge(c_sq, 1)
                nc.scalar.activation(mean[:, :], mean[:, :], ACT.Sqrt).then_inc(c_sqd, 1)
                for rnd, rows in ((0, 3 * F), (1, P), (2, 3 * F)):
                    for n in range(CHUNKS):
                        act.wait_ge(c_agg, rnd * CHUNKS + n + 1)
                        nc.scalar.activation(agg[0:rows, n * CW:(n + 1) * CW], acc[0:rows, n, 0:CW],
                                             ACT.Copy).then_inc(c_evac, 1)
                act.wait_ge(c_evac, 3 * CHUNKS)

            @block.tensor
            def _(pe):
                lo = lambda k: parts[:, k, 0:P]
                hi = lambda k: parts[:, k, P:2 * P]
                pe.wait_ge(c_parts, 1)
                times_edges(pe, nc, acc, [lo], edges, c_agg)
                pe.wait_ge(c_w, 16 * 12)
                pe.wait_ge(c_evac, CHUNKS)
                for g, tiles in enumerate(G1):
                    if g:
                        pe.wait_ge(c_used, g)
                    for t in tiles:
                        ins = nc.tensor.matmul(small[:, (t % 8) * HID0:(t % 8 + 1) * HID0],
                                               agg[0:3 * F, t * P:(t + 1) * P], w1[:, :], start=True, stop=True)
                    ins.then_inc(c_small, 1)
                pe.wait_ge(c_parts, 2)
                times_edges(pe, nc, acc, [lo, hi], edges, c_agg)
                pe.wait_ge(c_evac, 2 * CHUNKS)
                n1 = len(G1)
                for g, tiles in enumerate(G1):
                    pe.wait_ge(c_used, n1 + g)
                    for t in tiles:
                        ins = nc.tensor.matmul(small[:, (t % 8) * HID0:(t % 8 + 1) * HID0],
                                               agg[:, t * P:(t + 1) * P], w2[:, :], start=True, stop=True)
                    ins.then_inc(c_small, 1)
                for g, tiles in enumerate(G3):
                    pe.wait_ge(c_used, 2 * n1 + 2 * g)
                    for t in tiles:
                        ins = nc.tensor.transpose(small[0:HID0, (t % 4) * P:(t % 4 + 1) * P], y[:, t, :], ident[:, :])
                    ins.then_inc(c_small, 1)
                    pe.wait_ge(c_used, 2 * n1 + 2 * g + 1)
                    for t in tiles:
                        ins = nc.tensor.matmul(small[:, (t % 4) * F:(t % 4 + 1) * F],
                                               h2T[:, (t % 4) * P:(t % 4 + 1) * P], w3[:, :], start=True, stop=True)
                    ins.then_inc(c_small, 1)
                pe.wait_ge(c_parts, 3)
                times_edges(pe, nc, acc, [lo], edges, c_agg)
                pe.wait_ge(c_evac, 3 * CHUNKS)
                for t in range(TILES):
                    ins = nc.tensor.matmul(small[:, t * F:(t + 1) * F], agg[0:3 * F, t * P:(t + 1) * P], sel[:, :],
                                           start=True, stop=True)
                ins.then_inc(c_small, 1)

            @block.vector
            def _(dve):
                v = Line(dve, c_dve)
                v.add(nc.vector.memset(parts[:, :, :], 0.0))
                v.add(nc.vector.memset(agg[:, COLS:NPAD], 0.0))
                layer_norm(dve, v, x, h, mean, cen, c_sq, c_sqd, 1)
                v.then(nc.vector.tensor_tensor(y[:, :, 0:F], h, bc(dis, 2, F), ALU.mult))
                split3(dve, v, y[:, :, 0:F], cen, [parts[:, :, a * F:(a + 1) * F] for a in range(3)])
                nc.vector.tensor_copy(mean[:, :], dis).then_inc(c_parts, 1)
                dve.wait_ge(c_w, 16 * 12)
                small_count = 0
                for rnd, b in ((0, b1), (1, b2)):
                    for g, tiles in enumerate(G1):
                        a, e = tiles[0], tiles[-1] + 1
                        small_count += 1
                        dve.wait_ge(c_small, small_count)
                        part = y[:, a:e, :]
                        v.then(nc.vector.tensor_tensor(
                            part, small[:, 0:(e - a) * HID0].rearrange("p (t f) -> p t f", f=HID0),
                            bc(dis[:, a:e], 2, HID0), ALU.mult))
                        v.then(nc.vector.tensor_tensor(part, part, bc(b[:, :], 1, e - a), ALU.add))
                        nc.vector.tensor_scalar(part, part, 0.0, None, ALU.max).then_inc(c_used, 1)
                    if rnd == 0:
                        dve.wait_ge(c_used, len(G1))
                        v.then(nc.vector.tensor_tensor(y[:, :, :], y[:, :, :], bc(dis, 2, HID0), ALU.mult))
                        split3(dve, v, y[:, :, :], rest[:, :, :],
                               [parts[:, :, a * HID0:(a + 1) * HID0] for a in range(3)])
                        nc.vector.tensor_copy(mean[:, :], dis).then_inc(c_parts, 1)
                for g, tiles in enumerate(G3):
                    a, e = tiles[0], tiles[-1] + 1
                    small_count += 1
                    dve.wait_ge(c_small, small_count)
                    nc.vector.tensor_copy(h2T[:, 0:(e - a) * P], small[0:HID0, 0:(e - a) * P]).then_inc(c_used, 1)
                    small_count += 1
                    dve.wait_ge(c_small, small_count)
                    nc.vector.tensor_tensor(h[:, a:e, :], small[:, 0:(e - a) * F].rearrange("p (t f) -> p t f", f=F),
                                            bc(dis[:, a:e], 2, F), ALU.mult).then_inc(c_used, 1)
                dve.wait_ge(c_used, 2 * len(G1) + 2 * len(G3))
                v.add(nc.vector.memset(parts[:, :, 3 * F:2 * P], 0.0))
                split3(dve, v, h, cen, [parts[:, :, a * F:(a + 1) * F] for a in range(3)])
                nc.vector.tensor_copy(mean[:, :], dis).then_inc(c_parts, 1)
                small_count += 1
                dve.wait_ge(c_small, small_count)
                v.then(nc.vector.tensor_tensor(h, small[:, 0:TILES * F].rearrange("p (t f) -> p t f", f=F),
                                               bc(dis, 2, F), ALU.mult))
                v.then(nc.vector.tensor_tensor(h, h, bc(b3[:, :], 1, TILES), ALU.add))
                v.then(nc.vector.tensor_tensor(x[:, :, :], x[:, :, :], h, ALU.add))


def layer1_nodes(nc, io, keep, d, sem):
    ident, edges, x = keep["ident"], keep["edges"], keep["x"]
    PART = 5
    PN = PART * P
    HALF = PN // 2
    ROUNDS = TILES // PART
    with ExitStack() as ctx:
        def sb(name, shape, dt=F32):
            return ctx.enter_context(nc.sbuf_tensor(name, shape, dt))

        h, cen, mean = sb("h1", [P, TILES, F]), sb("cen1", [P, TILES, F]), sb("mean1", [P, TILES])
        w1, w2, wc = sb("pre_w1", [F, HID1]), sb("pre_w2", [P, 2, HID1]), sb("conv_w", [P, 2, HID1])
        b1, b2, bconv = sb("pre_b1", [P, 2]), sb("pre_b2", [P, 2]), sb("conv_b", [P, HID1])
        hT, a1T, h2T = sb("hT", [F, PN]), sb("a1T", [P, 2, PN]), sb("h2T_part", [P, 2, PN])
        m, rest = sb("m", [P, PART, HID1]), sb("m_rest", [P, PART, HID1])
        parts = sb("m_parts", [P, PART, 3, HID1], BF16)
        low = ctx.enter_context(nc.psum_tensor("low1", [P, 4, 512], F32))
        high = ctx.enter_context(nc.psum_tensor("high1", [P, 4, 512], F32))
        (n_w, n_dve, n_sq, n_sqd, n_h, n_tr, n_hT, n_a, n_a1, n_h2, n_h2T, n_m, n_read, n_split, n_dh, n_dm) = (
            sem("n_" + s) for s in "w dve sq sqd h tr hT a a1 h2 h2T m read split dh dm".split())
        with nc.Block() as block:
            @block.sync
            def _(sp):
                sp.dma_start(w1[:, :], io["L1_gnn_pre_w1"]).then_inc(n_w, 16)
                sp.dma_start(w2[:, :, :], io["L1_gnn_pre_w2"].rearrange("(k p) n -> p k n", p=P)).then_inc(n_w, 16)
                sp.dma_start(wc[:, :, :], io["L1_gnn_conv_w"].rearrange("(k p) n -> p k n", p=P)).then_inc(n_w, 16)
                sp.dma_start(b1[:, :], io["L1_gnn_pre_b1"]).then_inc(n_w, 16)
                sp.dma_start(b2[:, :], io["L1_gnn_pre_b2"]).then_inc(n_w, 16)
                sp.dma_start(bconv[:, :], io["L1_gnn_conv_b"].rearrange("(a n) -> a n", a=1).broadcast_to([P, HID1])
                             ).then_inc(n_w, 16)
                for c in range(ROUNDS):
                    sp.wait_ge(n_h2T, 2 * (c + 1))
                    sp.dma_start(d["h2T"][:, :, c * PN:(c + 1) * PN].rearrange("k p n -> p k n"), h2T[:, :, :]
                                 ).then_inc(n_dh, 16)
                    sp.wait_ge(n_split, c + 1)
                    for f in range(2):
                        sp.dma_start(d["msg"][f, :, c * PART:(c + 1) * PART, :, :],
                                     parts[:, :, :, f * P:(f + 1) * P]).then_inc(n_dm, 16)
                sp.wait_ge(n_dh, 16 * ROUNDS)
                sp.wait_ge(n_dm, 32 * ROUNDS)

            @block.tensor
            def _(pe):
                pe.wait_ge(n_w, 16 * 6)
                pe.wait_ge(n_h, 1)
                for c in range(ROUNDS):
                    if c:
                        pe.wait_ge(n_h2T, 2 * c)
                    for t in range(PART):
                        ins = nc.tensor.transpose(high[0:F, t // 4, (t % 4) * P:(t % 4 + 1) * P],
                                                  h[:, c * PART + t, :], ident[:, :])
                    ins.then_inc(n_tr, 1)
                    pe.wait_ge(n_hT, 2 * (c + 1))
                    if c:
                        pe.wait_ge(n_read, c)
                    for g in range(2):
                        for b in range(2):
                            ins = nc.tensor.matmul(low[:, 2 * g + b, 0:HALF], w1[:, g * P:(g + 1) * P],
                                                   hT[:, b * HALF:(b + 1) * HALF], start=True, stop=True)
                        ins.then_inc(n_a, 1)
                    pe.wait_ge(n_a1, 2 * (c + 1))
                    for g in range(2):
                        for b in range(2):
                            for k in range(2):
                                ins = nc.tensor.matmul(high[:, 2 * g + b, 0:HALF], w2[:, k, g * P:(g + 1) * P],
                                                       a1T[:, k, b * HALF:(b + 1) * HALF], start=(k == 0), stop=(k == 1))
                        ins.then_inc(n_h2, 1)
                    pe.wait_ge(n_h2T, 2 * (c + 1))
                    for t in range(PART):
                        for k in range(2):
                            ins = nc.tensor.matmul(low[:, t // 2, (t % 2) * HID1:(t % 2 + 1) * HID1],
                                                   h2T[:, k, t * P:(t + 1) * P], wc[:, k, :],
                                                   start=(k == 0), stop=(k == 1))
                    ins.then_inc(n_m, 1)

            @block.scalar
            def _(act):
                act.wait_ge(n_sq, 1)
                nc.scalar.activation(mean[:, :], mean[:, :], ACT.Sqrt).then_inc(n_sqd, 1)
                act.wait_ge(n_w, 16 * 6)
                for c in range(ROUNDS):
                    act.wait_ge(n_tr, c + 1)
                    if c:
                        act.wait_ge(n_a, 2 * c)
                    nc.scalar.copy(hT[:, 0:4 * P], high[0:F, 0, :]).then_inc(n_hT, 1)
                    nc.scalar.copy(hT[:, 4 * P:PN], high[0:F, 1, 0:PN - 4 * P]).then_inc(n_hT, 1)
                    for g in range(2):
                        act.wait_ge(n_a, 2 * c + g + 1)
                        if c:
                            act.wait_ge(n_h2, 2 * c)
                        nc.scalar.activation(a1T[:, g, :].rearrange("p (b n) -> p b n", b=2),
                                             low[:, 2 * g:2 * g + 2, 0:HALF], ACT.Relu, bias=b1[:, g:g + 1]
                                             ).then_inc(n_a1, 1)
                    for g in range(2):
                        act.wait_ge(n_h2, 2 * c + g + 1)
                        if c:
                            act.wait_ge(n_m, c)
                            act.wait_ge(n_dh, 16 * c)
                        nc.scalar.activation(h2T[:, g, :].rearrange("p (b n) -> p b n", b=2),
                                             high[:, 2 * g:2 * g + 2, 0:HALF], ACT.Identity, bias=b2[:, g:g + 1]
                                             ).then_inc(n_h2T, 1)

            @block.vector
            def _(dve):
                v = Line(dve, n_dve)
                layer_norm(dve, v, x, h, mean, cen, n_sq, n_sqd, 1)
                nc.vector.tensor_copy(cen[:, :, :], h[:, :, :]).then_inc(n_h, 1)
                for t in range(TILES):
                    w = min(P, COLS - t * P)
                    cell = edges[:, t, t * P:t * P + w]
                    v.add(nc.vector.tensor_tensor(cell, cell, ident[:, 0:w], ALU.subtract))
                dve.wait_ge(n_w, 16 * 6)
                for c in range(ROUNDS):
                    dve.wait_ge(n_m, c + 1)
                    for t0 in range(0, PART, 2):
                        n = min(2, PART - t0)
                        v.add(nc.vector.tensor_tensor(m[:, t0:t0 + n, :],
                                                      low[:, t0 // 2, 0:n * HID1].rearrange("p (t f) -> p t f", f=HID1),
                                                      bc(bconv[:, :], 1, n), ALU.add))
                    dve.wait_ge(n_dve, v.n)
                    nc.vector.tensor_scalar(m[:, :, :], m[:, :, :], 0.0, None, ALU.max).then_inc(n_read, 1)
                    dve.wait_ge(n_read, c + 1)
                    if c:
                        dve.wait_ge(n_dm, 32 * c)
                    v.then(nc.vector.tensor_copy(parts[:, :, 0, :], m[:, :, :]))
                    v.then(nc.vector.tensor_tensor(rest[:, :, :], m[:, :, :], parts[:, :, 0, :], ALU.subtract))
                    v.then(nc.vector.tensor_copy(parts[:, :, 1, :], rest[:, :, :]))
                    nc.vector.tensor_tensor(parts[:, :, 2, :], rest[:, :, :], parts[:, :, 1, :], ALU.subtract
                                            ).then_inc(n_split, 1)


def layer1_sum(nc, io, keep, d, sem):
    edges, deg, ident = keep["edges"], keep["deg"], keep["ident"]
    src_order, missing = keep["src"], keep["missing"]
    SCOLS = COLS // (2 * CHUNKS * TURNS_IN_CHUNK)
    with ExitStack() as ctx:
        def sb(name, shape, dt=F32):
            return ctx.enter_context(nc.sbuf_tensor(name, shape, dt))

        parts = sb("msg_parts", [P, 2, TILES, 3, P], BF16)
        stage = sb("agg_stage", [P, CW])
        got = [sb(f"got_order{v}", [P, TURN, SLOTS, F + 1]) for v in range(2)]
        efT = [sb(f"efT{v}", [SLOTS * (F + 1), TURN, 3, P], BF16) for v in range(2)]
        rowsum, raw = sb("rowsum", [P, TILES]), sb("outdeg", [P, TILES])
        acc = ctx.enter_context(nc.psum_tensor("acc1", [P, CHUNKS, 512], F32))
        tr = ctx.enter_context(nc.psum_tensor("tr1", [SLOTS * (F + 1), TURN, P], F32))
        m_load = [sem("m_load0"), sem("m_load1")]
        m_store, m_sum, m_evac, m_dve, m_raw, m_sqrt = (sem("m_" + n) for n in "store sum evac dve raw sqrt".split())
        u_load = [sem("u_load0"), sem("u_load1")]
        u_stored = [sem("u_stored0"), sem("u_stored1")]
        y_turned, y_part, y_rest, y_evac, y_copied, y_masked = (
            sem("u_" + n) for n in "turned part rest evac copied masked".split())

        def chunks(eng, f, do):
            do(f * CHUNKS)
            with eng.Fori(1, CHUNKS) as n:
                do(n + f * CHUNKS)

        def gathered(eng, j, r):
            eng.wait_ge(u_load[r % 2], (j * 2 + (r // 2 + 1)) * 16)

        with nc.Block() as block:
            @block.sync
            def _(sp):
                for f in range(2):
                    sp.dma_start(parts[:, f, :, :, :], d["msg"][f]).then_inc(m_load[f], 16)

                def load(turn, v):
                    sp.dma_start(got[v][:, :, :, :].rearrange("p g c k -> p (g c k)"),
                                 d["edges_order"][bass.ds(turn * P, P), :]).then_inc(u_load[v], 16)

                load(0, 0)
                load(1, 1)

                def chunk(f, j):
                    for r in range(TURNS_IN_CHUNK):
                        turn = j * TURNS_IN_CHUNK + r
                        sp.wait_ge(y_evac, turn + 1)
                        if r < TURNS_IN_CHUNK - 2 or not isinstance(j, int) or j < 2 * CHUNKS - 1:
                            sp.wait_ge(y_copied, turn + 1)
                            load(turn + 2, r % 2)
                        for c in range(SLOTS):
                            groups = bass.ds(j * (TURNS_IN_CHUNK * TURN) + r * TURN, TURN)
                            sp.dma_start(d["ef_order"][:, groups, :, c, :].rearrange("k g a p -> k (g a) p"),
                                         efT[r % 2][c * (F + 1):(c + 1) * (F + 1), :, :, :].rearrange(
                                             "k g a p -> k (g a) p")).then_inc(u_stored[r % 2], 16)
                    sp.wait_ge(m_evac, j + 1)
                    sp.dma_start(d["aggT"][f, :, bass.ds((j - f * CHUNKS) * CW, CW)], stage[:, :]).then_inc(m_store, 16)

                chunk(0, 0)
                with sp.Fori(1, CHUNKS) as n:
                    chunk(0, n)
                chunk(1, CHUNKS)
                with sp.Fori(1, CHUNKS - 1) as n:
                    chunk(1, n + CHUNKS)
                chunk(1, 2 * CHUNKS - 1)
                sp.wait_ge(m_store, 16 * 2 * CHUNKS)
                for s in u_stored:
                    sp.wait_ge(s, 16 * SLOTS * CHUNKS * TURNS_IN_CHUNK)

            @block.tensor
            def _(pe):
                def chunk(f, j):
                    if f:
                        pe.wait_ge(m_evac, j - f * CHUNKS + 1)
                    n, r = 0, 0
                    for a in range(3):
                        for k in range(TILES):
                            ins = nc.tensor.matmul(acc[:, bass.ds(j - f * CHUNKS, 1), 0:CW], parts[:, f, k, a, :],
                                                   edges[:, k, bass.ds((j - f * CHUNKS) * CW, CW)],
                                                   start=(n == 0), stop=(n == 3 * TILES - 1))
                            n += 1
                            if n == (r + 1) * 3 * TILES // TURNS_IN_CHUNK - 4:
                                pe.wait_ge(y_masked, j * TURNS_IN_CHUNK + (r + 1))
                                if r or not isinstance(j, int) or j > 0:
                                    pe.wait_ge(y_evac, j * TURNS_IN_CHUNK + r)
                                for g in range(TURN):
                                    turned = nc.tensor.transpose(
                                        tr[:, g, :], got[r % 2][:, g, :, :].rearrange("p c k -> p (c k)"), ident[:, :])
                                turned.then_inc(y_turned, 1)
                                r += 1
                    ins.then_inc(m_sum, 1)

                for f in range(2):
                    pe.wait_ge(m_load[f], 16)
                    chunks(pe, f, lambda j: chunk(f, j))

            @block.scalar
            def _(act):
                def chunk(j):
                    later = not isinstance(j, int) or j > 0
                    for r in range(TURNS_IN_CHUNK):
                        act.wait_ge(y_turned, j * TURNS_IN_CHUNK + (r + 1))
                        if r >= 2 or later:
                            act.wait_ge(u_stored[r % 2], (j * 2 + r // 2) * (16 * SLOTS))
                        nc.scalar.copy(efT[r % 2][:, :, 0, :], tr[:, :, :]).then_inc(y_part, 1)
                        act.wait_ge(y_rest, j * TURNS_IN_CHUNK + (r + 1))
                        nc.scalar.copy(efT[r % 2][:, :, 1, :], tr[:, :, :]).then_inc(y_part, 1)
                    act.wait_ge(m_sum, j + 1)
                    if later:
                        act.wait_ge(m_store, j * 16)

                for f in range(2):
                    def whole(j):
                        chunk(j)
                        nc.scalar.copy(stage[:, :], acc[:, bass.ds(j - f * CHUNKS, 1), 0:CW]).then_inc(m_evac, 1)
                    chunks(act, f, whole)
                act.wait_ge(m_raw, 1)
                nc.scalar.activation(raw[:, :], raw[:, :], ACT.Sqrt).then_inc(m_sqrt, 1)

            @block.vector
            def _(dve):
                def chunk(j):
                    for r in range(TURNS_IN_CHUNK):
                        gathered(dve, j, r)
                        groups = bass.ds(j * (TURNS_IN_CHUNK * TURN) + r * TURN, TURN)
                        nc.vector.scalar_tensor_tensor(
                            src_order[:, groups, :], missing[:, groups, :], float(NPAD),
                            got[r % 2][:, :, :, :].bitcast(I32)[:, :, :, F], ALU.mult, ALU.max).then_inc(y_copied, 1)
                        dve.wait_ge(y_copied, j * TURNS_IN_CHUNK + (r + 1))
                        nc.vector.tensor_scalar(got[r % 2][:, :, :, F], missing[:, groups, :], -BIG, None, ALU.mult
                                                ).then_inc(y_masked, 1)
                        turn = j * TURNS_IN_CHUNK + r
                        nc.vector.tensor_reduce(
                            rowsum[:, :], edges[:, :, bass.ds(j * (TURNS_IN_CHUNK * SCOLS) + r * SCOLS, SCOLS)],
                            X, ALU.add).then_inc(m_dve, 1)
                        dve.wait_ge(m_dve, turn * 2 + 2)
                        nc.vector.tensor_tensor(raw[:, :], raw[:, :], rowsum[:, :], ALU.add).then_inc(m_dve, 1)
                        dve.wait_ge(y_part, turn * 2 + 1)
                        nc.vector.tensor_tensor(tr[:, :, :], tr[:, :, :], efT[r % 2][:, :, 0, :], ALU.subtract
                                                ).then_inc(y_rest, 1)
                        dve.wait_ge(y_part, turn * 2 + 2)
                        nc.vector.tensor_tensor(efT[r % 2][:, :, 2, :], tr[:, :, :], efT[r % 2][:, :, 1, :],
                                                ALU.subtract).then_inc(y_evac, 1)

                nc.vector.memset(raw[:, :], 0.0).then_inc(m_dve, 1)
                for f in range(2):
                    chunks(dve, f, chunk)
                v = Line(dve, m_dve)
                v.n = 1 + 2 * (2 * CHUNKS * TURNS_IN_CHUNK)
                v.wait_all()
                nc.vector.tensor_scalar(raw[:, :], raw[:, :], 1.0, None, ALU.max).then_inc(m_raw, 1)
                dve.wait_ge(m_sqrt, 1)
                v.then(nc.vector.reciprocal(deg[:, 1, :], raw[:, :]))


def layer1_post(nc, io, keep, d, sem):
    ident, x = keep["ident"], keep["x"]
    with ExitStack() as ctx:
        def sb(name, shape, dt=F32):
            return ctx.enter_context(nc.sbuf_tensor(name, shape, dt))

        w1, w2 = sb("post_w1", [P, 4, HID1]), sb("post_w2", [P, 2, F])
        b1, b2 = sb("post_b1", [P, 2]), sb("post_b2", [F, 1])
        hid = sb("hid", [P, 2, 4, CW])
        z = sb("z", [P, 2, CW])
        oT = sb("oT", [F, NPAD])
        zps = ctx.enter_context(nc.psum_tensor("zps", [P, 4, 512], F32))
        ops = ctx.enter_context(nc.psum_tensor("ops", [F, 2, 512], F32))
        xps = ctx.enter_context(nc.psum_tensor("xps", [P, TILES * F], F32))
        p_w, p_tail, p_z, p_zr, p_o, p_oT, p_x, p_dve = (sem("p_" + s) for s in "w tail z zr o oT x dve".split())
        p_load = [sem("p_load0"), sem("p_load1")]
        with nc.Block() as block:
            @block.sync
            def _(sp):
                sp.dma_start(w1[:, :, :], io["L1_gnn_post_w1"].rearrange("(k p) n -> p k n", p=P)).then_inc(p_w, 16)
                sp.dma_start(w2[:, :, :], io["L1_gnn_post_w2"].rearrange("(k p) n -> p k n", p=P)).then_inc(p_w, 16)
                sp.dma_start(b1[:, :], io["L1_gnn_post_b1"]).then_inc(p_w, 16)
                sp.dma_start(b2[:, :], io["L1_gnn_post_b2"].rearrange("(n a) -> n a", a=1)).then_inc(p_w, 16)
                for n in range(CHUNKS):
                    if n >= 2:
                        sp.wait_ge(p_z, n - 1)
                    at = slice(n * CW, (n + 1) * CW)
                    sp.dma_start(hid[:, n % 2, 0:2, :], d["h2T"][:, :, at].rearrange("k p n -> p k n")
                                 ).then_inc(p_load[n % 2], 16)
                    sp.dma_start(hid[:, n % 2, 2:4, :], d["aggT"][:, :, at].rearrange("k p n -> p k n")
                                 ).then_inc(p_load[n % 2], 16)

            @block.tensor
            def _(pe):
                pe.wait_ge(p_w, 16 * 4)

                def out_part(n):
                    pe.wait_ge(p_zr, n + 1)
                    if n >= 2:
                        pe.wait_ge(p_oT, n - 1)
                    for k in range(2):
                        ins = nc.tensor.matmul(ops[:, n % 2, 0:CW], w2[:, k, :], z[:, k, :],
                                               start=(k == 0), stop=(k == 1))
                    ins.then_inc(p_o, 1)

                for n in range(CHUNKS):
                    pe.wait_ge(p_load[n % 2], 32 * (n // 2 + 1))
                    if n >= 2:
                        pe.wait_ge(p_zr, n - 1)
                    for g in range(2):
                        for k in range(4):
                            ins = nc.tensor.matmul(zps[:, 2 * (n % 2) + g, 0:CW], w1[:, k, g * P:(g + 1) * P],
                                                   hid[:, n % 2, k, :], start=(k == 0), stop=(k == 3))
                    ins.then_inc(p_z, 1)
                    if n:
                        out_part(n - 1)
                out_part(CHUNKS - 1)
                pe.wait_ge(p_oT, CHUNKS)
                pe.wait_ge(p_tail, 1)
                for t in range(TILES):
                    ins = nc.tensor.transpose(xps[:, t * F:(t + 1) * F], oT[:, t * P:(t + 1) * P], ident[0:F, 0:F])
                ins.then_inc(p_x, 1)

            @block.scalar
            def _(act):
                act.wait_ge(p_w, 16 * 4)
                for n in range(CHUNKS):
                    act.wait_ge(p_z, n + 1)
                    if n:
                        act.wait_ge(p_o, n)
                    nc.scalar.activation(z[:, 0, :], zps[:, 2 * (n % 2), 0:CW], ACT.Relu, bias=b1[:, 0:1])
                    nc.scalar.activation(z[:, 1, :], zps[:, 2 * (n % 2) + 1, 0:CW], ACT.Relu, bias=b1[:, 1:2]
                                         ).then_inc(p_zr, 1)
                    act.wait_ge(p_o, n + 1)
                    nc.scalar.activation(oT[:, n * CW:(n + 1) * CW], ops[:, n % 2, 0:CW], ACT.Tanh, bias=b2[:, :]
                                         ).then_inc(p_oT, 1)

            @block.vector
            def _(dve):
                nc.vector.memset(oT[:, COLS:NPAD], 0.0).then_inc(p_tail, 1)
                dve.wait_ge(p_x, 1)
                v = Line(dve, p_dve)
                v.then(nc.vector.tensor_tensor(x[:, :, :], x[:, :, :],
                                               xps[:, :].rearrange("p (t f) -> p t f", f=F), ALU.add))


def layer2(nc, io, keep, d, sem):
    ident, ones, edges, deg, x = (keep[n] for n in ("ident", "ones", "edges", "deg", "x"))
    with ExitStack() as ctx:
        def sb(name, shape, dt=F32):
            return ctx.enter_context(nc.sbuf_tensor(name, shape, dt))

        parts = sb("parts2", [P, TILES, P], BF16)
        h, cen, mean = sb("h_2", [P, TILES, F]), sb("cen2", [P, TILES, F]), sb("mean2", [P, TILES])
        agg = sb("agg2", [3 * F, NPAD])
        sel = sb("sel2", [3 * F, F])
        blank = sb("blank", [P, ROW])
        acc = ctx.enter_context(nc.psum_tensor("acc2", [P, CHUNKS, 512], F32))
        small = ctx.enter_context(nc.psum_tensor("small2", [P, TILES * F], F32))
        r_sel, r_dve, r_sq, r_sqd, r_parts, r_agg, r_evac, r_small, r_h, r_st, r_blank = (
            sem("r_" + s) for s in "sel dve sq sqd parts agg evac small h st blank".split())
        with nc.Block() as block:
            @block.sync
            def _(sp):
                for a in range(3):
                    sp.dma_start(sel[a * F:(a + 1) * F, :], ident[0:F, 0:F]).then_inc(r_sel, 16)
                sp.wait_ge(r_blank, 2)
                for t in range(TABLE // P):
                    sp.dma_start(d["table"][t * P:(t + 1) * P, :], blank[:, :]).then_inc(r_st, 16)
                sp.wait_ge(r_h, 1)
                sp.dma_start(d["h_table"][0:NPAD].rearrange("(t p) f -> p t f", p=P), h[:, :, :]).then_inc(r_st, 16)
                sp.dma_start(d["h_table"][NPAD:NPAD + 1, :], ones[0:1, 0:F]).then_inc(r_st, 16)
                sp.wait_ge(r_st, 16 * (TABLE // P + 2))

            @block.gpsimd
            def _(pool):
                nc.gpsimd.memset(blank[:, :], 0.0).then_inc(r_blank, 1)
                pool.wait_ge(r_blank, 1)
                nc.gpsimd.memset(blank[:, CH:ROW].rearrange("p (i a o) -> p i a o", a=2, o=F)[:, :, 0, :], 1.0
                                 ).then_inc(r_blank, 1)

            @block.tensor
            def _(pe):
                pe.wait_ge(r_parts, 1)
                times_edges(pe, nc, acc, [lambda k: parts[:, k, :]], edges, r_agg)
                pe.wait_ge(r_sel, 48)
                pe.wait_ge(r_evac, CHUNKS)
                for t in range(TILES):
                    ins = nc.tensor.matmul(small[:, t * F:(t + 1) * F], agg[:, t * P:(t + 1) * P], sel[:, :],
                                           start=True, stop=True)
                ins.then_inc(r_small, 1)

            @block.scalar
            def _(act):
                for n in range(2):
                    act.wait_ge(r_sq, n + 1)
                    nc.scalar.activation(mean[:, :], mean[:, :], ACT.Sqrt).then_inc(r_sqd, 1)
                    if n == 0:
                        for c in range(CHUNKS):
                            act.wait_ge(r_agg, c + 1)
                            nc.scalar.copy(agg[:, c * CW:(c + 1) * CW], acc[0:3 * F, c, 0:CW]).then_inc(r_evac, 1)

            @block.vector
            def _(dve):
                v = Line(dve, r_dve)
                v.add(nc.vector.memset(parts[:, :, :], 0.0))
                v.add(nc.vector.memset(agg[:, COLS:NPAD], 0.0))
                layer_norm(dve, v, x, h, mean, cen, r_sq, r_sqd, 1)
                v.then(nc.vector.tensor_tensor(h[:, :, :], h[:, :, :], bc(deg[:, 1, :], 2, F), ALU.mult))
                split3(dve, v, h[:, :, :], cen[:, :, :], [parts[:, :, a * F:(a + 1) * F] for a in range(3)])
                nc.vector.tensor_copy(mean[:, :], deg[:, 1, :]).then_inc(r_parts, 1)
                dve.wait_ge(r_small, 1)
                v.then(nc.vector.tensor_tensor(h[:, :, :], small[:, :].rearrange("p (t f) -> p t f", f=F),
                                               bc(deg[:, 2, :], 2, F), ALU.mult))
                v.then(nc.vector.tensor_tensor(x[:, :, :], x[:, :, :], h[:, :, :], ALU.add))
                layer_norm(dve, v, x, h, mean, cen, r_sq, r_sqd, 2)
                nc.vector.tensor_copy(cen[:, :, :], h[:, :, :]).then_inc(r_h, 1)


class Steps:

    def __init__(self, eng, sem):
        self.eng, self.sem, self.n = eng, sem, 0

    def add(self, ins):
        ins.then_inc(self.sem, 1)
        self.n += 1
        return self.n

    def wait(self, n):
        self.eng.wait_ge(self.sem, n)

    def then(self, ins):
        self.wait(self.add(ins))

    def restart(self):
        self.wait(self.n)
        self.eng.sem_clear(self.sem)
        self.n = 0


def attention(nc, io, keep, d, sem, out):
    ident, ones, x = keep["ident"], keep["ones"], keep["x"]
    with ExitStack() as ctx:
        def sb(name, shape, dt=F32, c=ctx):
            return c.enter_context(nc.sbuf_tensor(name, shape, dt))

        row = sb("row_slab", [P, GSTEPS], I32)
        marks = sb("marks", [P, GSTEPS, 2])
        merge_row = sb("merge_row", [P, 1], I32)
        flags = sb("flags", [P, 2])
        lastrow = sb("lastrow", [P, ROW])
        attention_masks(nc, keep, d, sem, row, marks, merge_row, flags)
        attention_edges(nc, io, keep, d, sem, row, marks, lastrow)
        attention_merge(nc, keep, d, sem, merge_row, flags, lastrow)
        attention_out(nc, keep, d, sem, out)


def attention_masks(nc, keep, d, sem, row, marks, merge_row, flags):
    with ExitStack() as ctx:
        def sb(name, shape, dt=F32):
            return ctx.enter_context(nc.sbuf_tensor(name, shape, dt))

        ids = sb("node_ids", [P, 3, GSTEPS])
        same = sb("same", [P, GSTEPS])
        t1, t2 = sb("mask1", [P, GSTEPS]), sb("mask2", [P, GSTEPS])
        head, headI, s = sb("head", [P, 1]), sb("headI", [P, 1], I32), sb("mask_small", [P, 4])
        k_load, k_head, k_dve = sem("k_load"), sem("k_head"), sem("k_dve")
        before, this, after = (ids[:, n, :] for n in range(3))
        with nc.Block() as block:
            @block.sync
            def _(sp):
                for n in range(3):
                    sp.dma_start(ids[:, n, :], d["node_wide"][n:n + GTOTAL].rearrange("(p j) -> p j", p=P)
                                 ).then_inc(k_load, 16)
                sp.wait_ge(k_load, 48)

            @block.gpsimd
            def _(pool):
                nc.gpsimd.iota(headI[:, :], [[1, 1]], base=NPAD, channel_multiplier=1).then_inc(k_head, 1)

            @block.vector
            def _(dve):
                v = Line(dve, k_dve)
                dve.wait_ge(k_head, 1)
                v.add(nc.vector.tensor_copy(head[:, :], headI[:, :]))
                dve.wait_ge(k_load, 48)
                v.then(nc.vector.tensor_tensor(same[:, :], this, before, ALU.is_equal))
                whole, going = flags[:, 0:1], flags[:, 1:2]
                v.then(nc.vector.tensor_copy(going, same[:, 0:1]))
                v.then(nc.vector.memset(same[:, 0:1], 0.0))
                v.add(nc.vector.tensor_scalar(marks[:, :, 0], same[:, :], BIG, -BIG, ALU.mult, ALU.add))
                v.then(nc.vector.tensor_copy(marks[:, :, 1], same[:, :]))
                first, last = ids[:, 1, 0:1], ids[:, 1, GSTEPS - 1:GSTEPS]
                v.then(nc.vector.tensor_tensor(s[:, 0:1], first, last, ALU.is_equal))
                v.then(nc.vector.tensor_tensor(whole, s[:, 0:1], going, ALU.mult))
                v.then(nc.vector.tensor_scalar(s[:, 1:2], first, 5.0, None, ALU.add))
                v.then(nc.vector.tensor_tensor(s[:, 1:2], s[:, 1:2], going, ALU.mult))
                v.then(nc.vector.tensor_scalar(s[:, 1:2], s[:, 1:2], -5.0, None, ALU.add))
                v.then(nc.vector.tensor_scalar(t1[:, :], this, -1.0, head[:, :], ALU.mult, ALU.add))
                v.then(nc.vector.scalar_tensor_tensor(t1[:, :], this, s[:, 1:2], t1[:, :], ALU.is_equal, ALU.mult))
                v.then(nc.vector.tensor_tensor(t1[:, :], t1[:, :], this, ALU.add))
                v.then(nc.vector.tensor_tensor(t2[:, :], this, after, ALU.is_equal))
                v.then(nc.vector.scalar_tensor_tensor(t1[:, :], t2[:, :], float(FAR), t1[:, :], ALU.mult, ALU.add))
                v.then(nc.vector.tensor_copy(row[:, :], t1[:, :]))
                v.then(nc.vector.tensor_tensor(s[:, 2:3], whole, t2[:, GSTEPS - 1:GSTEPS], ALU.mult))
                v.then(nc.vector.tensor_tensor(s[:, 2:3], going, s[:, 2:3], ALU.subtract))
                v.then(nc.vector.tensor_scalar(s[:, 3:4], s[:, 2:3], -float(FAR), float(FAR), ALU.mult, ALU.add))
                v.then(nc.vector.tensor_tensor(s[:, 3:4], s[:, 3:4], first, ALU.add))
                v.then(nc.vector.tensor_copy(merge_row[:, :], s[:, 3:4]))


def attention_edges(nc, io, keep, d, sem, row, marks, lastrow):
    src = keep["src"]
    EARLY = range(2 * SLOTS - 2, 2 * SLOTS)
    LATE = [*range(3 * SLOTS, 4 * SLOTS), *range(BLK - 2, BLK)]
    VSTEPS = {0: (0, SLOTS), 1: (SLOTS, EARLY[0]), 2: (2 * SLOTS, 3 * SLOTS), 4: (4 * SLOTS, BLK - 2)}
    NV, NS = 4, 3
    NM = 2
    assert BG == 5 and SLOTS == 4
    with ExitStack() as ctx:
        def sb(name, shape, dt=F32):
            return ctx.enter_context(nc.sbuf_tensor(name, shape, dt))

        KW = 3 * (F + 1) + 1
        K2 = 64 + KW
        w_full, w_rest = sb("w_full", [K2, 2 * CH]), sb("w_rest", [K2, 2 * CH])
        w = sb("w_edge", [K2, 3, 2 * CH], BF16)
        ef = [sb(f"ef{u}", [K2, BLK * P], BF16) for u in range(2)]
        hs = [sb(f"hs{u}", [P, BLK, F]) for u in range(2)]
        gix = [sb(f"gix{u}", [P, BLK], I32) for u in range(2)]
        six = [sb(f"six{u}", [P, BG], I32) for u in range(2)]
        mk = [sb(f"mk{u}", [P, BG, NM]) for u in range(2)]
        e = [sb(f"e{u}", [P, BLK, 2 * CH]) for u in range(2)]
        rows = [sb(f"rows{u}", [P, BG, ROW]) for u in range(2)]
        scale = [sb(f"scale{u}", [P, CH]) for u in range(2)]
        pairs = sb("pairs", [P, BG, 2 * F, F])
        wps = ctx.enter_context(nc.psum_tensor("wps", [P, BANKS, 2 * CH], F32))
        a_w, a_ones, a_split, a_mult, a_read_v, a_read_s, a_e, a_sub, a_exp, a_rows, a_step, a_idx, a_go = (
            sem("a_" + s) for s in "w ones split mult read_v read_s e sub exp rows step idx go".split())
        a_ef = [sem("a_ef0"), sem("a_ef1")]
        a_gather = [sem("a_gather0"), sem("a_gather1")]
        a_scatter = [sem("a_scatter0"), sem("a_scatter1")]
        GM, SM = 16 * BLK, 16 * BG
        ef_t = d["ef_order"].rearrange("k g a c p -> k g a (c p)")
        src_t = src[:, :, :].rearrange("p g c -> p (g c)")

        def bank(u, s):
            return BANKS // 2 * ((u * BG + s // SLOTS) % 2) + s % SLOTS

        def all_e2(u, g0, g1):
            return e[u][:, g0 * SLOTS:g1 * SLOTS, :].rearrange(
                "p (g c) (i a o) -> p g (c i) a o", c=SLOTS, a=2, o=F)[:, :, :, 0, :]

        def four(ap):
            return ap.rearrange("p (i a o) -> p i a o", a=2, o=F)

        def cols(b, n):
            return slice(b * n, (b + 1) * n) if isinstance(b, int) else bass.ds(b * n, n)

        with nc.Block() as block:
            @block.sync
            def _(sp):
                sp.wait_ge(a_ones, 1)
                for r in (0, 64):
                    for a in range(3):
                        sp.dma_start(w_full[r + a * (F + 1):r + (a + 1) * (F + 1), :], io["w_edge"][0:F + 1, :]
                                     ).then_inc(a_w, 16)
                    sp.dma_start(w_full[r + KW - 1:r + KW, :], io["w_edge"][F + 1:F + 2, :]).then_inc(a_w, 16)
                def features(u, b):
                    for r in (0, 64):
                        for a in range(3):
                            sp.dma_start(
                                ef[u][r + a * (F + 1):r + (a + 1) * (F + 1), :].rearrange("k (g n) -> k g n", g=BG),
                                ef_t[:, cols(b, BG), a, :]).then_inc(a_ef[u], 16)

                features(0, 0)
                features(1, 1)
                with sp.Fori(0, BLOCKS // 2 - 1) as i:
                    for u in range(2):
                        sp.wait_ge(a_mult, i * 2 * BLK + (u + 1) * BLK)
                        features(u, i * 2 + (2 + u))
                sp.wait_ge(a_scatter[0], SM * (BLOCKS // 2))
                sp.wait_ge(a_scatter[1], SM * (BLOCKS // 2))

            @block.gpsimd
            def _(pool):
                def gather(u, b, copies):
                    nc.gpsimd.tensor_copy(gix[u][:, :], src_t[:, cols(b, BLK)]).then_inc(a_idx, 1)
                    pool.wait_ge(a_idx, copies)
                    pool.sem_inc(a_go, 1)
                    for s in range(BLK):
                        nc.gpsimd.indirect_dma_start(
                            out=hs[u][:, s, :], out_offset=None, in_=d["h_table"],
                            in_offset=bass.IndirectOffsetOnAxis(ap=gix[u][:, s:s + 1], axis=0)).then_inc(a_gather[u], 16)

                def scatter(u, b, before, copies):
                    if before is not None:
                        pool.wait_ge(a_scatter[u], before)
                    nc.gpsimd.tensor_copy(six[u][:, :], row[:, cols(b, BG)]).then_inc(a_idx, 1)
                    pool.wait_ge(a_idx, copies)
                    pool.wait_ge(a_rows, b + 1)
                    pool.sem_inc(a_go, 1)
                    for g in range(BG):
                        nc.gpsimd.indirect_dma_start(
                            out=d["table"], out_offset=bass.IndirectOffsetOnAxis(ap=six[u][:, g:g + 1], axis=0),
                            in_=rows[u][:, g, :], in_offset=None, bounds_check=TABLE - 1, oob_is_err=False,
                        ).then_inc(a_scatter[u], 16)

                def turn(k):
                    for u in range(2):
                        pool.wait_ge(a_gather[u], k * GM + GM)
                        pool.wait_ge(a_read_v, k * 2 * NV + NV * (u + 2))
                        pool.wait_ge(a_read_s, k * 2 * NS + NS * (u + 2))
                        gather(u, k * 2 + (u + 2), k * 4 + (3 + 2 * u))
                        scatter(u, k * 2 + u, None if isinstance(k, int) else k * SM, k * 4 + (4 + 2 * u))

                nc.gpsimd.memset(w_full[:, :], 0.0)
                nc.gpsimd.memset(ef[0][:, :], 1.0)
                nc.gpsimd.memset(ef[1][:, :], 1.0).then_inc(a_ones, 1)
                gather(0, 0, 1)
                gather(1, 1, 2)
                turn(0)
                with pool.Fori(1, BLOCKS // 2 - 1) as k:
                    turn(k)
                n = 2 + 4 * (BLOCKS // 2 - 1)
                for u in range(2):
                    scatter(u, BLOCKS - 2 + u, SM * (BLOCKS // 2 - 1), n + 1 + u)

            @block.tensor
            def _(pe):
                pe.wait_ge(a_split, 1)
                with pe.Fori(0, BLOCKS // 2) as i:
                    for u in range(2):
                        pe.wait_ge(a_ef[u], i * 96 + 96)
                        for s in range(BLK):
                            if s == 0:
                                pe.wait_ge(a_read_s, i * 2 * NS + (u * NS + 2))
                            if s == SLOTS:
                                pe.wait_ge(a_read_s, i * 2 * NS + (u * NS + 3))
                                pe.wait_ge(a_read_v, i * 2 * NV + (u * NV + NV))
                            if s in (2 * SLOTS, 3 * SLOTS, 4 * SLOTS):
                                pe.wait_ge(a_read_v, i * 2 * NV + (u * NV + NV + s // SLOTS - 1))
                            if s == 3 * SLOTS:
                                pe.wait_ge(a_read_s, i * 2 * NS + (u * NS + NS + 1))
                            nc.tensor.matmul(wps[:, bank(u, s), :], ef[u][:, s * P:(s + 1) * P], w[:, 0, :],
                                             start=True, stop=False)
                            nc.tensor.matmul(wps[:, bank(u, s), :], ef[u][0:KW, s * P:(s + 1) * P], w[0:KW, 2, :],
                                             start=False, stop=True).then_inc(a_mult, 1)

            @block.scalar
            def _(act):
                def multiply(u, b, steps):
                    for s in steps:
                        act.wait_ge(a_mult, b * BLK + (s + 1))
                        for f in range(F):
                            at = slice(f * 2 * F, (f + 1) * 2 * F)
                            ins = nc.scalar.mul(e[u][:, s, at], wps[:, bank(u, s), at], hs[u][:, s, f:f + 1])
                        if s % SLOTS == SLOTS - 1:
                            ins.then_inc(a_read_s, 1)

                def exponentials(u, b):
                    act.wait_ge(a_sub, b * (BG + 1) + 1)
                    nc.scalar.activation(scale[u][:, :], scale[u][:, :], ACT.Exp).then_inc(a_exp, 1)
                    for n, g in enumerate(reversed(range(BG))):
                        act.wait_ge(a_sub, b * (BG + 1) + (n + 2))
                        e2 = all_e2(u, g, g + 1)[:, 0, :, :]
                        nc.scalar.activation(e2, e2, ACT.Exp).then_inc(a_exp, 1)

                act.sem_inc(a_read_s, NS)
                act.wait_ge(a_gather[0], GM)
                multiply(0, 0, EARLY)
                multiply(0, 0, LATE)

                def turn(u, b, gathered):
                    act.wait_ge(a_e, b + 1)
                    act.wait_ge(a_gather[1 - u], gathered)
                    multiply(1 - u, b + 1, EARLY)
                    exponentials(u, b)
                    multiply(1 - u, b + 1, LATE)

                with act.Fori(0, BLOCKS // 2 - 1) as i:
                    turn(0, i * 2, i * GM + GM)
                    turn(1, i * 2 + 1, i * GM + 2 * GM)
                turn(0, BLOCKS - 2, BLOCKS // 2 * GM)
                exponentials(1, BLOCKS - 1)

            @block.vector
            def _(dve):
                def multiply(u, b, g):
                    s0, s1 = VSTEPS[g]
                    dve.wait_ge(a_mult, b * BLK + s1)
                    nc.vector.tensor_tensor(
                        e[u][:, s0:s1, :].rearrange("p s (i c) -> p (s i) c", c=2 * F),
                        wps[:, bank(u, s0):bank(u, s0) + s1 - s0, :].rearrange("p s (i c) -> p (s i) c", c=2 * F),
                        bc(hs[u][:, s0:s1, :].rearrange("p s i -> p (s i)"), 2, 2 * F), ALU.mult
                    ).then_inc(a_read_v, 1)

                def masks(v, u, b):
                    v.add(nc.vector.tensor_copy(mk[u][:, :, :], marks[:, cols(b, BG), :]))

                def shift(u, g):
                    return rows[u][:, g, 0:CH].rearrange("p (i o) -> p i o", o=F)

                def state(u, g):
                    return rows[u][:, g, CH:ROW]

                def largest(v, u, b):
                    dve.wait_ge(a_read_v, b * NV + 2 * NV)
                    v.wait(v.n)
                    for g0, g1, read in ((0, 3, 1), (3, BG, NS)):
                        dve.wait_ge(a_read_s, b * NS + (NS + read))
                        e2 = all_e2(u, g0, g1)
                        v.then(nc.vector.tensor_tensor(pairs[:, g0:g1, :, :], e2[:, :, 0:2 * F, :],
                                                       e2[:, :, 2 * F:4 * F, :], ALU.max))
                        v.add(nc.vector.tensor_tensor(
                            rows[u][:, g0:g1, 0:CH].rearrange("p g (i o) -> p g i o", o=F),
                            pairs[:, g0:g1, 0:F, :], pairs[:, g0:g1, F:2 * F, :], ALU.max))

                def up(u, g):
                    before = shift(u, g - 1) if g else shift(1 - u, BG - 1)
                    return nc.vector.scalar_tensor_tensor(shift(u, g), before, mk[u][:, g, 0:1], shift(u, g),
                                                          ALU.add, ALU.max)

                def subtract(u, g):
                    e2 = e[u][:, g * SLOTS:(g + 1) * SLOTS, :].rearrange("p c (i a o) -> p c i a o", a=2, o=F)[
                        :, :, :, 0, :]
                    nc.vector.tensor_tensor(e2, e2, bc(shift(u, g), 1, SLOTS), ALU.subtract).then_inc(a_sub, 1)

                def rescale(u):
                    return nc.vector.scalar_tensor_tensor(
                        scale[u][:, :].rearrange("p (i o) -> p i o", o=F), shift(1 - u, BG - 1), mk[u][:, 0, 0:1],
                        shift(u, 0), ALU.add, ALU.subtract)

                def weigh(v, u, b):
                    dve.wait_ge(a_exp, (b + 1) * (BG + 1))
                    both = e[u][:, :, :].rearrange("p s (i a o) -> p (s i) a o", a=2, o=F)
                    v.then(nc.vector.tensor_tensor(both[:, :, 1, :], both[:, :, 0, :], both[:, :, 1, :], ALU.mult))
                    group = e[u][:, :, :].rearrange("p (g c) n -> p g (c n)", c=SLOTS)
                    half = SLOTS * CH
                    v.add(nc.vector.tensor_tensor(group[:, :, 0:half], group[:, :, 0:half], group[:, :, half:2 * half],
                                                  ALU.add))
                    v.then(nc.vector.tensor_tensor(
                        four(state(u, 0)), four(state(1 - u, BG - 1)),
                        bc(scale[u][:, :].rearrange("p (i o) -> p i o", o=F), 2, 2), ALU.mult))
                    v.add(nc.vector.tensor_tensor(group[:, :, 0:half // 2], group[:, :, 0:half // 2],
                                                  group[:, :, half // 2:half], ALU.add))

                def accumulate(u, g):
                    total = e[u][:, g * SLOTS, :]
                    if g == 0:
                        return nc.vector.tensor_tensor(state(u, 0), state(u, 0), total, ALU.add)
                    return nc.vector.scalar_tensor_tensor(state(u, g), state(u, g - 1), mk[u][:, g, 1:2],
                                                          total, ALU.mult, ALU.add)

                v = Steps(dve, a_step)
                dve.wait_ge(a_w, 128)
                split3(dve, v, w_full[:, :], w_rest[:, :], [w[:, a, :] for a in range(3)])
                nc.vector.tensor_copy(w[64:K2, 0, :], w[64:K2, 1, :]).then_inc(a_split, 1)
                v.then(nc.vector.memset(rows[1][:, BG - 1, :], 0.0))
                masks(v, 0, 0)
                dve.wait_ge(a_gather[0], GM)
                dve.sem_inc(a_read_v, NV)
                for g in (0, 1, 2, 4):
                    multiply(0, 0, g)
                largest(v, 0, 0)
                v.wait(v.n)
                for g in range(BG):
                    v.then(up(0, g))
                dve.sem_inc(a_e, 1)
                dve.wait_ge(a_gather[1], GM)
                multiply(1, 1, 0)
                multiply(1, 1, 1)

                def shifts_out(v, u, b, more=True):
                    for g in reversed(range(1, BG)):
                        v.then(nc.vector.scalar_tensor_tensor(
                            shift(u, g - 1), shift(u, g), mk[u][:, g, 0:1], shift(u, g - 1), ALU.add, ALU.max))
                    rescale(u).then_inc(a_sub, 1)
                    for g in (4, 3, 2):
                        subtract(u, g)
                    if more:
                        multiply(1 - u, b + 1, 2)
                    for g in (1, 0):
                        subtract(u, g)
                    if more:
                        multiply(1 - u, b + 1, 4)

                shifts_out(v, 0, 0)

                def block_step(v, u, b, i, more=True):
                    masks(v, u, b)
                    weigh(v, 1 - u, b - 1)
                    if not isinstance(i, int):
                        dve.wait_ge(a_scatter[u], i * SM)
                    largest(v, u, b)
                    v.wait(v.n)
                    shifted = summed = None
                    for g in range(BG):
                        if shifted is not None:
                            v.wait(shifted)
                        shifted = v.add(up(u, g))
                        if summed is not None:
                            v.wait(summed)
                        if g < BG - 1:
                            summed = v.add(accumulate(1 - u, g))
                        else:
                            accumulate(1 - u, g).then_inc(a_rows, 1)
                    v.wait(shifted)
                    dve.wait_ge(a_rows, b)
                    if more:
                        dve.sem_inc(a_e, 1)
                        dve.wait_ge(a_gather[1 - u], (i + (1 + u)) * GM)
                        multiply(1 - u, b + 1, 0)
                        multiply(1 - u, b + 1, 1)
                    shifts_out(v, u, b, more)

                block_step(v, 1, 1, 0)
                v.restart()
                with dve.Fori(0, BLOCKS // 2 - 2) as i:
                    block_step(v, 0, i * 2 + 2, i + 1)
                    block_step(v, 1, i * 2 + 3, i + 1)
                    v.restart()
                dve.wait_ge(a_scatter[0], (BLOCKS // 2 - 1) * SM)
                block_step(v, 0, BLOCKS - 2, BLOCKS // 2 - 1)
                dve.wait_ge(a_scatter[1], (BLOCKS // 2 - 1) * SM)
                block_step(v, 1, BLOCKS - 1, BLOCKS // 2 - 1, more=False)
                weigh(v, 1, BLOCKS - 1)
                v.wait(v.n)
                for g in range(BG):
                    v.then(accumulate(1, g))
                nc.vector.tensor_copy(lastrow[:, :], rows[1][:, BG - 1, :]).then_inc(a_rows, 1)
                dve.wait_ge(a_rows, BLOCKS)


def attention_merge(nc, keep, d, sem, merge_row, flags, lastrow):
    ident, ones = keep["ident"], keep["ones"]
    with ExitStack() as ctx:
        def sb(name, shape, dt=F32):
            return ctx.enter_context(nc.sbuf_tensor(name, shape, dt))

        heads = sb("heads", [P, ROW])
        flat = sb("flat", [P, 2, 3, CH])
        diag = sb("diag", [P, 2, P])
        mask = sb("mask", [P, 2, P])
        cols = sb("cols", [P, 12, P])
        sh = sb("sh", [P, 2, P])
        tmp = sb("mtmp", [P, 2, 4, P])
        acc = sb("macc", [P, 2, 2, P])
        joined = sb("joined", [P, 2, 2, P])
        prod = sb("mprod", [P, P])
        outrow = sb("outrow", [P, ROW])
        tps = ctx.enter_context(nc.psum_tensor("tps", [P, 12, P], F32))
        mps = ctx.enter_context(nc.psum_tensor("mps", [P, 2, P], F32))
        ops = ctx.enter_context(nc.psum_tensor("mops", [P, 4, P], F32))
        j_load, j_dve, j_flat, j_tr, j_in, j_exp, j_ready, j_back, j_row, j_out = (
            sem("j_" + s) for s in "load dve flat tr in exp ready back row out".split())
        with nc.Block() as block:
            @block.sync
            def _(sp):
                sp.dma_start(heads[:, :], d["table"][NPAD:TABLE, :]).then_inc(j_load, 16)

            @block.gpsimd
            def _(pool):
                pool.wait_ge(j_row, 1)
                nc.gpsimd.indirect_dma_start(
                    out=d["table"], out_offset=bass.IndirectOffsetOnAxis(ap=merge_row[:, 0:1], axis=0),
                    in_=outrow[:, :], in_offset=None, bounds_check=TABLE - 1, oob_is_err=False).then_inc(j_out, 16)
                pool.wait_ge(j_out, 16)

            @block.tensor
            def _(pe):
                pe.wait_ge(j_flat, 1)
                nc.tensor.matmul(mps[:, :, :], ones[:, :], diag[:, :, :], start=True, stop=True).then_inc(j_tr, 1)
                for n in range(12):
                    c, k, g = n // 6, n // 2 % 3, n % 2
                    ins = nc.tensor.transpose(tps[:, n, :], flat[:, c, k, g * P:(g + 1) * P], ident[:, :])
                ins.then_inc(j_tr, 1)
                pe.wait_ge(j_ready, 1)
                for k in range(2):
                    for g in range(2):
                        ins = nc.tensor.transpose(ops[:, 2 * k + g, :], joined[:, k, g, :], ident[:, :])
                ins.then_inc(j_back, 1)

            @block.scalar
            def _(act):
                for n in range(2):
                    act.wait_ge(j_in, n + 1)
                    nc.scalar.activation(tmp[:, :, 2 * n:2 * n + 2, :], tmp[:, :, 2 * n:2 * n + 2, :], ACT.Exp
                                         ).then_inc(j_exp, 1)

            @block.vector
            def _(dve):
                v = Line(dve, j_dve)
                dve.wait_ge(j_load, 16)
                for c, r in ((0, lastrow), (1, heads)):
                    v.add(nc.vector.tensor_copy(flat[:, c, 0, :], r[:, 0:CH]))
                    v.add(nc.vector.tensor_copy(
                        flat[:, c, 1:3, :].rearrange("p a (i o) -> p a i o", o=F),
                        r[:, CH:ROW].rearrange("p (i a o) -> p a i o", a=2, o=F)))
                v.add(nc.vector.tensor_scalar(diag[:, 0, :], ident[:, :], flags[:, 0:1], None, ALU.mult))
                v.then(nc.vector.tensor_scalar(diag[:, 1, :], ident[:, :], flags[:, 1:2], None, ALU.mult))
                nc.vector.memset(joined[:, :, :, :], 0.0).then_inc(j_flat, 1)
                dve.wait_ge(j_tr, 1)
                v.then(nc.vector.tensor_scalar(mask[:, :, :], mps[:, :, :], BIG, -BIG, ALU.mult, ALU.add))
                dve.wait_ge(j_tr, 2)
                v.then(nc.vector.tensor_copy(cols[:, :, :], tps[:, :, :]))
                for g in range(2):
                    last_sh = cols[:, g, :]
                    v.then(nc.vector.tensor_tensor_scan(sh[:, g, :], mask[:, 0, :], last_sh, 0.0, ALU.add, ALU.max))
                    v.then(nc.vector.tensor_tensor(tmp[:, g, 0, :], last_sh, sh[:, g, :], ALU.subtract))
                    v.then(nc.vector.memset(tmp[:, g, 1, 0:1], -BIG))
                    v.then(nc.vector.tensor_tensor(tmp[:, g, 1, 1:P], sh[:, g, 0:P - 1], mask[:, 0, 1:P], ALU.add))
                    v.then(nc.vector.tensor_tensor(tmp[:, g, 1, 1:P], tmp[:, g, 1, 1:P], sh[:, g, 1:P], ALU.subtract))
                dve.wait_ge(j_dve, v.n)
                nc.vector.tensor_copy(prod[:, :], cols[:, 0, :]).then_inc(j_in, 1)
                dve.wait_ge(j_exp, 1)
                for g in range(2):
                    for k in range(2):
                        own = cols[:, 2 * (k + 1) + g, :]
                        v.then(nc.vector.tensor_tensor(own, own, tmp[:, g, 0, :], ALU.mult))
                        v.then(nc.vector.tensor_tensor_scan(acc[:, k, g, :], tmp[:, g, 1, :], own, 0.0,
                                                            ALU.mult, ALU.add))
                    first_sh = cols[:, 6 + g, :]
                    v.then(nc.vector.memset(tmp[:, g, 3, 0:1], -BIG))
                    v.then(nc.vector.tensor_tensor(tmp[:, g, 3, 1:P], sh[:, g, 0:P - 1], mask[:, 1, 1:P], ALU.add))
                    v.then(nc.vector.tensor_tensor(sh[:, g, :], tmp[:, g, 3, :], first_sh, ALU.max))
                    v.then(nc.vector.tensor_tensor(tmp[:, g, 2, :], first_sh, sh[:, g, :], ALU.subtract))
                    v.then(nc.vector.tensor_tensor(tmp[:, g, 3, :], tmp[:, g, 3, :], sh[:, g, :], ALU.subtract))
                nc.vector.tensor_copy(prod[:, :], cols[:, 0, :]).then_inc(j_in, 1)
                dve.wait_ge(j_exp, 2)
                for g in range(2):
                    for k in range(2):
                        first = cols[:, 6 + 2 * (k + 1) + g, :]
                        v.then(nc.vector.tensor_tensor(prod[:, 1:P], acc[:, k, g, 0:P - 1], tmp[:, g, 3, 1:P], ALU.mult))
                        v.then(nc.vector.tensor_tensor(joined[:, k, g, :], first, tmp[:, g, 2, :], ALU.mult))
                        v.then(nc.vector.tensor_tensor(joined[:, k, g, 1:P], joined[:, k, g, 1:P], prod[:, 1:P],
                                                       ALU.add))
                nc.vector.memset(outrow[:, 0:CH], 0.0).then_inc(j_ready, 1)
                dve.wait_ge(j_back, 1)
                nc.vector.tensor_copy(outrow[:, CH:ROW].rearrange("p (i a o) -> p a i o", a=2, o=F),
                                      ops[:, :, :].rearrange("p (a g) (i o) -> p a (g i) o", a=2, o=F)
                                      ).then_inc(j_row, 1)


def attention_out(nc, keep, d, sem, out):
    x = keep["x"]
    PART = 5
    ROUNDS = TILES // PART
    full = NODES // P
    with ExitStack() as ctx:
        def sb(name, shape, dt=F32):
            return ctx.enter_context(nc.sbuf_tensor(name, shape, dt))

        t = sb("t_rows", [P, 2, PART, 2 * CH])
        inv = sb("inv", [P, PART, CH])
        o = sb("o", [P, PART, F])
        z_load = [sem("z_load0"), sem("z_load1")]
        z_dve, z_out = sem("z_dve"), sem("z_out")
        view = d["table"][0:NPAD, CH:ROW].rearrange("(t p) c -> p t c", p=P)
        PER = 4
        with nc.Block() as block:
            @block.sync
            def _(sp):
                for r in range(ROUNDS):
                    if r >= 2:
                        sp.wait_ge(z_dve, PER * (r - 1))
                    sp.dma_start(t[:, r % 2, :, :], view[:, r * PART:(r + 1) * PART, :]).then_inc(z_load[r % 2], 16)
                sp.wait_ge(z_dve, PER * ROUNDS)
                sp.dma_start(out[0:full * P, :].rearrange("(t p) f -> p t f", p=P), x[:, 0:full, :]).then_inc(z_out, 16)
                sp.dma_start(out[full * P:NODES, :], x[0:NODES - full * P, full, :]).then_inc(z_out, 16)
                sp.wait_ge(z_out, 32)

            @block.vector
            def _(dve):
                v = Line(dve, z_dve)
                for r in range(ROUNDS):
                    dve.wait_ge(z_load[r % 2], 16 * (r // 2 + 1))
                    both = t[:, r % 2, :, :].rearrange("p t (i a o) -> p (t i) a o", a=2, o=F)
                    flat = inv[:, :, :].rearrange("p t (i o) -> p (t i) o", o=F)
                    v.then(nc.vector.reciprocal(flat, both[:, :, 0, :]))
                    v.then(nc.vector.tensor_tensor(flat, flat, both[:, :, 1, :], ALU.mult))
                    v.then(nc.vector.tensor_reduce(o[:, :, :], inv[:, :, :].rearrange("p t (i o) -> p t o i", o=F),
                                                   X, ALU.add))
                    part = x[:, r * PART:(r + 1) * PART, :]
                    v.then(nc.vector.tensor_tensor(part, part, o[:, :, :], ALU.add))


def kernel(**inputs):
    import numpy as np
    import concourse.bacc as bacc
    from concourse import mybir as mb
    from concourse.bass_utils import run_bass_kernel_spmd as run

    arrays = {k: np.ascontiguousarray(v) for k, v in inputs.items()}
    src, dst, x = arrays.pop("src"), arrays.pop("dst"), arrays.pop("x")
    ef = arrays.pop("edge_attr_16")
    fill = np.full(EPAD - EDGES, NODES, np.int32)
    arrays["x"] = np.concatenate([x, np.zeros((NPAD - NODES, F), x.dtype)])
    arrays["src"] = np.concatenate([src, fill])
    arrays["dst"] = np.concatenate([dst, fill])
    arrays["group_ends"] = arrays["dst"].reshape(1, GROUPS, GROUP)[:, :, -1]
    more = EPAD + SLOTS - EDGES
    arrays["src_more"] = np.concatenate([src, np.full(more, NODES, np.int32)]).reshape(EPAD + SLOTS, 1)
    arrays["ef"] = np.concatenate([ef, np.zeros((more, F), ef.dtype)])
    wa, wm = arrays.pop("L3_gnn_W_attn"), arrays.pop("L3_gnn_W_msg")
    ba, bm = arrays.pop("L3_gnn_b_attn"), arrays.pop("L3_gnn_b_msg")
    wa = np.concatenate([wa, np.ones((1, CH), wa.dtype), ba[None]])
    wm = np.concatenate([wm, np.zeros((1, CH), wm.dtype), bm[None]])
    arrays["w_edge"] = np.stack([wa.reshape(F + 2, F, F), wm.reshape(F + 2, F, F)], axis=2).reshape(F + 2, 2 * CH)
    for name in ("pre_b1", "pre_b2", "post_b1"):
        arrays["L1_gnn_" + name] = arrays["L1_gnn_" + name].reshape(2, P).T
    arrays = {"in_" + k: np.ascontiguousarray(v) for k, v in arrays.items()}

    nc = bacc.Bacc("TRN2", target_bir_lowering=False, num_devices=1)
    io = {k[3:]: nc.dram_tensor(k, v.shape, mb.dt.from_np(v.dtype), kind="ExternalInput").ap()
          for k, v in arrays.items()}
    out = nc.dram_tensor("out_0", (NODES, F), mb.dt.float32, kind="ExternalOutput").ap()
    program(nc, io, out)
    return run(nc, [arrays], core_ids=[0]).results[0]["out_0"]
```
